# Optimizing a Trainium2 kernel written in Bass

```python
import numpy as np
import jax
import jax.numpy as jnp

def _softmax(x, axis=-1):
    return jax.nn.softmax(x, axis=axis)

def _gelu(x):
    return jax.nn.gelu(x, approximate=True)

def _silu(x):
    return jax.nn.silu(x)

def _sigmoid(x):
    return jax.nn.sigmoid(x)

def _layernorm(x, axis=-1, eps=1e-05):
    m = jnp.mean(x, axis=axis, keepdims=True)
    v = jnp.var(x, axis=axis, keepdims=True)
    return (x - m) / jnp.sqrt(v + eps)

def _scatter_add(tgt, idx, src, axis=0):
    return tgt.at[idx].add(src)

def _segment_sum(src, seg, n):
    return jax.ops.segment_sum(src, seg, n)
kernel_name = 'mk_recurrent_d2_jaxref_r8_bbf73d'

def setup_inputs(seed: int=0):
    np.random.seed(seed)
    _w = jnp.asarray

    def _L0_attn_setup():
        import jax, jax.numpy as jnp
        import numpy as np
        from jax import lax
        H = 4
        CHUNK = 64
        EPS = 1e-05

        def _rope(t, cos, sin):
            t1, t2 = jnp.split(t, 2, axis=-1)
            c = cos[None, :, None, :]
            s = sin[None, :, None, :]
            return jnp.concatenate([t1 * c - t2 * s, t2 * c + t1 * s], axis=-1)
        key = jax.random.key(seed)
        ks = jax.random.split(key, 8)
        B, T, D = (4, 512, 128)
        s = lambda fan: 1.0 / np.sqrt(fan)
        return {'x': jax.random.normal(ks[0], (B, T, D), jnp.float32), 'ln_w': jnp.ones((D,), jnp.float32), 'ln_b': jnp.zeros((D,), jnp.float32), 'Wq': jax.random.normal(ks[1], (D, D), jnp.float32) * s(D), 'Wk': jax.random.normal(ks[2], (D, D), jnp.float32) * s(D), 'Wv': jax.random.normal(ks[3], (D, 2 * D), jnp.float32) * s(D), 'Wg': jax.random.normal(ks[4], (D, 2 * D), jnp.float32) * s(D), 'g_norm_w': jnp.ones((2 * D // H,), jnp.float32), 'Wo': jax.random.normal(ks[5], (2 * D, D), jnp.float32) * s(2 * D)}
    _L0_attn_in = _L0_attn_setup()

    def _L0_ffn_setup():
        import jax, jax.numpy as jnp
        import numpy as np
        DIM = 128
        DEPTH = 6
        HEADS = 16
        DIM_HEAD = 64
        WINDOW = 32
        INNER = HEADS * DIM_HEAD
        DIM_INNER = int(DIM * 4 * 2 / 3)
        QK_SCALE = 8.0

        def shift_tokens(t):
            a, s = jnp.split(t, 2, -1)
            s = jnp.pad(s, ((0, 0), (1, 0), (0, 0)))[:, :-1]
            return jnp.concatenate([a, s], -1)

        def l2norm(t):
            return t / jnp.maximum(jnp.linalg.norm(t, axis=-1, keepdims=True), 1e-12)

        def rotate_half(x):
            x1, x2 = jnp.split(x, 2, -1)
            return jnp.concatenate([-x2, x1], -1)

        def rotary_tables(n):
            half = jnp.arange(0, DIM_HEAD, 2, dtype=jnp.float32)
            inv_freq = 1.0 / 10000.0 ** (half / DIM_HEAD)
            t = jnp.arange(n, dtype=jnp.float32)
            freqs = t[:, None] * inv_freq[None, :]
            freqs = jnp.concatenate([freqs, freqs], -1)
            base_scale = (half + 0.4 * DIM_HEAD) / (1.4 * DIM_HEAD)
            power = (t - n // 2) / (WINDOW // 2)
            scale = base_scale[None, :] ** power[:, None]
            scale = jnp.concatenate([scale, scale], -1)
            return (freqs, scale)

        def local_attention(q, k, v):
            b, h, n, d = q.shape
            w = WINDOW
            nw = n // w
            bq = q.reshape(b, h, nw, w, d)
            bk = k.reshape(b, h, nw, w, d)
            bv = v.reshape(b, h, nw, w, d)

            def look(t):
                p = jnp.pad(t, ((0, 0), (0, 0), (1, 0), (0, 0), (0, 0)))
                return jnp.concatenate([p[:, :, :nw], p[:, :, 1:]], axis=3)
            bk2, bv2 = (look(bk), look(bv))
            seq = jnp.arange(n).reshape(nw, w)
            seq_p = jnp.pad(seq, ((1, 0), (0, 0)), constant_values=-1)
            jt = jnp.concatenate([seq_p[:nw], seq_p[1:]], axis=1)
            it = seq[:, :, None]
            jb = jt[:, None, :]
            mask = (it < jb) | (it > jb + w) | (jb == -1)
            sim = jnp.einsum('bhwie,bhwje->bhwij', bq, bk2) * QK_SCALE
            sim = jnp.where(mask, -jnp.finfo(sim.dtype).max, sim)
            attn = jax.nn.softmax(sim, -1)
            out = jnp.einsum('bhwij,bhwje->bhwie', attn, bv2)
            return out.reshape(b, h, n, d)

        def attn_layer(x, Wqkv, qs, ksc, Wo):
            b, n, _ = x.shape
            qkv = x @ Wqkv
            q, k, v = jnp.split(qkv, 3, -1)
            sh = lambda t: t.reshape(b, n, HEADS, DIM_HEAD).transpose(0, 2, 1, 3)
            q, k, v = (sh(q), sh(k), sh(v))
            q = l2norm(q) * qs
            k = l2norm(k) * ksc
            freqs, scale = rotary_tables(n)
            cos, sin = (jnp.cos(freqs), jnp.sin(freqs))
            q = q * cos * scale + rotate_half(q) * sin * scale
            inv = 1.0 / scale
            k = k * cos * inv + rotate_half(k) * sin * inv
            out = local_attention(q, k, v)
            out = out.transpose(0, 2, 1, 3).reshape(b, n, INNER)
            return out @ Wo

        def ffn_layer(x, g, bln, W1, b1, W2, b2):
            mu = x.mean(-1, keepdims=True)
            var = ((x - mu) ** 2).mean(-1, keepdims=True)
            xn = (x - mu) / jnp.sqrt(var + 1e-05) * g + bln
            hg = xn @ W1 + b1
            a, gate = jnp.split(hg, 2, -1)
            return a * jax.nn.gelu(gate, approximate=False) @ W2 + b2
        key = jax.random.key(seed)
        ks = jax.random.split(key, 8)
        B, N = (2, 256)
        init = lambda k, shape: jax.random.normal(k, shape, jnp.float32) * 0.02
        return {'x': jax.random.normal(ks[0], (B, N, DIM), jnp.float32), 'Wqkv': init(ks[1], (DEPTH, DIM, 3 * INNER)), 'q_scale': jnp.ones((DEPTH, DIM_HEAD), jnp.float32), 'k_scale': jnp.ones((DEPTH, DIM_HEAD), jnp.float32), 'Wo': init(ks[2], (DEPTH, INNER, DIM)), 'ln_g': jnp.ones((DEPTH, DIM), jnp.float32), 'ln_b': jnp.zeros((DEPTH, DIM), jnp.float32), 'W1': init(ks[3], (DEPTH, DIM, 2 * DIM_INNER)), 'b1': jnp.zeros((DEPTH, 2 * DIM_INNER), jnp.float32), 'W2': init(ks[4], (DEPTH, DIM_INNER, DIM)), 'b2': jnp.zeros((DEPTH, DIM), jnp.float32)}
    _L0_ffn_in = _L0_ffn_setup()

    def _L1_attn_setup():
        import jax, jax.numpy as jnp
        import numpy as np

        def _rope_tables(T, d):
            half = d // 2
            i = jnp.arange(half, dtype=jnp.float32)
            theta = 10000.0 ** (-2.0 * i / d)
            m = jnp.arange(T, dtype=jnp.float32)[:, None]
            ang = m * theta[None, :]
            return (jnp.cos(ang), jnp.sin(ang))

        def _rotate(v, cos, sin):
            B, T, d = v.shape
            half = d // 2
            v2 = v.reshape(B, T, half, 2)
            even, odd = (v2[..., 0], v2[..., 1])
            c = cos[None, :, :]
            s = sin[None, :, :]
            new_even = even * c - odd * s
            new_odd = even * s + odd * c
            return jnp.stack([new_even, new_odd], axis=-1).reshape(B, T, d)
        key = jax.random.key(seed)
        k1, k2, k3, k4 = jax.random.split(key, 4)
        B, T, d = (4, 256, 128)
        x = jax.random.normal(k1, (B, T, d), dtype=jnp.float32)
        scale = 0.02
        Wq = jax.random.normal(k2, (d, d), dtype=jnp.float32) * scale
        Wk = jax.random.normal(k3, (d, d), dtype=jnp.float32) * scale
        Wv = jax.random.normal(k4, (d, d), dtype=jnp.float32) * scale
        return {'x': x, 'Wq': Wq, 'Wk': Wk, 'Wv': Wv}
    _L1_attn_in = _L1_attn_setup()

    def _L1_ffn_setup():
        import jax, jax.numpy as jnp
        import numpy as np
        D_MODEL = 128
        N_EXPERTS = 8
        TOP_K = 2
        BOTTLENECK = 64
        B, S = (2, 512)
        ADAPTER_SCALE = 0.5

        def _moe_forward(x, w_gate, w_noise, Wd, bd, Wu, bu):
            b, s, d = x.shape
            xf = x.reshape(-1, d)
            T = xf.shape[0]
            clean_logits = xf @ w_gate
            logits = clean_logits
            k1 = min(TOP_K + 1, N_EXPERTS)
            top_logits, top_idx = jax.lax.top_k(logits, k1)
            top_k_logits = top_logits[:, :TOP_K]
            top_k_idx = top_idx[:, :TOP_K]
            top_k_gates = jax.nn.softmax(top_k_logits, axis=-1)
            rows = jnp.arange(T)[:, None]
            gates = jnp.zeros((T, N_EXPERTS), dtype=top_k_gates.dtype)
            gates = gates.at[rows, top_k_idx].set(top_k_gates)
            h = jax.nn.relu(jnp.einsum('td,edb->teb', xf, Wd) + bd[None, :, :])
            y = jnp.einsum('teb,ebd->ted', h, Wu) + bu[None, :, :]
            y = ADAPTER_SCALE * y
            out = jnp.einsum('te,ted->td', gates, y)
            return out.reshape(b, s, d)
        key = jax.random.key(seed)
        ks = jax.random.split(key, 8)
        sd = 0.02
        x = jax.random.normal(ks[0], (B, S, D_MODEL), dtype=jnp.float32)
        w_gate = jax.random.normal(ks[1], (D_MODEL, N_EXPERTS), dtype=jnp.float32) * sd
        w_noise = jax.random.normal(ks[2], (D_MODEL, N_EXPERTS), dtype=jnp.float32) * sd
        Wd = jax.random.normal(ks[3], (N_EXPERTS, D_MODEL, BOTTLENECK), dtype=jnp.float32) * sd
        bd = jnp.zeros((N_EXPERTS, BOTTLENECK), dtype=jnp.float32)
        Wu = jax.random.normal(ks[4], (N_EXPERTS, BOTTLENECK, D_MODEL), dtype=jnp.float32) * sd
        bu = jnp.zeros((N_EXPERTS, D_MODEL), dtype=jnp.float32)
        return {'x': x, 'w_gate': w_gate, 'w_noise': w_noise, 'Wd': Wd, 'bd': bd, 'Wu': Wu, 'bu': bu}
    _L1_ffn_in = _L1_ffn_setup()
    _d = {'L0_attn_x': _L0_attn_in['x'], 'L0_attn_ln_w': _L0_attn_in['ln_w'], 'L0_attn_ln_b': _L0_attn_in['ln_b'], 'L0_attn_Wq': _L0_attn_in['Wq'], 'L0_attn_Wk': _L0_attn_in['Wk'], 'L0_attn_Wv': _L0_attn_in['Wv'], 'L0_attn_Wg': _L0_attn_in['Wg'], 'L0_attn_g_norm_w': _L0_attn_in['g_norm_w'], 'L0_attn_Wo': _L0_attn_in['Wo'], 'L0_ffn_Wqkv': _L0_ffn_in['Wqkv'], 'L0_ffn_q_scale': _L0_ffn_in['q_scale'], 'L0_ffn_k_scale': _L0_ffn_in['k_scale'], 'L0_ffn_Wo': _L0_ffn_in['Wo'], 'L0_ffn_ln_g': _L0_ffn_in['ln_g'], 'L0_ffn_ln_b': _L0_ffn_in['ln_b'], 'L0_ffn_W1': _L0_ffn_in['W1'], 'L0_ffn_b1': _L0_ffn_in['b1'], 'L0_ffn_W2': _L0_ffn_in['W2'], 'L0_ffn_b2': _L0_ffn_in['b2'], 'L1_attn_Wq': _L1_attn_in['Wq'], 'L1_attn_Wk': _L1_attn_in['Wk'], 'L1_attn_Wv': _L1_attn_in['Wv'], 'L1_ffn_w_gate': _L1_ffn_in['w_gate'], 'L1_ffn_w_noise': _L1_ffn_in['w_noise'], 'L1_ffn_Wd': _L1_ffn_in['Wd'], 'L1_ffn_bd': _L1_ffn_in['bd'], 'L1_ffn_Wu': _L1_ffn_in['Wu'], 'L1_ffn_bu': _L1_ffn_in['bu']}
    _x0 = _d['L0_attn_x']
    _d['L0_attn_x'] = jax.random.normal(jax.random.fold_in(jax.random.key(seed), 1), (4, 512, 128), dtype=_x0.dtype)
    del _x0
    return _d

def reference(L0_attn_x, L0_attn_ln_w, L0_attn_ln_b, L0_attn_Wq, L0_attn_Wk, L0_attn_Wv, L0_attn_Wg, L0_attn_g_norm_w, L0_attn_Wo, L0_ffn_Wqkv, L0_ffn_q_scale, L0_ffn_k_scale, L0_ffn_Wo, L0_ffn_ln_g, L0_ffn_ln_b, L0_ffn_W1, L0_ffn_b1, L0_ffn_W2, L0_ffn_b2, L1_attn_Wq, L1_attn_Wk, L1_attn_Wv, L1_ffn_w_gate, L1_ffn_w_noise, L1_ffn_Wd, L1_ffn_bd, L1_ffn_Wu, L1_ffn_bu):

    def _L0_attn_ref(x, ln_w, ln_b, Wq, Wk, Wv, Wg, g_norm_w, Wo):
        import jax, jax.numpy as jnp
        import numpy as np
        from jax import lax
        H = 4
        CHUNK = 64
        EPS = 1e-05

        def _rope(t, cos, sin):
            t1, t2 = jnp.split(t, 2, axis=-1)
            c = cos[None, :, None, :]
            s = sin[None, :, None, :]
            return jnp.concatenate([t1 * c - t2 * s, t2 * c + t1 * s], axis=-1)
        B, T, D = x.shape
        dk, dv = (D // H, 2 * D // H)
        C = CHUNK
        N = T // C
        mu = x.mean(-1, keepdims=True)
        var = ((x - mu) ** 2).mean(-1, keepdims=True)
        normed = (x - mu) * lax.rsqrt(var + EPS) * ln_w + ln_b
        q = (normed @ Wq).reshape(B, T, H, dk)
        k = (normed @ Wk).reshape(B, T, H, dk)
        v = (normed @ Wv).reshape(B, T, H, dv)
        g = (normed @ Wg).reshape(B, T, H, dv)
        inv_freq = 1.0 / 10000.0 ** (jnp.arange(0, dk, 2, dtype=jnp.float32) / dk)
        freqs = jnp.arange(T, dtype=jnp.float32)[:, None] * inv_freq[None, :]
        cos, sin = (jnp.cos(freqs), jnp.sin(freqs))
        q = _rope(q, cos, sin) * dk ** (-0.5)
        k = _rope(k, cos, sin)
        gamma = 1.0 - jnp.exp2(-5.0 - jnp.arange(H, dtype=jnp.float32))
        i = jnp.arange(C, dtype=jnp.float32)
        Dmask = jnp.where(i[:, None] >= i[None, :], gamma[:, None, None] ** (i[:, None] - i[None, :]), 0.0)
        cross = gamma[:, None] ** (i + 1.0)
        kdec = gamma[:, None] ** (C - 1.0 - i)
        gC = gamma ** C
        to_chunks = lambda t, d: t.reshape(B, N, C, H, d).transpose(1, 0, 3, 2, 4)
        qc, kc, vc = (to_chunks(q, dk), to_chunks(k, dk), to_chunks(v, dv))

        def step(S, inp):
            qn, kn, vn = inp
            attn = jnp.einsum('bhid,bhjd->bhij', qn, kn) * Dmask
            o = jnp.einsum('bhij,bhjv->bhiv', attn, vn) + jnp.einsum('bhid,bhdv->bhiv', qn * cross[None, :, :, None], S)
            S = S * gC[None, :, None, None] + jnp.einsum('bhid,bhiv->bhdv', kn * kdec[None, :, :, None], vn)
            return (S, o)
        S0 = jnp.zeros((B, H, dk, dv), x.dtype)
        _, o = lax.scan(step, S0, (qc, kc, vc))
        o = o.transpose(1, 0, 3, 2, 4).reshape(B, T, H, dv)
        o = o * lax.rsqrt((o ** 2).mean(-1, keepdims=True) + EPS) * g_norm_w
        o = o * (g * jax.nn.sigmoid(g))
        out = o.reshape(B, T, 2 * D) @ Wo
        return x + out

    def _L0_ffn_ref(x, Wqkv, q_scale, k_scale, Wo, ln_g, ln_b, W1, b1, W2, b2):
        import jax, jax.numpy as jnp
        import numpy as np
        DIM = 128
        DEPTH = 6
        HEADS = 16
        DIM_HEAD = 64
        WINDOW = 32
        INNER = HEADS * DIM_HEAD
        DIM_INNER = int(DIM * 4 * 2 / 3)
        QK_SCALE = 8.0

        def shift_tokens(t):
            a, s = jnp.split(t, 2, -1)
            s = jnp.pad(s, ((0, 0), (1, 0), (0, 0)))[:, :-1]
            return jnp.concatenate([a, s], -1)

        def l2norm(t):
            return t / jnp.maximum(jnp.linalg.norm(t, axis=-1, keepdims=True), 1e-12)

        def rotate_half(x):
            x1, x2 = jnp.split(x, 2, -1)
            return jnp.concatenate([-x2, x1], -1)

        def rotary_tables(n):
            half = jnp.arange(0, DIM_HEAD, 2, dtype=jnp.float32)
            inv_freq = 1.0 / 10000.0 ** (half / DIM_HEAD)
            t = jnp.arange(n, dtype=jnp.float32)
            freqs = t[:, None] * inv_freq[None, :]
            freqs = jnp.concatenate([freqs, freqs], -1)
            base_scale = (half + 0.4 * DIM_HEAD) / (1.4 * DIM_HEAD)
            power = (t - n // 2) / (WINDOW // 2)
            scale = base_scale[None, :] ** power[:, None]
            scale = jnp.concatenate([scale, scale], -1)
            return (freqs, scale)

        def local_attention(q, k, v):
            b, h, n, d = q.shape
            w = WINDOW
            nw = n // w
            bq = q.reshape(b, h, nw, w, d)
            bk = k.reshape(b, h, nw, w, d)
            bv = v.reshape(b, h, nw, w, d)

            def look(t):
                p = jnp.pad(t, ((0, 0), (0, 0), (1, 0), (0, 0), (0, 0)))
                return jnp.concatenate([p[:, :, :nw], p[:, :, 1:]], axis=3)
            bk2, bv2 = (look(bk), look(bv))
            seq = jnp.arange(n).reshape(nw, w)
            seq_p = jnp.pad(seq, ((1, 0), (0, 0)), constant_values=-1)
            jt = jnp.concatenate([seq_p[:nw], seq_p[1:]], axis=1)
            it = seq[:, :, None]
            jb = jt[:, None, :]
            mask = (it < jb) | (it > jb + w) | (jb == -1)
            sim = jnp.einsum('bhwie,bhwje->bhwij', bq, bk2) * QK_SCALE
            sim = jnp.where(mask, -jnp.finfo(sim.dtype).max, sim)
            attn = jax.nn.softmax(sim, -1)
            out = jnp.einsum('bhwij,bhwje->bhwie', attn, bv2)
            return out.reshape(b, h, n, d)

        def attn_layer(x, Wqkv, qs, ksc, Wo):
            b, n, _ = x.shape
            qkv = x @ Wqkv
            q, k, v = jnp.split(qkv, 3, -1)
            sh = lambda t: t.reshape(b, n, HEADS, DIM_HEAD).transpose(0, 2, 1, 3)
            q, k, v = (sh(q), sh(k), sh(v))
            q = l2norm(q) * qs
            k = l2norm(k) * ksc
            freqs, scale = rotary_tables(n)
            cos, sin = (jnp.cos(freqs), jnp.sin(freqs))
            q = q * cos * scale + rotate_half(q) * sin * scale
            inv = 1.0 / scale
            k = k * cos * inv + rotate_half(k) * sin * inv
            out = local_attention(q, k, v)
            out = out.transpose(0, 2, 1, 3).reshape(b, n, INNER)
            return out @ Wo

        def ffn_layer(x, g, bln, W1, b1, W2, b2):
            mu = x.mean(-1, keepdims=True)
            var = ((x - mu) ** 2).mean(-1, keepdims=True)
            xn = (x - mu) / jnp.sqrt(var + 1e-05) * g + bln
            hg = xn @ W1 + b1
            a, gate = jnp.split(hg, 2, -1)
            return a * jax.nn.gelu(gate, approximate=False) @ W2 + b2
        for i in range(DEPTH):
            x = attn_layer(shift_tokens(x), Wqkv[i], q_scale[i], k_scale[i], Wo[i]) + x
            x = ffn_layer(shift_tokens(x), ln_g[i], ln_b[i], W1[i], b1[i], W2[i], b2[i]) + x
        return x

    def _L1_attn_ref(x, Wq, Wk, Wv):
        import jax, jax.numpy as jnp
        import numpy as np

        def _rope_tables(T, d):
            half = d // 2
            i = jnp.arange(half, dtype=jnp.float32)
            theta = 10000.0 ** (-2.0 * i / d)
            m = jnp.arange(T, dtype=jnp.float32)[:, None]
            ang = m * theta[None, :]
            return (jnp.cos(ang), jnp.sin(ang))

        def _rotate(v, cos, sin):
            B, T, d = v.shape
            half = d // 2
            v2 = v.reshape(B, T, half, 2)
            even, odd = (v2[..., 0], v2[..., 1])
            c = cos[None, :, :]
            s = sin[None, :, :]
            new_even = even * c - odd * s
            new_odd = even * s + odd * c
            return jnp.stack([new_even, new_odd], axis=-1).reshape(B, T, d)
        B, T, d = x.shape
        cos, sin = _rope_tables(T, d)
        Q = jnp.einsum('btd,ed->bte', x, Wq)
        K = jnp.einsum('btd,ed->bte', x, Wk)
        V = jnp.einsum('btd,ed->bte', x, Wv)
        Qr = _rotate(Q, cos, sin)
        Kr = _rotate(K, cos, sin)
        scores = jnp.einsum('bqd,bkd->bqk', Qr, Kr) / jnp.sqrt(jnp.float32(d))
        mask = jnp.tril(jnp.ones((T, T), dtype=bool), k=1)
        scores = jnp.where(mask[None, :, :], scores, -jnp.inf)
        attn = jax.nn.softmax(scores, axis=-1)
        out = jnp.einsum('bqk,bkd->bqd', attn, V)
        return out

    def _L1_ffn_ref(x, w_gate, w_noise, Wd, bd, Wu, bu):
        import jax, jax.numpy as jnp
        import numpy as np
        D_MODEL = 128
        N_EXPERTS = 8
        TOP_K = 2
        BOTTLENECK = 64
        B, S = (2, 512)
        ADAPTER_SCALE = 0.5

        def _moe_forward(x, w_gate, w_noise, Wd, bd, Wu, bu):
            b, s, d = x.shape
            xf = x.reshape(-1, d)
            T = xf.shape[0]
            clean_logits = xf @ w_gate
            logits = clean_logits
            k1 = min(TOP_K + 1, N_EXPERTS)
            top_logits, top_idx = jax.lax.top_k(logits, k1)
            top_k_logits = top_logits[:, :TOP_K]
            top_k_idx = top_idx[:, :TOP_K]
            top_k_gates = jax.nn.softmax(top_k_logits, axis=-1)
            rows = jnp.arange(T)[:, None]
            gates = jnp.zeros((T, N_EXPERTS), dtype=top_k_gates.dtype)
            gates = gates.at[rows, top_k_idx].set(top_k_gates)
            h = jax.nn.relu(jnp.einsum('td,edb->teb', xf, Wd) + bd[None, :, :])
            y = jnp.einsum('teb,ebd->ted', h, Wu) + bu[None, :, :]
            y = ADAPTER_SCALE * y
            out = jnp.einsum('te,ted->td', gates, y)
            return out.reshape(b, s, d)
        return _moe_forward(x, w_gate, w_noise, Wd, bd, Wu, bu)
    x = L0_attn_x
    xn = _layernorm(x, axis=-1)
    s = _L0_attn_ref(xn, L0_attn_ln_w, L0_attn_ln_b, L0_attn_Wq, L0_attn_Wk, L0_attn_Wv, L0_attn_Wg, L0_attn_g_norm_w, L0_attn_Wo)
    g = _silu(_L0_ffn_ref(xn, L0_ffn_Wqkv, L0_ffn_q_scale, L0_ffn_k_scale, L0_ffn_Wo, L0_ffn_ln_g, L0_ffn_ln_b, L0_ffn_W1, L0_ffn_b1, L0_ffn_W2, L0_ffn_b2))
    x = x + s * g
    xn = _layernorm(x, axis=-1)
    s = _L1_attn_ref(xn, L1_attn_Wq, L1_attn_Wk, L1_attn_Wv)
    g = _silu(_L1_ffn_ref(xn, L1_ffn_w_gate, L1_ffn_w_noise, L1_ffn_Wd, L1_ffn_bd, L1_ffn_Wu, L1_ffn_bu))
    x = x + s * g
    return x

_drawn_inputs = setup_inputs


def setup_inputs(seed=0):
    import zlib

    import numpy as np

    out = dict(_drawn_inputs(seed))
    spreads = {'L0_attn_ln_w': (1.0, 0.2),
     'L0_attn_ln_b': (0.0, 0.1),
     'L0_attn_g_norm_w': (1.0, 0.2),
     'L0_ffn_q_scale': (1.0, 0.6),
     'L0_ffn_k_scale': (1.0, 0.6),
     'L0_ffn_ln_g': (1.0, 0.6),
     'L0_ffn_ln_b': (0.0, 0.8),
     'L0_ffn_b1': (0.0, 0.8),
     'L0_ffn_b2': (0.0, 0.1),
     'L1_ffn_bd': (0.0, 2.0),
     'L1_ffn_bu': (0.0, 2.0)}
    factors = {'L0_ffn_W1': 4.069,
     'L0_ffn_W2': 4.005,
     'L1_attn_Wq': 8.0,
     'L1_attn_Wk': 8.0,
     'L1_attn_Wv': 8.0,
     'L1_ffn_w_gate': 8.0,
     'L1_ffn_Wd': 8.0,
     'L1_ffn_Wu': 8.0}
    for name, (base, spread) in spreads.items():
        noise = np.random.default_rng([zlib.crc32(name.encode()), seed]).standard_normal(out[name].shape)
        drawn = base * np.exp(spread * noise) if base else spread * noise
        out[name] = jnp.asarray(drawn.astype(out[name].dtype))
    for name, factor in factors.items():
        out[name] = (out[name] * factor).astype(out[name].dtype)
    return out
```

```python
from contextlib import ExitStack

import numpy as np

import concourse.bass as bass
from concourse import mybir

F32 = mybir.dt.float32
BF16 = mybir.dt.bfloat16
ALU = mybir.AluOpType
ACT = mybir.ActivationFunctionType
AX = mybir.AxisListType

P = 128
B, T = 4, 512
TILES = T // P
EPS = 1e-5
MASKED = -1e30

DEPTH = 6
HEADS, DH = 16, 64
PAIRS = HEADS // 2
INNER = HEADS * DH
WIN = 32
WINDOWS = T // WIN
TW = P // WIN
FF = int(P * 4 * 2 / 3)
FCH = [128, 128, FF - 256]
SHIFTED = T + 4
NORM_FLOOR = 1e-24
LN_SCALE = 2.0 ** 20


class Signal:

    def __init__(self, ctx, nc, name, per=1):
        self.sem, self.per = ctx.enter_context(nc.semaphore(name)), per

    def at(self, rnd, n):
        return rnd * self.per + n


def build_network(nc, x, w_qkv, w_o, w_1, w_2, cols, qk_scale, rotary, win_mask, state):
    ctx = ExitStack()
    with ctx:
        def sb(name, shape, dt=F32):
            return ctx.enter_context(nc.sbuf_tensor(name, shape, dt))

        def sig(name, per=1):
            return Signal(ctx, nc, name, per)

        qk_ps = ctx.enter_context(nc.psum_tensor("qk_ps", [P, 4, 512], F32))
        sc_ps = ctx.enter_context(nc.psum_tensor("sc_ps", [P, 2, 512], F32))
        ring = ctx.enter_context(nc.psum_tensor("ring", [P, 2, 512], F32))

        ident = sb("ident", [P, P])
        ident_bf = sb("ident_bf", [P, P], BF16)
        mean_w = sb("mean_w", [P, P])
        mask_f = sb("mask_f", [P, 2, 2 * WIN])
        mask_bf = sb("mask_bf", [P, 2, PAIRS, 2 * WIN], BF16)
        rot_base = sb("rot_base", [P, 4, TILES, DH])
        rot = sb("rot", [P, 4, TILES, DH])
        qks = sb("qks", [P, 4, DH])
        wqkv = sb("wqkv", [P, 3 * INNER])
        wo = sb("wo", [P, PAIRS, P])
        w1 = sb("w1", [P, 2 * FF])
        w2 = sb("w2", [P, 3, P])
        col = sb("col", [P, 9])
        xs = sb("xs", [P, T])
        t1 = sb("t1", [P, 2 * INNER])
        t2 = sb("t2", [P, 2 * INNER])
        sq = sb("sq", [P, 2 * INNER])
        qkn = sb("qkn", [P, 2 * INNER])
        ss = sb("ss", [P, 2 * HEADS])
        rs = sb("rs", [P, 2 * HEADS])
        lnss = sb("lnss", [P, 2 * HEADS])
        nw1 = sb("nw1", [P, 2 * HEADS])
        nw2 = sb("nw2", [P, 2 * HEADS])
        rn = sb("rn", [P, 2 * HEADS])
        qT = sb("qT", [P, PAIRS, P])
        kT = sb("kT", [P, PAIRS, WIN + T])
        v_tok = sb("v_tok", [P, 2, 2, PAIRS * DH])
        v_win = sb("v_win", [P, WINDOWS, PAIRS * DH])
        smax = sb("smax", [P, HEADS])
        den = sb("den", [P, HEADS])
        rden = sb("rden", [P, 2, HEADS])
        pr = sb("pr", [P, INNER])
        pe_ = sb("pexp", [P, INNER])
        prT = sb("prT", [P, PAIRS, P])
        o_tok = sb("o_tok", [P, INNER])
        oT = sb("oT", [P, PAIRS, T])
        xc = sb("xc", [P, T])
        xsq = sb("xsq", [P, T])
        lnv = sb("lnv", [P, T])
        rstd = sb("rstd", [P, T])
        xh = sb("xh", [P, T])
        xn = sb("xn", [P, T])
        gel = sb("gel", [P, 3, T])
        u = sb("u", [P, 3, T])
        msum = sb("msum", [P, TILES])
        mmean = sb("mmean", [P, TILES])
        vsum = sb("vsum", [P, TILES])
        veps = sb("veps", [P, TILES])
        lnsum = sb("lnsum", [P, 2 * HEADS])
        eps_col = sb("eps_col", [P, 1])
        lv = sb("lv", [P, TILES])
        rstd0 = sb("rstd0", [P, TILES])
        xtok = xc[:, :].rearrange("p (t d) -> p t d", t=TILES)
        xctok = xn[:, :].rearrange("p (t d) -> p t d", t=TILES)
        sqtok = lnv[:, :].rearrange("p (t d) -> p t d", t=TILES)
        xntok = xh[:, :].rearrange("p (t d) -> p t d", t=TILES)

        s_const = sig("s_const")
        s_wqkv = sig("s_wqkv", 16)
        s_qks = sig("s_qks", 16)
        s_wrest = sig("s_wrest", 64)
        v_moved = [sig(f"v_moved{t}", 16 * (16 - 2 * (t == TILES - 1))) for t in range(TILES)]
        c_ident = sig("c_ident")
        c_dve = sig("c_dve")
        n_x = sig("n_x", 16)
        n_steps = sig("n_steps", 5)
        n_var = sig("n_var")
        n_lnv = sig("n_lnv")
        n_rstd = sig("n_rstd")
        n_xn = sig("n_xn")
        n_tr = sig("n_tr")
        n_state = sig("n_state")
        rot_ready = sig("rot_ready")
        xs_ready = sig("xs_ready", 2)
        FILLS = 10 * TILES
        ring_full = sig("ring_full", FILLS)
        ring_copied = sig("ring_copied", FILLS)
        qk_full = sig("qk_full", 2 * TILES)
        qk_sq = sig("qk_sq", 2 * TILES)
        qk_rot = sig("qk_rot", 4 * TILES)
        ss_sum = sig("ss_sum", TILES)
        ss_ready = sig("ss_ready", TILES)
        ss_ln = sig("ss_ln", TILES)
        rs_ready = sig("rs_ready", TILES)
        newton = sig("newton", 2 * TILES)
        rn_ready = sig("rn_ready", TILES)
        qk_added = sig("qk_added", TILES)
        qk_scaled = sig("qk_scaled", TILES)
        sc_full = sig("sc_full", TILES)
        max_ready = sig("max_ready", TILES)
        sc_sub = sig("sc_sub", TILES)
        exp_ready = sig("exp_ready", TILES)
        den_ready = sig("den_ready", TILES)
        rden_ready = sig("rden_ready", TILES)
        av_full = sig("av_full", TILES)
        o_ready = sig("o_ready", TILES)
        wo_full = sig("wo_full")
        x_attn = sig("x_attn")
        xs2_ready = sig("xs2_ready", 2)
        mean_full = sig("mean_full")
        xc_ready = sig("xc_ready")
        xsq_ready = sig("xsq_ready")
        var_full = sig("var_full")
        lnv_ready = sig("lnv_ready")
        rstd_ready = sig("rstd_ready")
        xh_ready = sig("xh_ready")
        xn_ready = sig("xn_ready")
        gate_full = sig("gate_full", 3)
        lin_full = sig("lin_full", 3)
        gelu_ready = sig("gelu_ready", 3)
        u_ready = sig("u_ready", 3)
        w2_full = sig("w2_full")
        x_ffn = sig("x_ffn")

        SLOTS = TILES + 2
        order = []
        for s in range(SLOTS):
            order += [("v", s)] * 2 * (s < TILES)
            order += [("p", s - 2)] * 2 * (s >= 2)
            order += [("t", s - 1)] * 4 * (1 <= s <= TILES)
            order += [("o", s - 2)] * 2 * (s >= 2)
        assert len(order) == FILLS

        def first_fill(kind, t):
            return order.index((kind, t))

        def state_cols(b, first, n):
            return bass.ds(b * SHIFTED + first, n)

        with nc.Block() as block:

            @block.sync
            def _(sp):
                for n, (to, of) in enumerate(((mask_f[:, :, :], win_mask), (rot_base[:, :, :, :], rotary))):
                    sp.dma_start(to, of).then_inc(s_const.sem, 16)
                with sp.Fori(0, B) as b:
                    sp.wait_ge(n_xn.sem, n_xn.at(b, 0))
                    sp.dma_start(xtok, x[bass.ds(b, 1), :, :].rearrange("o (t p) d -> p (o t) d", p=P)).then_inc(n_x.sem, 16)
                with sp.Fori(0, DEPTH) as l:
                    sp.wait_ge(qk_full.sem, l * (B * qk_full.per))
                    sp.dma_start(wqkv[:, :], w_qkv[bass.ds(l, 1), :, :].rearrange("o p n -> p (o n)")).then_inc(s_wqkv.sem, 16)
                    sp.wait_ge(rot_ready.sem, rot_ready.at(l, 0))
                    sp.dma_start(qks[:, :, :], qk_scale[bass.ds(l, 1), :, :].to_broadcast([P, 4, DH])).then_inc(s_qks.sem, 16)
                    sp.wait_ge(x_ffn.sem, l * B)
                    sp.dma_start(wo[:, :, :], w_o[bass.ds(l, 1), :, :].rearrange("o p (c n) -> p (o c) n", n=P)).then_inc(s_wrest.sem, 16)
                    sp.dma_start(w1[:, :], w_1[bass.ds(l, 1), :, :].rearrange("o p n -> p (o n)")).then_inc(s_wrest.sem, 16)
                    sp.dma_start(w2[:, :, :], w_2[bass.ds(l, 1), :, :].rearrange("o p (c n) -> p (o c) n", n=P)).then_inc(s_wrest.sem, 16)
                    sp.dma_start(col[:, :], cols[bass.ds(l, 1), :, :].rearrange("o p n -> p (o n)")).then_inc(s_wrest.sem, 16)
                    with sp.Fori(0, B) as b:
                        it = l * B + b
                        sp.wait_ge(av_full.sem, av_full.at(it, 0))
                        for t in range(TILES):
                            sp.wait_ge(ring_copied.sem, ring_copied.at(it, first_fill("v", t) + 2))
                            for q in range(TW):
                                w = TW * t + q
                                for par in range(2):
                                    of = v_tok[WIN * q:WIN * (q + 1), t % 2, par, :]
                                    sp.dma_start(v_win[64 * par + WIN:64 * par + 2 * WIN, w, :], of).then_inc(v_moved[t].sem, 16)
                                    if w + 1 < WINDOWS:
                                        sp.dma_start(v_win[64 * par:64 * par + WIN, w + 1, :], of).then_inc(v_moved[t].sem, 16)

            @block.gpsimd
            def _(pool):
                nc.gpsimd.memset(ident[:, :], 0.0).then_inc(c_ident.sem, 1)
                pool.wait_ge(c_ident.sem, 1)
                nc.gpsimd.affine_select(out=ident[:, :], in_=ident[:, :], compare_op=ALU.not_equal, fill=1.0,
                                        base=0, pattern=[[-1, P]], channel_multiplier=1).then_inc(c_ident.sem, 1)
                pool.wait_ge(s_const.sem, 32)
                with pool.Fori(0, DEPTH) as l:
                    pool.wait_ge(s_qks.sem, s_qks.at(l, 16))
                    pool.wait_ge(qk_rot.sem, l * (B * qk_rot.per))
                    for k in range(4):
                        ins = nc.gpsimd.tensor_tensor(
                            rot[:, k, :, :], rot_base[:, k, :, :],
                            qks[:, k:k + 1, :].to_broadcast([P, TILES, DH]), ALU.mult)
                    ins.then_inc(rot_ready.sem, 1)
                    with pool.Fori(0, B) as b:
                        it = l * B + b
                        for t in range(TILES):
                            pool.wait_ge(qk_rot.sem, qk_rot.at(it, 4 * (t + 1)))
                            nc.gpsimd.tensor_tensor(t1[:, :], t1[:, :], t2[:, :], ALU.add).then_inc(qk_added.sem, 1)
                            pool.wait_ge(qk_added.sem, qk_added.at(it, t + 1))
                            pool.wait_ge(rn_ready.sem, rn_ready.at(it, t + 1))
                            if t >= 1:
                                pool.wait_ge(ring_full.sem, ring_full.at(it, first_fill("t", t - 1) + 4))
                            else:
                                pool.wait_ge(ring_full.sem, ring_full.at(it, 0))
                            nc.gpsimd.tensor_tensor(
                                qkn[:, :].rearrange("p (h d) -> p h d", d=DH), t1[:, :].rearrange("p (h d) -> p h d", d=DH),
                                rn[:, :].unsqueeze(2).to_broadcast([P, 2 * HEADS, DH]), ALU.mult).then_inc(qk_scaled.sem, 1)

            @block.tensor
            def _(pe):
                pe.wait_ge(c_ident.sem, 2)
                with pe.Fori(0, B) as b:
                    pe.wait_ge(n_state.sem, n_state.at(b, 0))
                    pe.wait_ge(n_xn.sem, n_xn.at(b, 1))
                    for t in range(TILES):
                        ins = nc.tensor.transpose(ring[:, 0, t * P:(t + 1) * P], xntok[:, t, :], ident[:, :])
                    ins.then_inc(n_tr.sem, 1)
                pe.wait_ge(n_state.sem, B)
                pe.wait_ge(c_dve.sem, 6 + B)

                with pe.Fori(0, DEPTH) as l:
                    with pe.Fori(0, B) as b:
                        it = l * B + b

                        def ring_bank(f):
                            pe.wait_ge(ring_copied.sem, ring_copied.at(it, max(f - 1, 0)))
                            return ring[:, f % 2, :]

                        def project_v(t):
                            for par in range(2):
                                to = ring_bank(first_fill("v", t) + par)
                                nc.tensor.matmul(to, xs[:, t * P:(t + 1) * P], wqkv[:, 2 * INNER + 512 * par:2 * INNER + 512 * (par + 1)],
                                                 start=True, stop=True).then_inc(ring_full.sem, 1)

                        def project_qk(t):
                            pe.wait_ge(qk_rot.sem, qk_rot.at(it, 4 * t))
                            pe.wait_ge(qk_sq.sem, qk_sq.at(it, 2 * t))
                            if t == 0:
                                pe.wait_ge(x_ffn.sem, x_ffn.at(it, 0))
                            for half in range(2):
                                for n in range(2):
                                    c = 2 * half + n
                                    ins = nc.tensor.matmul(qk_ps[:, c, :], xs[:, t * P:(t + 1) * P], wqkv[:, 512 * c:512 * (c + 1)],
                                                           start=True, stop=True)
                                ins.then_inc(qk_full.sem, 1)

                        def transpose_qk(t):
                            pe.wait_ge(qk_scaled.sem, qk_scaled.at(it, t + 1))
                            for f in range(4):
                                to = ring_bank(first_fill("t", t) + f)
                                for n in range(4):
                                    c = 4 * f + n
                                    ins = nc.tensor.transpose(to[:, n * P:(n + 1) * P], qkn[:, c * P:(c + 1) * P], ident[:, :])
                                ins.then_inc(ring_full.sem, 1)

                        def scores(t):
                            pe.wait_ge(ring_copied.sem, ring_copied.at(it, first_fill("t", t) + 4))
                            pe.wait_ge(o_ready.sem, o_ready.at(it, t))
                            for par in range(2):
                                nc.tensor.matmul(sc_ps[:, par, :], ident_bf[:, :], mask_bf[:, int(t > 0), :, :],
                                                 start=True, stop=False, skip_group_check=True)
                            for pair in range(PAIRS):
                                for q in range(TW):
                                    for par in range(2):
                                        ins = nc.tensor.matmul(
                                            sc_ps[WIN * q:WIN * (q + 1), par, 64 * pair:64 * (pair + 1)],
                                            qT[64 * par:64 * (par + 1), pair, WIN * q:WIN * (q + 1)],
                                            kT[64 * par:64 * (par + 1), pair, P * t + WIN * q:P * t + WIN * (q + 2)],
                                            start=False, stop=True, skip_group_check=True)
                            ins.then_inc(sc_full.sem, 1)

                        def transpose_p(t):
                            pe.wait_ge(exp_ready.sem, exp_ready.at(it, t + 1))
                            for f in range(2):
                                to = ring_bank(first_fill("p", t) + f)
                                for n in range(4):
                                    c = 4 * f + n
                                    ins = nc.tensor.transpose(to[:, n * P:(n + 1) * P], pe_[:, c * P:(c + 1) * P], ident[:, :])
                                ins.then_inc(ring_full.sem, 1)

                        def attend(t):
                            pe.wait_ge(ring_copied.sem, ring_copied.at(it, first_fill("p", t) + 2))
                            pe.wait_ge(v_moved[t].sem, v_moved[t].at(it, v_moved[t].per))
                            pe.wait_ge(sc_sub.sem, sc_sub.at(it, t + 1))
                            nc.tensor.matmul(sc_ps[:, 0, 0:DH], prT[0:64, 0, :], v_win[0:64, TW * t, 0:DH], start=True, stop=True)
                            for pair in range(PAIRS):
                                for q in range(TW):
                                    for par in range(2):
                                        ins = nc.tensor.matmul(
                                            sc_ps[WIN * q:WIN * (q + 1), par, DH * pair:DH * (pair + 1)],
                                            prT[64 * par:64 * (par + 1), pair, WIN * q:WIN * (q + 1)],
                                            v_win[64 * par:64 * (par + 1), TW * t + q, DH * pair:DH * (pair + 1)],
                                            start=True, stop=True)
                            ins.then_inc(av_full.sem, 1)

                        def transpose_o(t):
                            pe.wait_ge(o_ready.sem, o_ready.at(it, t + 1))
                            for f in range(2):
                                to = ring_bank(first_fill("o", t) + f)
                                for n in range(4):
                                    c = 4 * f + n
                                    ins = nc.tensor.transpose(to[:, n * P:(n + 1) * P], o_tok[:, c * P:(c + 1) * P], ident[:, :])
                                ins.then_inc(ring_full.sem, 1)

                        pe.wait_ge(s_wqkv.sem, s_wqkv.at(l, 16))
                        pe.wait_ge(xs_ready.sem, xs_ready.at(it, 2))
                        for s in range(SLOTS):
                            if s < TILES:
                                project_v(s)
                                project_qk(s)
                            if s >= 2:
                                transpose_p(s - 2)
                                attend(s - 2)
                            if 1 <= s <= TILES:
                                transpose_qk(s - 1)
                            if s >= 2:
                                transpose_o(s - 2)
                            if 1 <= s <= TILES:
                                scores(s - 1)

                        pe.wait_ge(s_wrest.sem, s_wrest.at(l, 64))
                        pe.wait_ge(ring_copied.sem, ring_copied.at(it, FILLS))
                        pe.wait_ge(qk_rot.sem, qk_rot.at(it, 4 * TILES))
                        pe.wait_ge(qk_sq.sem, qk_sq.at(it, 2 * TILES))
                        for c in range(PAIRS):
                            ins = nc.tensor.matmul(qk_ps[:, 0, :], wo[:, c, :], oT[:, c, :], start=(c == 0), stop=(c == PAIRS - 1))
                        ins.then_inc(wo_full.sem, 1)

                        pe.wait_ge(xs2_ready.sem, xs2_ready.at(it, 2))
                        nc.tensor.matmul(qk_ps[:, 1, :], mean_w[:, :], xs[:, :], start=True, stop=True).then_inc(mean_full.sem, 1)
                        pe.wait_ge(xsq_ready.sem, xsq_ready.at(it, 1))
                        nc.tensor.matmul(qk_ps[:, 2, :], mean_w[:, :], xsq[:, :], start=True, stop=True).then_inc(var_full.sem, 1)
                        pe.wait_ge(xn_ready.sem, xn_ready.at(it, 1))
                        for c, m in enumerate(FCH):
                            if c == 2:
                                pe.wait_ge(u_ready.sem, u_ready.at(it, 1))
                            nc.tensor.matmul(qk_ps[0:m, c % 2, :], w1[:, FF + P * c:FF + P * c + m], xn[:, :],
                                             start=True, stop=True).then_inc(gate_full.sem, 1)
                            nc.tensor.matmul(qk_ps[0:m, 2 + c % 2, :], w1[:, P * c:P * c + m], xn[:, :],
                                             start=True, stop=True).then_inc(lin_full.sem, 1)
                        for c, m in enumerate(FCH):
                            pe.wait_ge(u_ready.sem, u_ready.at(it, max(c + 1, 2)))
                            ins = nc.tensor.matmul(qk_ps[:, 1, :], w2[0:m, c, :], u[0:m, c, :], start=(c == 0), stop=(c == 2))
                        ins.then_inc(w2_full.sem, 1)

            @block.scalar
            def _(act):
                with act.Fori(0, B) as b:
                    act.wait_ge(n_var.sem, n_var.at(b, 1))
                    nc.scalar.activation(lv[:, :], veps[:, :], ACT.Ln).then_inc(n_lnv.sem, 1)
                    act.wait_ge(n_lnv.sem, n_lnv.at(b, 1))
                    nc.scalar.activation(rstd0[:, :], lv[:, :], ACT.Exp, scale=-0.5).then_inc(n_rstd.sem, 1)

                with act.Fori(0, DEPTH) as l:
                    with act.Fori(0, B) as b:
                        it = l * B + b

                        def ring_out(to, kind, t, f):
                            n = first_fill(kind, t) + f
                            act.wait_ge(ring_full.sem, ring_full.at(it, n + 1))
                            nc.scalar.copy(to, ring[:, n % 2, :]).then_inc(ring_copied.sem, 1)

                        for s in range(SLOTS):
                            if s < TILES:
                                before = v_moved[(s - 2) % TILES]
                                act.wait_ge(before.sem, before.at(it, before.per if s >= 2 else 0))
                                for par in range(2):
                                    ring_out(v_tok[:, s % 2, par, :], "v", s, par)
                                for half in range(2):
                                    act.wait_ge(ss_sum.sem, ss_sum.at(it, s))
                                    act.wait_ge(qk_full.sem, qk_full.at(it, 2 * s + half + 1))
                                    nc.scalar.activation(sq[:, INNER * half:INNER * (half + 1)].rearrange("p (a n) -> p a n", a=2), qk_ps[:, 2 * half:2 * half + 2, :],
                                                         ACT.Square).then_inc(qk_sq.sem, 1)
                            if s >= 2:
                                for f in range(2):
                                    ring_out(prT[:, 4 * f:4 * f + 4, :], "p", s - 2, f)
                            if 1 <= s <= TILES:
                                for f in range(4):
                                    if f < 2:
                                        to = qT[:, 4 * f:4 * f + 4, :]
                                    else:
                                        to = kT[:, 4 * f - 8:4 * f - 4, WIN + P * (s - 1):WIN + P * s]
                                    ring_out(to, "t", s - 1, f)
                            if s < TILES:
                                act.wait_ge(ss_ready.sem, ss_ready.at(it, s + 1))
                                nc.scalar.activation(lnss[:, :], ss[:, :], ACT.Ln, scale=LN_SCALE).then_inc(ss_ln.sem, 1)
                                act.wait_ge(ss_ln.sem, ss_ln.at(it, s + 1))
                                act.wait_ge(rn_ready.sem, rn_ready.at(it, s))
                                nc.scalar.activation(rs[:, :], lnss[:, :], ACT.Exp, scale=-0.5).then_inc(rs_ready.sem, 1)
                            if s >= 2:
                                for f in range(2):
                                    ring_out(oT[:, 4 * f:4 * f + 4, P * (s - 2):P * (s - 1)], "o", s - 2, f)
                            if 1 <= s <= TILES:
                                act.wait_ge(sc_sub.sem, sc_sub.at(it, s))
                                act.wait_ge(den_ready.sem, den_ready.at(it, s - 1))
                                nc.scalar.activation(pe_[:, :], pr[:, :], ACT.Exp, scale=8.0).then_inc(exp_ready.sem, 1)

                        act.wait_ge(xc_ready.sem, xc_ready.at(it, 1))
                        nc.scalar.activation(xsq[:, :], xc[:, :], ACT.Square).then_inc(xsq_ready.sem, 1)
                        act.wait_ge(var_full.sem, var_full.at(it, 1))
                        nc.scalar.activation(lnv[:, :], qk_ps[:, 2, :], ACT.Ln, bias=eps_col[:, 0:1]).then_inc(lnv_ready.sem, 1)
                        act.wait_ge(lnv_ready.sem, lnv_ready.at(it, 1))
                        nc.scalar.activation(rstd[:, :], lnv[:, :], ACT.Exp, scale=-0.5).then_inc(rstd_ready.sem, 1)
                        for c, m in enumerate(FCH):
                            act.wait_ge(gate_full.sem, gate_full.at(it, c + 1))
                            nc.scalar.activation(gel[0:m, c, :], qk_ps[0:m, c % 2, :], ACT.Gelu, bias=col[0:m, 3 + c:4 + c]).then_inc(gelu_ready.sem, 1)

            @block.vector
            def _(dve):
                def copy_at(to, of):
                    return nc.vector.tensor_scalar(to, of, 1.0, None, ALU.mult)

                nc.vector.memset(mean_w[:, :], 1.0 / P).then_inc(c_dve.sem, 1)
                nc.vector.memset(kT[:, :, 0:WIN], 0.0).then_inc(c_dve.sem, 1)
                nc.vector.memset(v_win[:, 0, :], 0.0).then_inc(c_dve.sem, 1)
                dve.wait_ge(s_const.sem, 32)
                nc.vector.tensor_copy(mask_bf[:, :, :, :], mask_f[:, :, :].unsqueeze(2).to_broadcast([P, 2, PAIRS, 2 * WIN])).then_inc(c_dve.sem, 1)
                dve.wait_ge(c_ident.sem, 2)
                nc.vector.tensor_copy(ident_bf[:, :], ident[:, :]).then_inc(c_dve.sem, 1)
                nc.vector.memset(eps_col[:, :], EPS).then_inc(c_dve.sem, 1)
                for b in range(B):
                    nc.vector.memset(state[:, b * SHIFTED:b * SHIFTED + 1], 0.0).then_inc(c_dve.sem, 1)
                dve.wait_ge(c_dve.sem, 6 + B)
                with dve.Fori(0, B) as b:
                    dve.wait_ge(n_x.sem, n_x.at(b, 16))
                    dve.wait_ge(n_state.sem, n_state.at(b, 0))
                    per_token = lambda a: a[:, :].unsqueeze(2).to_broadcast([P, TILES, P])
                    nc.vector.tensor_reduce(msum[:, :], xtok, AX.X, ALU.add).then_inc(n_steps.sem, 1)
                    dve.wait_ge(n_steps.sem, n_steps.at(b, 1))
                    nc.vector.tensor_scalar(mmean[:, :], msum[:, :], 1.0 / P, None, ALU.mult).then_inc(n_steps.sem, 1)
                    dve.wait_ge(n_steps.sem, n_steps.at(b, 2))
                    nc.vector.tensor_tensor(xctok, xtok, per_token(mmean), ALU.subtract).then_inc(n_steps.sem, 1)
                    dve.wait_ge(n_steps.sem, n_steps.at(b, 3))
                    nc.vector.tensor_tensor(sqtok, xctok, xctok, ALU.mult).then_inc(n_steps.sem, 1)
                    dve.wait_ge(n_steps.sem, n_steps.at(b, 4))
                    nc.vector.tensor_reduce(vsum[:, :], sqtok, AX.X, ALU.add).then_inc(n_steps.sem, 1)
                    dve.wait_ge(n_steps.sem, n_steps.at(b, 5))
                    nc.vector.tensor_scalar(veps[:, :], vsum[:, :], 1.0 / P, EPS, ALU.mult, ALU.add).then_inc(n_var.sem, 1)
                    dve.wait_ge(n_rstd.sem, n_rstd.at(b, 1))
                    nc.vector.tensor_tensor(xntok, xctok, per_token(rstd0), ALU.mult).then_inc(n_xn.sem, 1)
                    dve.wait_ge(n_tr.sem, n_tr.at(b, 1))
                    copy_at(state[:, state_cols(b, 1, T)], ring[:, 0, :]).then_inc(n_state.sem, 1)
                dve.wait_ge(n_state.sem, B)

                with dve.Fori(0, DEPTH) as l:
                    with dve.Fori(0, B) as b:
                        it = l * B + b

                        def shift_tokens(done):
                            copy_at(xs[0:64, :], state[0:64, state_cols(b, 1, T)]).then_inc(done.sem, 1)
                            copy_at(xs[64:P, :], state[64:P, state_cols(b, 0, T)]).then_inc(done.sem, 1)

                        def rotate(t):
                            if t == 0:
                                dve.wait_ge(rot_ready.sem, rot_ready.at(l, 1))
                            dve.wait_ge(qk_scaled.sem, qk_scaled.at(it, t))
                            for half in range(2):
                                dve.wait_ge(qk_full.sem, qk_full.at(it, 2 * t + half + 1))
                                dve.wait_ge(qk_sq.sem, qk_sq.at(it, 2 * t + half + 1))
                                of = qk_ps[:, 2 * half:2 * half + 2, :].rearrange("p a n -> p (a n)")
                                own = of.rearrange("p (h d) -> p h d", d=DH)
                                to = slice(INNER * half, INNER * (half + 1))
                                nc.vector.tensor_tensor(
                                    t1[:, to].rearrange("p (h d) -> p h d", d=DH), own,
                                    rot[:, 2 * half, t:t + 1, :].to_broadcast([P, HEADS, DH]), ALU.mult).then_inc(qk_rot.sem, 1)
                                swapped = of.rearrange("p (h s d) -> p h s d", s=2, d=DH // 2)[:, :, ::-1, :]
                                nc.vector.tensor_tensor(
                                    t2[:, to].rearrange("p (h s d) -> p h s d", s=2, d=DH // 2), swapped,
                                    rot[:, 2 * half + 1, t:t + 1, :].to_broadcast([P, HEADS, DH]).rearrange("p h (s d) -> p h s d", s=2),
                                    ALU.mult).then_inc(qk_rot.sem, 1)

                        def sum_squares(t):
                            dve.wait_ge(qk_sq.sem, qk_sq.at(it, 2 * t + 2))
                            nc.vector.tensor_reduce(lnsum[:, :], sq[:, :].rearrange("p (h d) -> p h d", d=DH), AX.X, ALU.add).then_inc(ss_sum.sem, 1)
                            dve.wait_ge(ss_sum.sem, ss_sum.at(it, t + 1))
                            nc.vector.tensor_scalar(ss[:, :], lnsum[:, :], NORM_FLOOR, None, ALU.max).then_inc(ss_ready.sem, 1)

                        def newton_step(t):
                            dve.wait_ge(rs_ready.sem, rs_ready.at(it, t + 1))
                            dve.wait_ge(qk_scaled.sem, qk_scaled.at(it, t))
                            nc.vector.tensor_tensor(nw1[:, :], rs[:, :], rs[:, :], ALU.mult).then_inc(newton.sem, 1)
                            dve.wait_ge(newton.sem, newton.at(it, 2 * t + 1))
                            nc.vector.scalar_tensor_tensor(nw2[:, :], nw1[:, :], -0.5 * LN_SCALE * LN_SCALE ** 0.5, ss[:, :], ALU.mult, ALU.mult).then_inc(newton.sem, 1)
                            dve.wait_ge(newton.sem, newton.at(it, 2 * t + 2))
                            nc.vector.scalar_tensor_tensor(rn[:, :], nw2[:, :], 1.5 * LN_SCALE ** 0.5, rs[:, :], ALU.add, ALU.mult).then_inc(rn_ready.sem, 1)

                        def row_max(t):
                            dve.wait_ge(sc_full.sem, sc_full.at(it, t + 1))
                            sc = sc_ps[:, :, :].rearrange("p a (h k) -> p a h k", k=64)
                            nc.vector.tensor_reduce(smax[:, :], sc_ps[:, :, :].rearrange("p a n -> p (a n)").rearrange("p (h k) -> p h k", k=64), AX.X, ALU.max).then_inc(max_ready.sem, 1)
                            dve.wait_ge(max_ready.sem, max_ready.at(it, t + 1))
                            for par in range(2):
                                ins = nc.vector.tensor_tensor(
                                    pr[:, :].rearrange("p (h a k) -> p a h k", a=2, k=64)[:, par, :, :], sc[:, par, :, :],
                                    smax[:, PAIRS * par:PAIRS * (par + 1)].unsqueeze(2).to_broadcast([P, PAIRS, 64]), ALU.subtract)
                            ins.then_inc(sc_sub.sem, 1)

                        def row_sum(t):
                            dve.wait_ge(exp_ready.sem, exp_ready.at(it, t + 1))
                            nc.vector.tensor_reduce(den[:, :], pe_[:, :].rearrange("p (h k) -> p h k", k=64), AX.X, ALU.add).then_inc(den_ready.sem, 1)
                            dve.wait_ge(den_ready.sem, den_ready.at(it, t + 1))
                            nc.vector.reciprocal(rden[:, t % 2, :], den[:, :]).then_inc(rden_ready.sem, 1)

                        def normalise(t):
                            dve.wait_ge(av_full.sem, av_full.at(it, t + 1))
                            dve.wait_ge(rden_ready.sem, rden_ready.at(it, t + 1))
                            if t >= 1:
                                dve.wait_ge(ring_full.sem, ring_full.at(it, first_fill("o", t - 1) + 2))
                            for par in range(2):
                                ins = nc.vector.tensor_tensor(
                                    o_tok[:, :].rearrange("p (h a d) -> p a h d", a=2, d=DH)[:, par, :, :],
                                    sc_ps[:, par, :].rearrange("p (h d) -> p h d", d=DH),
                                    rden[:, t % 2, :].rearrange("p (h a) -> p a h", a=2)[:, par, :].unsqueeze(2).to_broadcast([P, PAIRS, DH]), ALU.mult)
                            ins.then_inc(o_ready.sem, 1)

                        dve.wait_ge(x_ffn.sem, x_ffn.at(it, 0))
                        shift_tokens(xs_ready)
                        for s in range(SLOTS):
                            if s < TILES:
                                rotate(s)
                                sum_squares(s)
                            if 2 <= s:
                                row_sum(s - 2)
                                normalise(s - 2)
                            if s < TILES:
                                newton_step(s)
                            if 1 <= s <= TILES:
                                row_max(s - 1)

                        dve.wait_ge(wo_full.sem, wo_full.at(it, 1))
                        now = state[:, state_cols(b, 1, T)]
                        nc.vector.tensor_tensor(now, qk_ps[:, 0, :], now, ALU.add).then_inc(x_attn.sem, 1)
                        dve.wait_ge(x_attn.sem, x_attn.at(it, 1))
                        shift_tokens(xs2_ready)
                        dve.wait_ge(xs2_ready.sem, xs2_ready.at(it, 2))
                        dve.wait_ge(mean_full.sem, mean_full.at(it, 1))
                        nc.vector.tensor_tensor(xc[:, :], xs[:, :], qk_ps[:, 1, :], ALU.subtract).then_inc(xc_ready.sem, 1)
                        dve.wait_ge(rstd_ready.sem, rstd_ready.at(it, 1))
                        nc.vector.tensor_tensor(xh[:, :], xc[:, :], rstd[:, :], ALU.mult).then_inc(xh_ready.sem, 1)
                        dve.wait_ge(xh_ready.sem, xh_ready.at(it, 1))
                        nc.vector.tensor_scalar(xn[:, :], xh[:, :], col[:, 6:7], col[:, 7:8], ALU.mult, ALU.add).then_inc(xn_ready.sem, 1)
                        for c, m in enumerate(FCH):
                            dve.wait_ge(gelu_ready.sem, gelu_ready.at(it, c + 1))
                            dve.wait_ge(lin_full.sem, lin_full.at(it, c + 1))
                            nc.vector.scalar_tensor_tensor(u[0:m, c, :], qk_ps[0:m, 2 + c % 2, :], col[0:m, c:c + 1], gel[0:m, c, :],
                                                           ALU.add, ALU.mult).then_inc(u_ready.sem, 1)
                        dve.wait_ge(w2_full.sem, w2_full.at(it, 1))
                        nc.vector.scalar_tensor_tensor(now, qk_ps[:, 1, :], col[:, 8:9], now, ALU.add, ALU.add).then_inc(x_ffn.sem, 1)


RH, RK, RV = 4, 32, 64
NE, BN = 8, 64
AK = P ** -0.5
STEPS = 52


def build_mixers(nc, state, x, out, w_ret, w_ro, ret_cols, g_norm, ret_rot, ret_decay, ret_diag, ret_block,
                 w_att, att_rot, att_mask, w_gate, w_down, w_up, b_down, b_up, expert_rows, before):
    ctx = ExitStack()
    with ctx:
        def sb(name, shape, dt=F32):
            return ctx.enter_context(nc.sbuf_tensor(name, shape, dt))

        def sig(name, per=1):
            return Signal(ctx, nc, name, per)

        proj = ctx.enter_context(nc.psum_tensor("proj", [P, 2, 512], F32))
        head = ctx.enter_context(nc.psum_tensor("head", [P, 4, 512], F32))
        turn = ctx.enter_context(nc.psum_tensor("turn", [P, 512], F32))
        outs = ctx.enter_context(nc.psum_tensor("outs", [P, 512], F32))

        c_ident = sb("m_ident", [P, P])
        mean_w = sb("m_mean_w", [P, P])
        eps_col = sb("m_eps_col", [P, 1])
        wr = sb("wr", [P, 6 * P])
        wro = sb("wro", [P, 2, P])
        rcol = sb("rcol", [P, 3])
        gnw = sb("gnw", [P, 2 * P])
        rrot = sb("rrot", [P, 2, TILES, 2 * P])
        rdec = sb("rdec", [P, 2, P])
        rdiag = sb("rdiag", [P, RH, P])
        rblock = sb("rblock", [P, 2 * P])
        wa = sb("wa", [P, 3 * P])
        arot = sb("arot", [P, 2, TILES, 2 * P])
        amask = sb("amask", [P, TILES, T])
        wg = sb("wg", [P, NE])
        wd = sb("wd", [P, NE * BN])
        wu = sb("wu", [P, 4, P])
        bd = sb("bd", [P, 4])
        bu = sb("bu", [NE, P])
        erows = sb("erows", [NE, 4, P])
        ebefore = sb("ebefore", [P, NE, NE])

        xtok = sb("m_xtok", [P, TILES, P])
        msum = sb("m_msum", [P, TILES])
        mmean = sb("m_mmean", [P, TILES])
        vsum = sb("m_vsum", [P, TILES])
        xctok = sb("m_xctok", [P, TILES, P])
        sqtok = sb("m_sqtok", [P, TILES, P])
        var = sb("m_var", [P, TILES])
        lv = sb("m_lv", [P, TILES])
        rstd0 = sb("m_rstd0", [P, TILES])
        xntok = sb("m_xntok", [P, TILES, P])
        nrtok = sb("m_nrtok", [P, TILES, P])
        x0T = sb("x0T", [P, T])
        xnT = sb("xnT", [P, T])
        nrT = sb("nrT", [P, T])
        rt1 = sb("rt1", [P, 2 * P])
        rt2 = sb("rt2", [P, 2 * P])
        rqk = sb("rqk", [P, 2 * P])
        qcr = sb("qcr", [P, P])
        kst = sb("kst", [P, P])
        vsb = sb("vsb", [P, 2 * P])
        sg = sb("sg", [P, 2 * P])
        rT = sb("rT", [P, 3, P])
        at = sb("at", [P, RH, P])
        st = sb("st", [P, 2 * P])
        stn = sb("stn", [P, 2 * P])
        osq = sb("osq", [P, 2 * P])
        oss = sb("oss", [P, RH])
        oln = sb("oln", [P, RH])
        orst = sb("orst", [P, RH])
        o1 = sb("o1", [P, 2 * P])
        o2 = sb("o2", [P, 2 * P])
        o3 = sb("o3", [P, 2 * P])
        orT = sb("orT", [P, 2, T])
        sT = sb("sT", [P, T])
        gT = sb("gT", [P, T])
        sgT = sb("sgT", [P, T])
        x1T = sb("x1T", [P, T])
        xc = sb("m_xc", [P, T])
        xsq = sb("m_xsq", [P, T])
        lnv = sb("m_lnv", [P, T])
        rstd = sb("m_rstd", [P, T])
        xm = sb("xm", [P, T])
        aq1 = sb("aq1", [P, 2 * P])
        aq2 = sb("aq2", [P, 2 * P])
        aqk = sb("aqk", [P, 2 * P])
        aqT = sb("aqT", [P, TILES, P])
        akT = sb("akT", [P, TILES, P])
        av = sb("av", [P, TILES, P])
        asc = sb("asc", [P, T])
        amx = sb("amx", [P, 1])
        aneg = sb("aneg", [P, 1])
        aex = sb("aex", [P, T])
        aden = sb("aden", [P, 1])
        arden = sb("arden", [P, 1])
        apr = sb("apr", [P, T])
        apT = sb("apT", [P, TILES, P])
        s1T = sb("s1T", [P, T])
        lg = sb("lg", [P, TILES, NE])
        beats = sb("beats", [P, TILES, NE, NE])
        ties = sb("ties", [P, TILES, NE, NE])
        tied = sb("tied", [P, TILES, NE, NE])
        wins = sb("wins", [P, TILES, NE, NE])
        rank = sb("rank", [P, TILES, NE])
        sel = sb("sel", [P, TILES, NE])
        gmx = sb("gmx", [P, TILES])
        gsub = sb("gsub", [P, TILES, NE])
        gex = sb("gex", [P, TILES, NE])
        gsel = sb("gsel", [P, TILES, NE])
        gden = sb("gden", [P, TILES])
        grd = sb("grd", [P, TILES])
        gate = sb("gate", [P, TILES, NE])
        gaT = sb("gaT", [NE, T])
        hid = sb("hid", [P, 4, T])
        hg = sb("hg", [P, 4, T])
        moe = sb("moe", [P, T])
        x2T = sb("x2T", [P, T])
        xo = sb("xo", [P, TILES, P])

        loads = [(wr[:, :], w_ret), (wro[:, :, :], w_ro), (rcol[:, :], ret_cols), (rrot[:, :, :, :], ret_rot),
                 (rdec[:, :, :], ret_decay), (rdiag[:, :, :], ret_diag), (rblock[:, :], ret_block), (wa[:, :], w_att),
                 (arot[:, :, :, :], att_rot), (amask[:, :, :], att_mask), (wg[:, :], w_gate), (wd[:, :], w_down),
                 (wu[:, :, :], w_up), (bd[:, :], b_down), (bu[:, :], b_up), (erows[:, :, :], expert_rows)]
        c_loads = sig("c_loads")
        m_ident = sig("m_identity")
        c_set = sig("c_set")
        x_in = sig("x_in", 16)
        steps = sig("steps", 0)
        x_stats = sig("x_stats", 2)
        x_ln = sig("x_ln", 2)
        x_rstd = sig("x_rstd", 2)
        xn_there = sig("xn_there", 2)
        xT_full = sig("xT_full", 3)
        xT_there = sig("xT_there", 3)
        r_proj = sig("r_proj", TILES)
        r_v = sig("r_v", TILES)
        r_sg = sig("r_sg", TILES)
        r_rot = sig("r_rot", TILES)
        r_dec = sig("r_dec", TILES)
        r_turned = sig("r_turned", TILES)
        r_T = sig("r_T", TILES)
        r_sc = sig("r_sc", TILES)
        r_at = sig("r_at", TILES)
        r_out = sig("r_out", TILES)
        r_upd = sig("r_upd", TILES - 1)
        r_state = sig("r_state", TILES - 1)
        r_sq = sig("r_sq", TILES)
        r_ms = sig("r_ms", TILES)
        r_ln = sig("r_ln", TILES)
        r_rstd = sig("r_rstd", TILES)
        r_o = sig("r_o", TILES)
        r_oturn = sig("r_oturn", TILES)
        r_oT = sig("r_oT", TILES)
        r_wo = sig("r_wo")
        s_gate = sig("s_gate")
        x1_there = sig("x1_there")
        m_mean = sig("m_mean")
        m_xc = sig("m_xc_there")
        m_sq = sig("m_sq")
        m_varf = sig("m_varf")
        m_lnv = sig("m_lnv_there")
        m_rstd = sig("m_rstd_there")
        xm_there = sig("xm_there")
        a_proj = sig("a_proj", TILES)
        a_v = sig("a_v", TILES)
        a_rot = sig("a_rot", TILES)
        a_turned = sig("a_turned", TILES)
        a_T = sig("a_T", TILES)
        a_sc = sig("a_sc", TILES)
        a_max = sig("a_max", TILES)
        a_exp = sig("a_exp", TILES)
        a_p = sig("a_p", TILES)
        a_pturn = sig("a_pturn", TILES)
        a_pT = sig("a_pT", TILES)
        a_out = sig("a_out", TILES)
        s1_there = sig("s1_there")
        e_lg = sig("e_lg")
        e_sub = sig("e_sub")
        e_exp = sig("e_exp")
        e_gate = sig("e_gate")
        e_gturn = sig("e_gturn")
        e_gT = sig("e_gT")
        e_down = sig("e_down", 4)
        e_hid = sig("e_hid", 4)
        e_spread = sig("e_spread", 4)
        e_hg = sig("e_hg", 4)
        e_up = sig("e_up")
        e_silu = sig("e_silu")
        x2_there = sig("x2_there")
        x2_turn = sig("x2_turn")
        xo_there = sig("xo_there")
        stored = sig("stored", 16)

        with nc.Block() as block:

            @block.sync
            def _(sp):
                sp.dma_start(gnw[:, :], g_norm.to_broadcast([P, 2 * P])).then_inc(c_loads.sem, 16)
                sp.dma_start(ebefore[:, :, :].rearrange("p e f -> p (e f)"), before.to_broadcast([P, NE * NE])).then_inc(c_loads.sem, 16)
                for to, of in loads:
                    sp.dma_start(to, of).then_inc(c_loads.sem, 16)
                with sp.Fori(0, B) as b:
                    sp.wait_ge(xT_full.sem, xT_full.at(b, 0))
                    sp.dma_start(xtok[:, :, :], x[bass.ds(b, 1), :, :].rearrange("o (t p) d -> p (o t) d", p=P)).then_inc(x_in.sem, 16)
                    sp.wait_ge(xo_there.sem, xo_there.at(b, 1))
                    sp.dma_start(out[bass.ds(b, 1), :, :].rearrange("o (t p) d -> p (o t) d", p=P), xo[:, :, :]).then_inc(stored.sem, 16)
                sp.wait_ge(stored.sem, 16 * B)

            all_loads = 16 * (len(loads) + 2)

            @block.gpsimd
            def _(pool):
                nc.gpsimd.memset(c_ident[:, :], 0.0).then_inc(m_ident.sem, 1)
                pool.wait_ge(m_ident.sem, 1)
                nc.gpsimd.affine_select(out=c_ident[:, :], in_=c_ident[:, :], compare_op=ALU.not_equal, fill=1.0,
                                        base=0, pattern=[[-1, P]], channel_multiplier=1).then_inc(m_ident.sem, 1)

            @block.tensor
            def _(pe):
                pe.wait_ge(m_ident.sem, 2)
                pe.wait_ge(c_set.sem, 2)
                pe.wait_ge(c_loads.sem, all_loads)
                with pe.Fori(0, B) as b:
                    def turn4(of, done, to=turn):
                        for t in range(TILES):
                            ins = nc.tensor.transpose(to[:, t * P:(t + 1) * P], of(t), c_ident[:, :])
                        ins.then_inc(done.sem, 1)

                    for n, of in enumerate((xtok, xntok, nrtok)):
                        if n == 0:
                            pe.wait_ge(x_in.sem, x_in.at(b, 16))
                            pe.wait_ge(xo_there.sem, xo_there.at(b, 0))
                        else:
                            pe.wait_ge(xn_there.sem, xn_there.at(b, n))
                            pe.wait_ge(xT_there.sem, xT_there.at(b, n))
                        turn4(lambda t: of[:, t, :], xT_full)
                    pe.wait_ge(xT_there.sem, xT_there.at(b, 3))

                    for t in range(TILES):
                        xt = nrT[:, t * P:(t + 1) * P]
                        pe.wait_ge(r_rot.sem, r_rot.at(b, t))
                        pe.wait_ge(r_sg.sem, r_sg.at(b, t))
                        if t == 0:
                            pe.wait_ge(a_rot.sem, a_rot.at(b, 0))
                        nc.tensor.matmul(proj[:, 0, :], xt, wr[:, 0:512], start=True, stop=True)
                        nc.tensor.matmul(proj[:, 1, 0:2 * P], xt, wr[:, 512:768], start=True, stop=True).then_inc(r_proj.sem, 1)
                        pe.wait_ge(r_dec.sem, r_dec.at(b, t + 1))
                        pe.wait_ge(r_oT.sem, r_oT.at(b, t))
                        for n, of in enumerate((rqk[:, 0:P], rqk[:, P:2 * P], qcr[:, :])):
                            ins = nc.tensor.transpose(turn[:, n * P:(n + 1) * P], of, c_ident[:, :])
                        ins.then_inc(r_turned.sem, 1)
                        pe.wait_ge(r_T.sem, r_T.at(b, t + 1))
                        pe.wait_ge(r_state.sem, r_state.at(b, t))
                        if t == 0:
                            pe.wait_ge(x2_there.sem, x2_there.at(b, 0))
                        for h in range(RH):
                            rows = slice(RK * h, RK * (h + 1))
                            ins = nc.tensor.matmul(head[:, h, 0:P], rT[rows, 1, :], rT[rows, 0, :], start=True, stop=True)
                        ins.then_inc(r_sc.sem, 1)
                        pe.wait_ge(r_v.sem, r_v.at(b, t + 1))
                        pe.wait_ge(r_at.sem, r_at.at(b, t + 1))
                        pe.wait_ge(r_o.sem, r_o.at(b, t))
                        if t > 0:
                            nc.tensor.matmul(outs[:, 0:2 * P], rT[:, 2, :], st[:, :], start=True, stop=False, skip_group_check=True)
                        for h in range(RH):
                            cols = slice(RV * h, RV * (h + 1))
                            ins = nc.tensor.matmul(outs[:, cols], at[:, h, :], vsb[:, cols], start=(t == 0 and h == 0), stop=(h == RH - 1),
                                                   skip_group_check=True)
                        ins.then_inc(r_out.sem, 1)
                        if t < TILES - 1:
                            nc.tensor.matmul(head[:, 3, 0:2 * P], kst[:, :], vsb[:, :], start=True, stop=True).then_inc(r_upd.sem, 1)
                        pe.wait_ge(r_o.sem, r_o.at(b, t + 1))
                        for n in range(2):
                            ins = nc.tensor.transpose(turn[:, n * P:(n + 1) * P], o3[:, n * P:(n + 1) * P], c_ident[:, :])
                        ins.then_inc(r_oturn.sem, 1)
                    pe.wait_ge(r_oT.sem, r_oT.at(b, TILES))
                    for n in range(2):
                        ins = nc.tensor.matmul(head[:, 0, :], wro[:, n, :], orT[:, n, :], start=(n == 0), stop=(n == 1))
                    ins.then_inc(r_wo.sem, 1)

                    pe.wait_ge(x1_there.sem, x1_there.at(b, 1))
                    nc.tensor.matmul(head[:, 1, :], mean_w[:, :], x1T[:, :], start=True, stop=True).then_inc(m_mean.sem, 1)
                    pe.wait_ge(m_sq.sem, m_sq.at(b, 1))
                    nc.tensor.matmul(head[:, 2, :], mean_w[:, :], xsq[:, :], start=True, stop=True).then_inc(m_varf.sem, 1)
                    pe.wait_ge(xm_there.sem, xm_there.at(b, 1))

                    for t in range(TILES):
                        ins = nc.tensor.matmul(head[:, 3, NE * t:NE * (t + 1)], xm[:, t * P:(t + 1) * P], wg[:, :], start=True, stop=True)
                    ins.then_inc(e_lg.sem, 1)

                    for t in range(TILES):
                        pe.wait_ge(a_rot.sem, a_rot.at(b, t))
                        pe.wait_ge(a_v.sem, a_v.at(b, t))
                        nc.tensor.matmul(proj[:, 0, 0:3 * P], xm[:, t * P:(t + 1) * P], wa[:, :], start=True, stop=True).then_inc(a_proj.sem, 1)
                        pe.wait_ge(a_rot.sem, a_rot.at(b, t + 1))
                        pe.wait_ge(a_T.sem, a_T.at(b, t))
                        for n in range(2):
                            ins = nc.tensor.transpose(turn[:, n * P:(n + 1) * P], aqk[:, n * P:(n + 1) * P], c_ident[:, :])
                        ins.then_inc(a_turned.sem, 1)
                    pe.wait_ge(a_T.sem, a_T.at(b, TILES))
                    for t in range(TILES):
                        pe.wait_ge(a_max.sem, a_max.at(b, t))
                        nc.tensor.matmul(head[:, 0, :], aqT[:, t, :], akT[:, :, :], start=True, stop=True).then_inc(a_sc.sem, 1)
                        pe.wait_ge(a_p.sem, a_p.at(b, t + 1))
                        turn4(lambda n: apr[:, n * P:(n + 1) * P], a_pturn)
                        pe.wait_ge(a_pT.sem, a_pT.at(b, t + 1))
                        for n in range(TILES):
                            ins = nc.tensor.matmul(outs[:, t * P:(t + 1) * P], av[:, n, :], apT[:, n, :], start=(n == 0), stop=(n == TILES - 1))
                        ins.then_inc(a_out.sem, 1)

                    pe.wait_ge(e_gate.sem, e_gate.at(b, 1))
                    for t in range(TILES):
                        ins = nc.tensor.transpose(turn[0:NE, t * P:(t + 1) * P], gate[:, t, :], c_ident[:, :])
                    ins.then_inc(e_gturn.sem, 1)
                    pe.wait_ge(e_gT.sem, e_gT.at(b, 1))
                    for c in range(4):
                        pe.wait_ge(e_hg.sem, e_hg.at(b, c))
                        nc.tensor.matmul(head[:, 1, :], wd[:, P * c:P * (c + 1)], xm[:, :], start=True, stop=True).then_inc(e_down.sem, 1)
                        nc.tensor.matmul(head[:, 2, :], erows[:, c, :], gaT[:, :], start=True, stop=True).then_inc(e_spread.sem, 1)
                    pe.wait_ge(e_hg.sem, e_hg.at(b, 4))
                    for c in range(4):
                        nc.tensor.matmul(head[:, 3, :], wu[:, c, :], hg[:, c, :], start=(c == 0), stop=False)
                    nc.tensor.matmul(head[:, 3, :], bu[:, :], gaT[:, :], start=False, stop=True).then_inc(e_up.sem, 1)
                    pe.wait_ge(x2_there.sem, x2_there.at(b, 1))
                    turn4(lambda t: x2T[:, t * P:(t + 1) * P], x2_turn)

            @block.scalar
            def _(act):
                act.wait_ge(c_set.sem, 2)
                act.wait_ge(c_loads.sem, all_loads)
                with act.Fori(0, B) as b:
                    for n in range(2):
                        act.wait_ge(x_stats.sem, x_stats.at(b, n + 1))
                        nc.scalar.activation(lv[:, :], var[:, :], ACT.Ln).then_inc(x_ln.sem, 1)
                        act.wait_ge(x_ln.sem, x_ln.at(b, n + 1))
                        nc.scalar.activation(rstd0[:, :], lv[:, :], ACT.Exp, scale=-0.5).then_inc(x_rstd.sem, 1)
                    nc.scalar.activation(sgT[:, :], state[:, bass.ds(b * SHIFTED + 1, T)], ACT.Silu).then_inc(s_gate.sem, 1)
                    for n, to in enumerate((x0T, xnT)):
                        act.wait_ge(xT_full.sem, xT_full.at(b, n + 1))
                        nc.scalar.copy(to[:, :], turn[:, :]).then_inc(xT_there.sem, 1)
                    act.wait_ge(xT_full.sem, xT_full.at(b, 3))
                    nc.scalar.activation(nrT[:, :], turn[:, :], ACT.Identity, bias=rcol[:, 1:2], scale=rcol[:, 0:1]).then_inc(xT_there.sem, 1)

                    for t in range(TILES):
                        act.wait_ge(r_rot.sem, r_rot.at(b, t + 1))
                        nc.scalar.copy(vsb[:, :], proj[:, 0, 2 * P:4 * P]).then_inc(r_v.sem, 1)
                        nc.scalar.activation(sg[:, :], proj[:, 1, 0:2 * P], ACT.Silu).then_inc(r_sg.sem, 1)
                        act.wait_ge(r_turned.sem, r_turned.at(b, t + 1))
                        nc.scalar.copy(rT[:, :, :], turn[:, 0:3 * P]).then_inc(r_T.sem, 1)
                        act.wait_ge(r_out.sem, r_out.at(b, t + 1))
                        nc.scalar.activation(osq[:, :], outs[:, 0:2 * P], ACT.Square).then_inc(r_sq.sem, 1)
                        act.wait_ge(r_ms.sem, r_ms.at(b, t + 1))
                        nc.scalar.activation(oln[:, :], oss[:, :], ACT.Ln, bias=eps_col[:, 0:1], scale=1.0 / RV).then_inc(r_ln.sem, 1)
                        act.wait_ge(r_ln.sem, r_ln.at(b, t + 1))
                        nc.scalar.activation(orst[:, :], oln[:, :], ACT.Exp, scale=-0.5).then_inc(r_rstd.sem, 1)
                        act.wait_ge(r_oturn.sem, r_oturn.at(b, t + 1))
                        nc.scalar.copy(orT[:, :, t * P:(t + 1) * P], turn[:, 0:2 * P]).then_inc(r_oT.sem, 1)

                    act.wait_ge(m_xc.sem, m_xc.at(b, 1))
                    nc.scalar.activation(xsq[:, :], xc[:, :], ACT.Square).then_inc(m_sq.sem, 1)
                    act.wait_ge(m_varf.sem, m_varf.at(b, 1))
                    nc.scalar.activation(lnv[:, :], head[:, 2, :], ACT.Ln, bias=eps_col[:, 0:1]).then_inc(m_lnv.sem, 1)
                    act.wait_ge(m_lnv.sem, m_lnv.at(b, 1))
                    nc.scalar.activation(rstd[:, :], lnv[:, :], ACT.Exp, scale=-0.5).then_inc(m_rstd.sem, 1)

                    act.wait_ge(e_sub.sem, e_sub.at(b, 1))
                    nc.scalar.activation(gex[:, :, :], gsub[:, :, :], ACT.Exp).then_inc(e_exp.sem, 1)
                    for t in range(TILES):
                        act.wait_ge(a_rot.sem, a_rot.at(b, t + 1))
                        nc.scalar.copy(av[:, t, :], proj[:, 0, 2 * P:3 * P]).then_inc(a_v.sem, 1)
                        act.wait_ge(a_turned.sem, a_turned.at(b, t + 1))
                        nc.scalar.copy(aqT[:, t, :], turn[:, 0:P])
                        nc.scalar.copy(akT[:, t, :], turn[:, P:2 * P]).then_inc(a_T.sem, 1)
                    for t in range(TILES):
                        act.wait_ge(a_max.sem, a_max.at(b, t + 1))
                        act.wait_ge(a_p.sem, a_p.at(b, t))
                        nc.scalar.activation(aex[:, :], asc[:, :], ACT.Exp, bias=aneg[:, 0:1], scale=AK, accum_out=aden[:, 0:1]).then_inc(a_exp.sem, 1)
                        act.wait_ge(a_pturn.sem, a_pturn.at(b, t + 1))
                        nc.scalar.copy(apT[:, :, :], turn[:, :]).then_inc(a_pT.sem, 1)

                    act.wait_ge(a_out.sem, a_out.at(b, TILES))
                    nc.scalar.copy(s1T[:, :], outs[:, :]).then_inc(s1_there.sem, 1)
                    act.wait_ge(e_gturn.sem, e_gturn.at(b, 1))
                    nc.scalar.copy(gaT[:, :], turn[0:NE, :]).then_inc(e_gT.sem, 1)
                    for c in range(4):
                        act.wait_ge(e_down.sem, e_down.at(b, c + 1))
                        nc.scalar.activation(hid[:, c, :], head[:, 1, :], ACT.Relu, bias=bd[:, c:c + 1]).then_inc(e_hid.sem, 1)
                    act.wait_ge(e_up.sem, e_up.at(b, 1))
                    nc.scalar.activation(moe[:, :], head[:, 3, :], ACT.Silu, scale=0.5).then_inc(e_silu.sem, 1)

            @block.vector
            def _(dve):
                nc.vector.memset(mean_w[:, :], 1.0 / P).then_inc(c_set.sem, 1)
                nc.vector.memset(eps_col[:, :], EPS).then_inc(c_set.sem, 1)
                dve.wait_ge(c_loads.sem, all_loads)
                count = [0]
                with dve.Fori(0, B) as b:
                    def then(ins):
                        count[0] += 1
                        ins.then_inc(steps.sem, 1)
                        dve.wait_ge(steps.sem, steps.at(b, count[0]))

                    steps.per = STEPS
                    dve.wait_ge(x_in.sem, x_in.at(b, 16))
                    for n, (of, to) in enumerate(((xtok, xntok), (xntok, nrtok))):
                        per_token = lambda a: a[:, :].unsqueeze(2).to_broadcast([P, TILES, P])
                        then(nc.vector.tensor_reduce(msum[:, :], of[:, :, :], AX.X, ALU.add))
                        then(nc.vector.tensor_scalar(mmean[:, :], msum[:, :], 1.0 / P, None, ALU.mult))
                        then(nc.vector.tensor_tensor(xctok[:, :, :], of[:, :, :], per_token(mmean), ALU.subtract))
                        then(nc.vector.tensor_tensor(sqtok[:, :, :], xctok[:, :, :], xctok[:, :, :], ALU.mult))
                        then(nc.vector.tensor_reduce(vsum[:, :], sqtok[:, :, :], AX.X, ALU.add))
                        nc.vector.tensor_scalar(var[:, :], vsum[:, :], 1.0 / P, EPS, ALU.mult, ALU.add).then_inc(x_stats.sem, 1)
                        dve.wait_ge(x_rstd.sem, x_rstd.at(b, n + 1))
                        nc.vector.tensor_tensor(to[:, :, :], xctok[:, :, :], per_token(rstd0), ALU.mult).then_inc(xn_there.sem, 1)
                        dve.wait_ge(xn_there.sem, xn_there.at(b, n + 1))

                    for t in range(TILES):
                        dve.wait_ge(r_proj.sem, r_proj.at(b, t + 1))
                        if t > 0:
                            dve.wait_ge(r_upd.sem, r_upd.at(b, t))
                        of = proj[:, 0, 0:2 * P]
                        nc.vector.tensor_tensor(rt1[:, :], of, rrot[:, 0, t, :], ALU.mult)
                        then(nc.vector.tensor_tensor(
                            rt2[:, :].rearrange("p (h s d) -> p h s d", s=2, d=RK // 2),
                            of.rearrange("p (h s d) -> p h s d", s=2, d=RK // 2)[:, :, ::-1, :],
                            rrot[:, 1, t, :].rearrange("p (h s d) -> p h s d", s=2, d=RK // 2), ALU.mult))
                        nc.vector.tensor_tensor(rqk[:, :], rt1[:, :], rt2[:, :], ALU.add).then_inc(r_rot.sem, 1)
                        dve.wait_ge(r_rot.sem, r_rot.at(b, t + 1))
                        nc.vector.tensor_tensor(qcr[:, :], rqk[:, 0:P], rdec[:, 0, :], ALU.mult)
                        nc.vector.tensor_tensor(kst[:, :], rqk[:, P:2 * P], rdec[:, 1, :], ALU.mult).then_inc(r_dec.sem, 1)
                        dve.wait_ge(r_sc.sem, r_sc.at(b, t + 1))
                        nc.vector.tensor_tensor(at[:, :, :], head[:, :, 0:P], rdiag[:, :, :], ALU.mult).then_inc(r_at.sem, 1)
                        if t < TILES - 1:
                            dve.wait_ge(r_upd.sem, r_upd.at(b, t + 1))
                            if t == 0:
                                nc.vector.tensor_tensor(st[:, :], head[:, 3, 0:2 * P], rblock[:, :], ALU.mult).then_inc(r_state.sem, 1)
                            else:
                                then(nc.vector.tensor_tensor(stn[:, :], head[:, 3, 0:2 * P], rblock[:, :], ALU.mult))
                                nc.vector.scalar_tensor_tensor(st[:, :], st[:, :], rcol[:, 2:3], stn[:, :], ALU.mult, ALU.add).then_inc(r_state.sem, 1)
                        dve.wait_ge(r_sq.sem, r_sq.at(b, t + 1))
                        nc.vector.tensor_reduce(oss[:, :], osq[:, :].rearrange("p (h d) -> p h d", d=RV), AX.X, ALU.add).then_inc(r_ms.sem, 1)
                        dve.wait_ge(r_rstd.sem, r_rstd.at(b, t + 1))
                        then(nc.vector.tensor_tensor(o1[:, :].rearrange("p (h d) -> p h d", d=RV), outs[:, 0:2 * P].rearrange("p (h d) -> p h d", d=RV),
                                                     orst[:, :].unsqueeze(2).to_broadcast([P, RH, RV]), ALU.mult))
                        then(nc.vector.tensor_tensor(o2[:, :], o1[:, :], gnw[:, :], ALU.mult))
                        dve.wait_ge(r_sg.sem, r_sg.at(b, t + 1))
                        nc.vector.tensor_tensor(o3[:, :], o2[:, :], sg[:, :], ALU.mult).then_inc(r_o.sem, 1)

                    dve.wait_ge(r_wo.sem, r_wo.at(b, 1))
                    then(nc.vector.tensor_tensor(sT[:, :], head[:, 0, :], xnT[:, :], ALU.add))
                    dve.wait_ge(s_gate.sem, s_gate.at(b, 1))
                    then(nc.vector.tensor_tensor(gT[:, :], sT[:, :], sgT[:, :], ALU.mult))
                    nc.vector.tensor_tensor(x1T[:, :], gT[:, :], x0T[:, :], ALU.add).then_inc(x1_there.sem, 1)
                    dve.wait_ge(x1_there.sem, x1_there.at(b, 1))
                    dve.wait_ge(m_mean.sem, m_mean.at(b, 1))
                    nc.vector.tensor_tensor(xc[:, :], x1T[:, :], head[:, 1, :], ALU.subtract).then_inc(m_xc.sem, 1)
                    dve.wait_ge(m_rstd.sem, m_rstd.at(b, 1))
                    nc.vector.tensor_tensor(xm[:, :], xc[:, :], rstd[:, :], ALU.mult).then_inc(xm_there.sem, 1)

                    dve.wait_ge(e_lg.sem, e_lg.at(b, 1))
                    then(nc.vector.tensor_copy(lg[:, :, :], head[:, 3, 0:NE * TILES].rearrange("p (t e) -> p t e", e=NE)))
                    mine = lg[:, :, :].unsqueeze(3).to_broadcast([P, TILES, NE, NE])
                    theirs = lg[:, :, :].unsqueeze(2).to_broadcast([P, TILES, NE, NE])
                    nc.vector.tensor_tensor(beats[:, :, :, :], theirs, mine, ALU.is_gt)
                    then(nc.vector.tensor_tensor(ties[:, :, :, :], theirs, mine, ALU.is_equal))
                    then(nc.vector.tensor_tensor(tied[:, :, :, :], ties[:, :, :, :], ebefore[:, :, :].unsqueeze(1).to_broadcast([P, TILES, NE, NE]), ALU.mult))
                    then(nc.vector.tensor_tensor(wins[:, :, :, :], beats[:, :, :, :], tied[:, :, :, :], ALU.add))
                    then(nc.vector.tensor_reduce(rank[:, :, :], wins[:, :, :, :], AX.X, ALU.add))
                    nc.vector.tensor_scalar(sel[:, :, :], rank[:, :, :], 2.0, None, ALU.is_lt)
                    then(nc.vector.tensor_reduce(gmx[:, :], lg[:, :, :], AX.X, ALU.max))
                    nc.vector.tensor_tensor(gsub[:, :, :], lg[:, :, :], gmx[:, :].unsqueeze(2).to_broadcast([P, TILES, NE]), ALU.subtract).then_inc(e_sub.sem, 1)
                    dve.wait_ge(e_exp.sem, e_exp.at(b, 1))
                    then(nc.vector.tensor_tensor(gsel[:, :, :], gex[:, :, :], sel[:, :, :], ALU.mult))
                    then(nc.vector.tensor_reduce(gden[:, :], gsel[:, :, :], AX.X, ALU.add))
                    then(nc.vector.reciprocal(grd[:, :], gden[:, :]))
                    nc.vector.tensor_tensor(gate[:, :, :], gsel[:, :, :], grd[:, :].unsqueeze(2).to_broadcast([P, TILES, NE]), ALU.mult).then_inc(e_gate.sem, 1)

                    for t in range(TILES):
                        dve.wait_ge(a_proj.sem, a_proj.at(b, t + 1))
                        if t > 0:
                            dve.wait_ge(a_turned.sem, a_turned.at(b, t))
                        of = proj[:, 0, 0:2 * P]
                        nc.vector.tensor_tensor(aq1[:, :], of, arot[:, 0, t, :], ALU.mult)
                        then(nc.vector.tensor_tensor(
                            aq2[:, :].rearrange("p (h s d) -> p h s d", s=2, d=64),
                            of.rearrange("p (h s d) -> p h s d", s=2, d=64)[:, :, ::-1, :],
                            arot[:, 1, t, :].rearrange("p (h s d) -> p h s d", s=2, d=64), ALU.mult))
                        nc.vector.tensor_tensor(aqk[:, :], aq1[:, :], aq2[:, :], ALU.add).then_inc(a_rot.sem, 1)
                    for t in range(TILES):
                        dve.wait_ge(a_sc.sem, a_sc.at(b, t + 1))
                        if t > 0:
                            dve.wait_ge(a_exp.sem, a_exp.at(b, t))
                        then(nc.vector.tensor_tensor(asc[:, :], head[:, 0, :], amask[:, t, :], ALU.add))
                        then(nc.vector.tensor_reduce(amx[:, :], asc[:, :], AX.X, ALU.max))
                        nc.vector.tensor_scalar(aneg[:, :], amx[:, :], -AK, None, ALU.mult).then_inc(a_max.sem, 1)
                        dve.wait_ge(a_exp.sem, a_exp.at(b, t + 1))
                        then(nc.vector.reciprocal(arden[:, :], aden[:, :]))
                        if t > 0:
                            dve.wait_ge(a_pturn.sem, a_pturn.at(b, t))
                        nc.vector.tensor_scalar(apr[:, :], aex[:, :], arden[:, 0:1], None, ALU.mult).then_inc(a_p.sem, 1)

                    for c in range(4):
                        dve.wait_ge(e_hid.sem, e_hid.at(b, c + 1))
                        dve.wait_ge(e_spread.sem, e_spread.at(b, c + 1))
                        nc.vector.tensor_tensor(hg[:, c, :], head[:, 2, :], hid[:, c, :], ALU.mult).then_inc(e_hg.sem, 1)
                    dve.wait_ge(e_silu.sem, e_silu.at(b, 1))
                    dve.wait_ge(s1_there.sem, s1_there.at(b, 1))
                    then(nc.vector.tensor_tensor(gT[:, :], s1T[:, :], moe[:, :], ALU.mult))
                    nc.vector.tensor_tensor(x2T[:, :], gT[:, :], x1T[:, :], ALU.add).then_inc(x2_there.sem, 1)
                    dve.wait_ge(x2_turn.sem, x2_turn.at(b, 1))
                    dve.wait_ge(stored.sem, stored.at(b, 0))
                    nc.vector.tensor_copy(xo[:, :, :], turn[:, :].rearrange("p (t d) -> p t d", d=P)).then_inc(xo_there.sem, 1)
                assert count[0] == STEPS, count[0]


def rotary_tables():
    f = np.float32
    half = np.arange(0, DH, 2, dtype=f)
    freqs = np.arange(T, dtype=f)[:, None] * (f(1.0) / f(10000.0) ** (half / f(DH)))[None, :]
    freqs = np.concatenate([freqs, freqs], -1)
    base = (half + f(0.4 * DH)) / f(1.4 * DH)
    power = (np.arange(T, dtype=f) - T // 2) / f(WIN // 2)
    scale = base[None, :] ** power[:, None]
    scale = np.concatenate([scale, scale], -1)
    sign = np.where(np.arange(DH) < DH // 2, -1.0, 1.0).astype(f)
    cos, sin = np.cos(freqs), np.sin(freqs) * sign
    out = np.stack([cos * scale, sin * scale, cos / scale, sin / scale])
    return np.ascontiguousarray(out.reshape(4, TILES, P, DH).transpose(2, 0, 1, 3), dtype=f)


def window_mask():
    query = (np.arange(P) % WIN)[:, None]
    key = np.arange(2 * WIN)[None, :]
    ok = (key >= query) & (key <= query + WIN)
    first = ok & ((np.arange(P)[:, None] >= WIN) | (key >= WIN))
    return np.where(np.stack([first, ok], 1), 0.0, MASKED).astype(np.float32)


def pack_layers(a):
    f = np.float32
    g = lambda n: np.asarray(a["L0_ffn_" + n])
    qkv = g("Wqkv")
    v = qkv[:, :, 2 * INNER:].reshape(DEPTH, P, PAIRS, 2, DH).transpose(0, 1, 3, 2, 4).reshape(DEPTH, P, INNER)
    w_qkv = np.concatenate([qkv[:, :, :2 * INNER], v], 2)
    w_o = g("Wo").reshape(DEPTH, PAIRS, P, P).transpose(0, 2, 1, 3).reshape(DEPTH, P, PAIRS * P)
    w_2 = np.zeros((DEPTH, 3 * P, P), f)
    w_2[:, :FF] = g("W2")
    w_2 = w_2.reshape(DEPTH, 3, P, P).transpose(0, 2, 1, 3).reshape(DEPTH, P, 3 * P)
    cols = np.zeros((DEPTH, 9, P), f)
    b1 = g("b1")
    for k in range(2):
        for c, m in enumerate(FCH):
            cols[:, 3 * k + c, :m] = b1[:, FF * k + P * c:FF * k + P * c + m]
    cols[:, 6], cols[:, 7], cols[:, 8] = g("ln_g"), g("ln_b"), g("b2")
    cols = cols.transpose(0, 2, 1)
    qs, ks = g("q_scale"), g("k_scale")
    swap = lambda s: np.concatenate([s[:, DH // 2:], s[:, :DH // 2]], 1)
    scales = np.stack([qs, swap(qs), ks, swap(ks)], 1)
    return {k: np.ascontiguousarray(v) for k, v in dict(
        w_qkv=w_qkv, w_o=w_o, w_1=g("W1"), w_2=w_2, cols=cols, qk_scale=scales).items()}


def mixer_tables():
    f = np.float32
    t = np.arange(T, dtype=f)
    tiles = lambda a: a.reshape(TILES, P, -1).transpose(1, 0, 2)

    def rope(theta, groups, scale):
        ang = t[:, None] * theta[None, :]
        c, s = np.cos(ang), np.sin(ang)
        both = [np.concatenate([c, c], 1), np.concatenate([-s, s], 1)]
        rows = [np.concatenate([np.tile(a, (1, groups)) * f(scale), np.tile(a, (1, groups))], 1) for a in both]
        return np.stack([tiles(a) for a in rows], 1).astype(f)

    gamma = f(1.0) - np.exp2(f(-5.0) - np.arange(RH, dtype=f))
    i = np.arange(P, dtype=f)
    wide = lambda a: np.repeat(a.T, RK, axis=1)
    gap = i[None, :] - i[:, None]
    diag = np.where(gap >= 0, gamma[:, None, None] ** np.maximum(gap, 0), 0.0).transpose(1, 0, 2)
    rows, cols = np.arange(P), np.arange(2 * P)
    return {k: np.ascontiguousarray(v, dtype=f) for k, v in dict(
        ret_rot=rope(f(1.0) / f(10000.0) ** (np.arange(0, RK, 2, dtype=f) / f(RK)), RH, RK ** -0.5),
        ret_decay=np.stack([wide(gamma[:, None] ** (i + 1)), wide(gamma[:, None] ** (P - 1 - i))], 1),
        ret_diag=diag,
        ret_block=(rows[:, None] // RK == cols[None, :] // RV),
        state_decay=np.repeat(gamma ** P, RK),
        att_rot=rope(f(10000.0) ** (f(-2.0) * np.arange(P // 2, dtype=f) / f(P)), 1, 1.0),
        att_mask=tiles(np.where(np.arange(T)[None, :] <= np.arange(T)[:, None] + 1, 0.0, MASKED)),
        expert_rows=np.arange(NE)[:, None, None] == (BN * 2 * np.arange(4)[:, None] + rows)[None] // BN,
        before=(np.arange(NE)[None, :] < np.arange(NE)[:, None]).reshape(1, NE * NE)).items()}


def pack_mixers(a):
    g = lambda n: np.asarray(a[n])
    r = lambda n: g("L0_attn_" + n)
    pairs = np.concatenate([np.arange(0, P, 2), np.arange(1, P, 2)])
    att = np.concatenate([g("L1_attn_Wq")[pairs].T, g("L1_attn_Wk")[pairs].T, g("L1_attn_Wv").T], 1)
    return {k: np.ascontiguousarray(v) for k, v in dict(
        w_ret=np.concatenate([r("Wq"), r("Wk"), r("Wv"), r("Wg")], 1),
        w_ro=r("Wo").reshape(2, P, P).transpose(1, 0, 2),
        g_norm=np.tile(r("g_norm_w"), RH)[None, :],
        w_att=att,
        w_gate=g("L1_ffn_w_gate"),
        w_down=g("L1_ffn_Wd").transpose(1, 0, 2).reshape(P, NE * BN),
        w_up=g("L1_ffn_Wu").reshape(4, P, P).transpose(1, 0, 2),
        b_down=g("L1_ffn_bd").reshape(4, P).T,
        b_up=g("L1_ffn_bu")).items()}


def build(nc, x, out, net, mix):
    with nc.sbuf_tensor("state", [P, B * SHIFTED], F32) as state:
        build_network(nc, x=x, state=state, **net)
        build_mixers(nc, state=state, x=x, out=out, **mix)


def kernel(**inputs):
    import concourse.bacc as bacc
    from concourse.bass_utils import run_bass_kernel_spmd

    net = dict(pack_layers(inputs), rotary=rotary_tables(), win_mask=window_mask())
    mix = dict(pack_mixers(inputs), **mixer_tables())
    mix["ret_cols"] = np.ascontiguousarray(np.stack(
        [np.asarray(inputs["L0_attn_ln_w"]), np.asarray(inputs["L0_attn_ln_b"]), mix.pop("state_decay")], 1))
    nc = bacc.Bacc("TRN2", target_bir_lowering=False, num_devices=1)
    arrays = {}

    def dram(name, a):
        arrays[f"in_{name}"] = a
        return nc.dram_tensor(f"in_{name}", a.shape, mybir.dt.from_np(a.dtype), kind="ExternalInput").ap()

    x = dram("x", np.ascontiguousarray(inputs["L0_attn_x"]))
    out = nc.dram_tensor("out_x", (B, T, P), F32, kind="ExternalOutput").ap()
    build(nc, x, out, {k: dram(k, v) for k, v in net.items()}, {k: dram(k, v) for k, v in mix.items()})
    r = run_bass_kernel_spmd(nc, [arrays], core_ids=[0])
    return r.results[0]["out_x"]
```

```python
from contextlib import ExitStack

import numpy as np

import concourse.bass as bass
from concourse import mybir

F32 = mybir.dt.float32
BF16 = mybir.dt.bfloat16
ALU = mybir.AluOpType
ACT = mybir.ActivationFunctionType
AX = mybir.AxisListType

P = 128
B, T = 4, 512
TILES = T // P
EPS = 1e-5
LN_EXP_SET = "natural_log_exp_and_others"
MASKED = -1e30

DEPTH = 6
HEADS, DH = 16, 64
PAIRS = HEADS // 2
INNER = HEADS * DH
WIN = 32
WINDOWS = T // WIN
TW = P // WIN
FF = int(P * 4 * 2 / 3)
FCH = [128, 128, FF - 256]
SHIFTED = T + 4
NORM_FLOOR = 1e-24
LN_SCALE = 2.0 ** 20


class Signal:

    def __init__(self, ctx, nc, name, per=1):
        self.sem, self.per = ctx.enter_context(nc.semaphore(name)), per

    def at(self, rnd, n):
        return rnd * self.per + n


def build_network(nc, x, w_qkv, w_o, w_1, w_2, cols, qk_scale, rotary, win_mask, state):
    ctx = ExitStack()
    with ctx:
        def sb(name, shape, dt=F32):
            return ctx.enter_context(nc.sbuf_tensor(name, shape, dt))

        def sig(name, per=1):
            return Signal(ctx, nc, name, per)

        qk_ps = ctx.enter_context(nc.psum_tensor("qk_ps", [P, 4, 512], F32))
        sc_ps = ctx.enter_context(nc.psum_tensor("sc_ps", [P, 2, 512], F32))
        ring = ctx.enter_context(nc.psum_tensor("ring", [P, 2, 512], F32))

        ident = sb("ident", [P, P])
        ident_bf = sb("ident_bf", [P, P], BF16)
        mean_w = sb("mean_w", [P, P])
        centre_w = sb("centre_w", [P, P])
        mask_f = sb("mask_f", [P, 2, 2 * WIN])
        mask_bf = sb("mask_bf", [P, 2, PAIRS, 2 * WIN], BF16)
        rot_base = sb("rot_base", [P, 4, TILES, DH])
        rot = sb("rot", [P, 4, TILES, DH])
        qks = sb("qks", [P, 4, DH])
        wqkv = sb("wqkv", [P, 3 * INNER])
        wo = sb("wo", [P, PAIRS, P])
        w1 = sb("w1", [P, 2 * FF])
        w2 = sb("w2", [P, 3, P])
        col = sb("col", [P, 9])
        xs = sb("xs", [P, T])
        xs2 = sb("xs2", [P, T])
        t1 = sb("t1", [P, 2 * INNER])
        t2 = sb("t2", [P, 2 * INNER])
        sq = sb("sq", [P, 2 * INNER])
        qkn = sb("qkn", [P, 2 * INNER])
        ss = sb("ss", [P, 2 * HEADS])
        rs = sb("rs", [P, 2 * HEADS])
        lnss = sb("lnss", [P, 2 * HEADS])
        nw1 = sb("nw1", [P, 2 * HEADS])
        nw2 = sb("nw2", [P, 2 * HEADS])
        rn = sb("rn", [P, 2 * HEADS])
        qT = sb("qT", [P, PAIRS, P])
        kT = sb("kT", [P, PAIRS, WIN + T])
        v_tok = sb("v_tok", [P, 2, 2, PAIRS * DH])
        v_win = sb("v_win", [P, WINDOWS, PAIRS * DH])
        smax = sb("smax", [P, HEADS])
        den = sb("den", [P, HEADS])
        rden = sb("rden", [P, HEADS])
        pr = sb("pr", [P, INNER])
        pe_ = sb("pexp", [P, INNER])
        prT = sb("prT", [P, PAIRS, P])
        o_tok = sb("o_tok", [P, INNER])
        oT = sb("oT", [P, PAIRS, T])
        xc = sb("xc", [P, T])
        xsq = sb("xsq", [P, T])
        lnv = sb("lnv", [P, T])
        rstd = sb("rstd", [P, T])
        xh = sb("xh", [P, T])
        xn = sb("xn", [P, T])
        gel = sb("gel", [P, 3, T])
        u = sb("u", [P, 3, T])
        msum = sb("msum", [P, TILES])
        mmean = sb("mmean", [P, TILES])
        vsum = sb("vsum", [P, TILES])
        veps = sb("veps", [P, TILES])
        lnsum = sb("lnsum", [P, 2 * HEADS])
        eps_col = sb("eps_col", [P, 1])
        lv = sb("lv", [P, TILES])
        rstd0 = sb("rstd0", [P, TILES])
        xtok = xc[:, :].rearrange("p (t d) -> p t d", t=TILES)
        xctok = xn[:, :].rearrange("p (t d) -> p t d", t=TILES)
        sqtok = lnv[:, :].rearrange("p (t d) -> p t d", t=TILES)
        xntok = xh[:, :].rearrange("p (t d) -> p t d", t=TILES)

        s_const = sig("s_const")
        s_wqk = sig("s_wqk", 16)
        s_wv = sig("s_wv", 16)
        s_qks = sig("s_qks", 16)
        s_wrest = sig("s_wrest", 64)
        v_moved = [sig(f"v_moved{t}", 16 * (16 - 2 * (t == TILES - 1))) for t in range(TILES)]
        c_ident = sig("c_ident")
        c_dve = sig("c_dve")
        n_x = sig("n_x", 16)
        n_steps = sig("n_steps", 5)
        n_var = sig("n_var")
        n_lnv = sig("n_lnv")
        n_rstd = sig("n_rstd")
        n_xn = sig("n_xn")
        n_tr = sig("n_tr")
        n_state = sig("n_state")
        rot_ready = sig("rot_ready")
        xs_ready = sig("xs_ready", 2)
        v_full = sig("v_full", 2 * TILES)
        v_copied = sig("v_copied", 2 * TILES)
        qk_full = sig("qk_full", 4 * TILES)
        q_sq = sig("q_sq", TILES)
        k_sq = sig("k_sq", TILES)
        qk_rot = sig("qk_rot", 4 * TILES)
        ss_sum = sig("ss_sum", 2 * TILES)
        ss_ready = sig("ss_ready", TILES)
        ss_ln = sig("ss_ln", TILES)
        rs_ready = sig("rs_ready", TILES)
        newton = sig("newton", 2 * TILES)
        rn_ready = sig("rn_ready", TILES)
        qk_added = sig("qk_added", 2 * TILES)
        qk_scaled = sig("qk_scaled", 2 * TILES)
        qkT_full = sig("qkT_full", 4 * TILES)
        qkT_copied = sig("qkT_copied", 4 * TILES)
        sc_full = sig("sc_full", TILES)
        max_ready = sig("max_ready", TILES)
        sc_sub = sig("sc_sub", 2 * TILES)
        exp_ready = sig("exp_ready", 2 * TILES)
        den_ready = sig("den_ready", TILES)
        rden_ready = sig("rden_ready", TILES)
        pT_full = sig("pT_full", 2 * TILES)
        pT_copied = sig("pT_copied", 2 * TILES)
        av_full = sig("av_full", TILES)
        o_ready = sig("o_ready", 2 * TILES)
        oT_full = sig("oT_full", 2 * TILES)
        oT_copied = sig("oT_copied", 2 * TILES)
        wo_full = sig("wo_full")
        x_attn = sig("x_attn")
        xs2_ready = sig("xs2_ready", 2)
        xc_full = sig("xc_full")
        xc_copied = sig("xc_copied")
        xsq_ready = sig("xsq_ready")
        var_full = sig("var_full")
        lnv_ready = sig("lnv_ready")
        rstd_ready = sig("rstd_ready")
        xh_ready = sig("xh_ready")
        xn_ready = sig("xn_ready")
        gate_full = sig("gate_full", 3)
        lin_full = sig("lin_full", 3)
        gelu_ready = sig("gelu_ready", 3)
        u_ready = sig("u_ready", 3)
        w2_full = sig("w2_full")
        x_ffn = sig("x_ffn")

        ROUNDS = DEPTH * B

        class Round:

            def __init__(self, it, now, before):
                self.it, self.now, self.before = it, now, before

            def has(self, s, lag):
                return self.now if s >= lag else self.before

            def tile(self, s, lag):
                return (self.it, s - lag) if s >= lag else (self.it - 1, s - lag + TILES)

        order = []
        for s in range(TILES):
            order += [("wo", s, TILES, 0)] * (s == 2)
            order += [("t", s, 1, f) for f in range(2)]
            order += [("xc", s, TILES, 0)] * (s == 2)
            order += [("p", s, 2, f) for f in range(2)]
            order += [("t", s, 1, f) for f in range(2, 4)]
            order += [("var", s, TILES, 0)] * (s == 2)
            order += [(k, s, TILES, c) for c in range(3) for k in ("gate", "lin")] * (s == 3)
            order += [("v", s, 0, f) for f in range(2)]
            order += [("w2", s, TILES, 0)] * (s == 3)
            order += [("o", s, 2, f) for f in range(2)]

        def fills(r):
            of = [f for f in order if r.has(f[1], f[2])]
            assert len(of) % 2 == 0
            return of

        def bank_of(r, fill):
            return ring[:, fills(r).index(fill) % 2, :]

        readers = dict(v=(v_copied, 2), t=(qkT_copied, 4), p=(pT_copied, 2), o=(oT_copied, 2), wo=(x_attn, 1), xc=(xc_copied, 1),
                       var=(lnv_ready, 1), gate=(gelu_ready, 3), lin=(u_ready, 3), w2=(x_ffn, 1))

        def bank_free(r, fill):
            of = fills(r)
            n = of.index(fill)
            it = r.it
            if n < 2:
                if not r.before:
                    return None
                it, of = r.it - 1, order
            what, s, lag, f = of[n - 2]
            signal, many = readers[what]
            if lag == TILES:
                return signal.sem, signal.at(it - 1, f + 1)
            rnd, t = (it, s - lag) if s >= lag else (it - 1, s - lag + TILES)
            return signal.sem, signal.at(rnd, many * t + f + 1)

        def state_cols(b, first, n):
            return bass.ds(b * SHIFTED + first, n)

        with nc.Block() as block:

            @block.sync
            def _(sp):
                for n, (to, of) in enumerate(((mask_f[:, :, :], win_mask), (rot_base[:, :, :, :], rotary))):
                    sp.dma_start(to, of).then_inc(s_const.sem, 16)
                with sp.Fori(0, B) as b:
                    sp.wait_ge(n_xn.sem, n_xn.at(b, 0))
                    sp.dma_start(xtok, x[bass.ds(b, 1), :, :].rearrange("o (t p) d -> p (o t) d", p=P)).then_inc(n_x.sem, 16)

                def load_qk_weights(l):
                    sp.dma_start(wqkv[:, 0:2 * INNER], w_qkv[bass.ds(l, 1), :, 0:2 * INNER].rearrange("o p n -> p (o n)")).then_inc(s_wqk.sem, 16)

                def load_v_weights(l):
                    sp.dma_start(wqkv[:, 2 * INNER:], w_qkv[bass.ds(l, 1), :, 2 * INNER:].rearrange("o p n -> p (o n)")).then_inc(s_wv.sem, 16)

                def move_windows(it, t):
                    sp.wait_ge(v_copied.sem, v_copied.at(it, 2 * (t + 1)))
                    for q in range(TW):
                        w = TW * t + q
                        for par in range(2):
                            of = v_tok[WIN * q:WIN * (q + 1), t % 2, par, :]
                            sp.dma_start(v_win[64 * par + WIN:64 * par + 2 * WIN, w, :], of).then_inc(v_moved[t].sem, 16)
                            if w + 1 < WINDOWS:
                                sp.dma_start(v_win[64 * par:64 * par + WIN, w + 1, :], of).then_inc(v_moved[t].sem, 16)

                def layer(l, more):
                    sp.wait_ge(rot_ready.sem, rot_ready.at(l, 0))
                    sp.dma_start(qks[:, :, :], qk_scale[bass.ds(l, 1), :, :].to_broadcast([P, 4, DH])).then_inc(s_qks.sem, 16)
                    for t in range(TILES):
                        move_windows(l * B, t)
                    sp.wait_ge(x_ffn.sem, l * B)
                    sp.dma_start(wo[:, :, :], w_o[bass.ds(l, 1), :, :].rearrange("o p (c n) -> p (o c) n", n=P)).then_inc(s_wrest.sem, 16)
                    sp.dma_start(w1[:, :], w_1[bass.ds(l, 1), :, :].rearrange("o p n -> p (o n)")).then_inc(s_wrest.sem, 16)
                    sp.dma_start(w2[:, :, :], w_2[bass.ds(l, 1), :, :].rearrange("o p (c n) -> p (o c) n", n=P)).then_inc(s_wrest.sem, 16)
                    sp.dma_start(col[:, :], cols[bass.ds(l, 1), :, :].rearrange("o p n -> p (o n)")).then_inc(s_wrest.sem, 16)
                    with sp.Fori(1, B - 1) as b:
                        for t in range(TILES):
                            move_windows(l * B + b, t)
                    last = l * B + B - 1
                    for t in range(TILES):
                        if more and t == TILES - 1:
                            sp.wait_ge(qk_full.sem, qk_full.at(last, qk_full.per))
                            load_qk_weights(l + 1)
                        move_windows(last, t)
                    if more:
                        load_v_weights(l + 1)

                load_qk_weights(0)
                load_v_weights(0)
                if DEPTH > 1:
                    with sp.Fori(0, DEPTH - 1) as l:
                        layer(l, True)
                layer(DEPTH - 1, False)

            @block.gpsimd
            def _(pool):
                nc.gpsimd.memset(ident[:, :], 0.0).then_inc(c_ident.sem, 1)
                pool.wait_ge(c_ident.sem, 1)
                nc.gpsimd.affine_select(out=ident[:, :], in_=ident[:, :], compare_op=ALU.not_equal, fill=1.0,
                                        base=0, pattern=[[-1, P]], channel_multiplier=1).then_inc(c_ident.sem, 1)
                pool.wait_ge(s_const.sem, 32)
                with pool.Fori(0, DEPTH) as l:
                    pool.wait_ge(s_qks.sem, s_qks.at(l, 16))
                    pool.wait_ge(qk_rot.sem, l * (B * qk_rot.per))
                    for k in range(4):
                        ins = nc.gpsimd.tensor_tensor(
                            rot[:, k, :, :], rot_base[:, k, :, :],
                            qks[:, k:k + 1, :].to_broadcast([P, TILES, DH]), ALU.mult)
                    ins.then_inc(rot_ready.sem, 1)
                    with pool.Fori(0, B) as b:
                        it = l * B + b
                        for t in range(TILES):
                            for half in range(2):
                                pool.wait_ge(qk_rot.sem, qk_rot.at(it, 4 * t + 2 * (half + 1)))
                                to = slice(INNER * half, INNER * (half + 1))
                                nc.gpsimd.tensor_tensor(t1[:, to], t1[:, to], t2[:, to], ALU.add).then_inc(qk_added.sem, 1)
                            pool.wait_ge(qk_added.sem, qk_added.at(it, 2 * (t + 1)))
                            pool.wait_ge(rn_ready.sem, rn_ready.at(it, t + 1))
                            pool.wait_ge(qkT_full.sem, qkT_full.at(it, 4 * t))
                            for half in range(2):
                                to = slice(INNER * half, INNER * (half + 1))
                                nc.gpsimd.tensor_tensor(
                                    qkn[:, to].rearrange("p (h d) -> p h d", d=DH), t1[:, to].rearrange("p (h d) -> p h d", d=DH),
                                    rn[:, HEADS * half:HEADS * (half + 1)].unsqueeze(2).to_broadcast([P, HEADS, DH]), ALU.mult).then_inc(qk_scaled.sem, 1)

            @block.tensor
            def _(pe):
                pe.wait_ge(c_ident.sem, 2)
                with pe.Fori(0, B) as b:
                    pe.wait_ge(n_state.sem, n_state.at(b, 0))
                    pe.wait_ge(n_xn.sem, n_xn.at(b, 1))
                    for t in range(TILES):
                        ins = nc.tensor.transpose(ring[:, 0, t * P:(t + 1) * P], xntok[:, t, :], ident[:, :])
                    ins.then_inc(n_tr.sem, 1)
                pe.wait_ge(n_state.sem, B)
                pe.wait_ge(c_dve.sem, 7 + B)

                def ring_bank(r, what, s, lag, f):
                    fill = (what, s, lag, f)
                    before = bank_free(r, fill)
                    if before:
                        pe.wait_ge(before[0], before[1])
                    return bank_of(r, fill)

                def project_v(r, s):
                    if s == 0:
                        pe.wait_ge(s_wv.sem, s_wv.at(r.it >> 2, 16))
                    for par in range(2):
                        to = ring_bank(r, "v", s, 0, par)
                        nc.tensor.matmul(to, xs[:, s * P:(s + 1) * P], wqkv[:, 2 * INNER + 512 * par:2 * INNER + 512 * (par + 1)],
                                         start=True, stop=True).then_inc(v_full.sem, 1)

                def project_qk(r, s, c):
                    if c == 0:
                        if s == 0:
                            pe.wait_ge(s_wqk.sem, s_wqk.at(r.it >> 2, 16))
                            pe.wait_ge(xs_ready.sem, xs_ready.at(r.it, 2))
                        pe.wait_ge(q_sq.sem, q_sq.at(r.it, s))
                    if c == 2:
                        pe.wait_ge(qk_rot.sem, qk_rot.at(r.it, 4 * s))
                    nc.tensor.matmul(qk_ps[:, c, :], xs[:, s * P:(s + 1) * P], wqkv[:, 512 * c:512 * (c + 1)],
                                     start=True, stop=True).then_inc(qk_full.sem, 1)

                def transpose_qk(r, s, f):
                    it, t = r.tile(s, 1)
                    if f % 2 == 0:
                        pe.wait_ge(qk_scaled.sem, qk_scaled.at(it, 2 * t + f // 2 + 1))
                    to = ring_bank(r, "t", s, 1, f)
                    for n in range(4):
                        c = 4 * f + n
                        ins = nc.tensor.transpose(to[:, n * P:(n + 1) * P], qkn[:, c * P:(c + 1) * P], ident[:, :])
                    ins.then_inc(qkT_full.sem, 1)

                def scores(r, s):
                    it, t = r.tile(s, 1)
                    pe.wait_ge(qkT_copied.sem, qkT_copied.at(it, 4 * (t + 1)))
                    pe.wait_ge(o_ready.sem, o_ready.at(it, 2 * t))
                    for par in range(2):
                        nc.tensor.matmul(sc_ps[:, par, :], ident_bf[:, :], mask_bf[:, int(t > 0), :, :],
                                         start=True, stop=False, skip_group_check=True)
                    for pair in range(PAIRS):
                        for q in range(TW):
                            for par in range(2):
                                ins = nc.tensor.matmul(
                                    sc_ps[WIN * q:WIN * (q + 1), par, 64 * pair:64 * (pair + 1)],
                                    qT[64 * par:64 * (par + 1), pair, WIN * q:WIN * (q + 1)],
                                    kT[64 * par:64 * (par + 1), pair, P * t + WIN * q:P * t + WIN * (q + 2)],
                                    start=False, stop=True, skip_group_check=True)
                    ins.then_inc(sc_full.sem, 1)

                def transpose_p(r, s, f):
                    it, t = r.tile(s, 2)
                    pe.wait_ge(exp_ready.sem, exp_ready.at(it, 2 * t + f + 1))
                    to = ring_bank(r, "p", s, 2, f)
                    for n in range(4):
                        c = 4 * f + n
                        ins = nc.tensor.transpose(to[:, n * P:(n + 1) * P], pe_[:, c * P:(c + 1) * P], ident[:, :])
                    ins.then_inc(pT_full.sem, 1)

                def attend(r, s):
                    it, t = r.tile(s, 2)
                    pe.wait_ge(pT_copied.sem, pT_copied.at(it, 2 * (t + 1)))
                    pe.wait_ge(v_moved[t].sem, v_moved[t].at(it, v_moved[t].per))
                    pe.wait_ge(sc_sub.sem, sc_sub.at(it, 2 * (t + 1)))
                    nc.tensor.matmul(sc_ps[:, 0, 0:DH], prT[0:64, 0, :], v_win[0:64, TW * t, 0:DH], start=True, stop=True)
                    for pair in range(PAIRS):
                        for q in range(TW):
                            for par in range(2):
                                ins = nc.tensor.matmul(
                                    sc_ps[WIN * q:WIN * (q + 1), par, DH * pair:DH * (pair + 1)],
                                    prT[64 * par:64 * (par + 1), pair, WIN * q:WIN * (q + 1)],
                                    v_win[64 * par:64 * (par + 1), TW * t + q, DH * pair:DH * (pair + 1)],
                                    start=True, stop=True)
                    ins.then_inc(av_full.sem, 1)

                def transpose_o(r, s):
                    it, t = r.tile(s, 2)
                    for f in range(2):
                        pe.wait_ge(o_ready.sem, o_ready.at(it, 2 * t + f + 1))
                        to = ring_bank(r, "o", s, 2, f)
                        for n in range(4):
                            c = 4 * f + n
                            ins = nc.tensor.transpose(to[:, n * P:(n + 1) * P], o_tok[:, c * P:(c + 1) * P], ident[:, :])
                        ins.then_inc(oT_full.sem, 1)

                def output_projection(r):
                    pe.wait_ge(s_wrest.sem, s_wrest.at((r.it - 1) >> 2, 64))
                    pe.wait_ge(oT_copied.sem, oT_copied.at(r.it - 1, 2 * TILES))
                    to = bank_of(r, ("wo", 2, TILES, 0))
                    for c in range(PAIRS):
                        ins = nc.tensor.matmul(to, wo[:, c, :], oT[:, c, :], start=(c == 0), stop=(c == PAIRS - 1))
                    ins.then_inc(wo_full.sem, 1)

                def ffn_centre(r):
                    pe.wait_ge(xs2_ready.sem, xs2_ready.at(r.it - 1, 2))
                    nc.tensor.matmul(ring_bank(r, "xc", 2, TILES, 0), centre_w[:, :], xs2[:, :], start=True, stop=True).then_inc(xc_full.sem, 1)

                def ffn_variance(r):
                    pe.wait_ge(xsq_ready.sem, xsq_ready.at(r.it - 1, 1))
                    nc.tensor.matmul(ring_bank(r, "var", 2, TILES, 0), mean_w[:, :], xsq[:, :], start=True, stop=True).then_inc(var_full.sem, 1)

                def ffn_up(r):
                    pe.wait_ge(xn_ready.sem, xn_ready.at(r.it - 1, 1))
                    for c, m in enumerate(FCH):
                        nc.tensor.matmul(ring_bank(r, "gate", 3, TILES, c)[0:m, :], w1[:, FF + P * c:FF + P * c + m], xn[:, :],
                                         start=True, stop=True).then_inc(gate_full.sem, 1)
                        nc.tensor.matmul(ring_bank(r, "lin", 3, TILES, c)[0:m, :], w1[:, P * c:P * c + m], xn[:, :],
                                         start=True, stop=True).then_inc(lin_full.sem, 1)

                def ffn_down(r):
                    pe.wait_ge(u_ready.sem, u_ready.at(r.it - 1, 3))
                    to = ring_bank(r, "w2", 3, TILES, 0)
                    for c, m in enumerate(FCH):
                        ins = nc.tensor.matmul(to, w2[0:m, c, :], u[0:m, c, :], start=(c == 0), stop=(c == 2))
                    ins.then_inc(w2_full.sem, 1)

                def pe_round(r):
                    for s in range(TILES):
                        if r.before and s == 2:
                            output_projection(r)
                        for f in range(2):
                            if r.now:
                                project_qk(r, s, f)
                            if r.has(s, 1):
                                transpose_qk(r, s, f)
                        if r.before and s == 2:
                            ffn_centre(r)
                        for f in range(2):
                            if r.now:
                                project_qk(r, s, 2 + f)
                            if r.has(s, 2):
                                transpose_p(r, s, f)
                        if r.has(s, 1):
                            transpose_qk(r, s, 2)
                            transpose_qk(r, s, 3)
                        if r.has(s, 2):
                            attend(r, s)
                        if r.before and s == 2:
                            ffn_variance(r)
                        if r.before and s == 3:
                            ffn_up(r)
                        if r.now:
                            project_v(r, s)
                        if r.before and s == 3:
                            ffn_down(r)
                        if r.has(s, 2):
                            transpose_o(r, s)
                        if r.has(s, 1):
                            scores(r, s)

                pe_round(Round(0, True, False))
                with pe.Fori(1, ROUNDS) as it:
                    pe_round(Round(it, True, True))
                pe_round(Round(ROUNDS, False, True))

            @block.scalar
            def _(act):
                nc.scalar.preload_act_table_set(LN_EXP_SET)
                with act.Fori(0, B) as b:
                    act.wait_ge(n_var.sem, n_var.at(b, 1))
                    nc.scalar.activation(lv[:, :], veps[:, :], ACT.Ln).then_inc(n_lnv.sem, 1)
                    act.wait_ge(n_lnv.sem, n_lnv.at(b, 1))
                    nc.scalar.activation(rstd0[:, :], lv[:, :], ACT.Exp, scale=-0.5).then_inc(n_rstd.sem, 1)

                def copy_fill(r, to, what, s, lag, f, full, done, n):
                    it, t = r.tile(s, lag)
                    act.wait_ge(full.sem, full.at(it, n * t + f + 1))
                    nc.scalar.copy(to, bank_of(r, (what, s, lag, f))).then_inc(done.sem, 1)

                def squares(r, s, half, done):
                    act.wait_ge(ss_sum.sem, ss_sum.at(r.it, 2 * s))
                    if half == 0:
                        act.wait_ge(qk_rot.sem, qk_rot.at(r.it, 4 * s + 2))
                    else:
                        act.wait_ge(qk_full.sem, qk_full.at(r.it, 4 * (s + 1)))
                    nc.scalar.activation(sq[:, INNER * half:INNER * (half + 1)].rearrange("p (a n) -> p a n", a=2), qk_ps[:, 2 * half:2 * half + 2, :],
                                         ACT.Square).then_inc(done.sem, 1)

                def inverse_norms(r, s):
                    act.wait_ge(ss_ready.sem, ss_ready.at(r.it, s + 1))
                    nc.scalar.activation(lnss[:, :], ss[:, :], ACT.Ln, scale=LN_SCALE).then_inc(ss_ln.sem, 1)
                    act.wait_ge(ss_ln.sem, ss_ln.at(r.it, s + 1))
                    act.wait_ge(rn_ready.sem, rn_ready.at(r.it, s))
                    nc.scalar.activation(rs[:, :], lnss[:, :], ACT.Exp, scale=-0.5).then_inc(rs_ready.sem, 1)

                def centred(r):
                    act.wait_ge(xh_ready.sem, xh_ready.at(r.it - 1, 0))
                    act.wait_ge(xc_full.sem, xc_full.at(r.it - 1, 1))
                    nc.scalar.copy(xc[:, :], bank_of(r, ("xc", 2, TILES, 0))).then_inc(xc_copied.sem, 1)
                    act.wait_ge(xc_copied.sem, xc_copied.at(r.it - 1, 1))
                    nc.scalar.activation(xsq[:, :], xc[:, :], ACT.Square).then_inc(xsq_ready.sem, 1)

                def inverse_deviation(r):
                    act.wait_ge(var_full.sem, var_full.at(r.it - 1, 1))
                    nc.scalar.activation(lnv[:, :], bank_of(r, ("var", 2, TILES, 0)), ACT.Ln, bias=eps_col[:, 0:1]).then_inc(lnv_ready.sem, 1)
                    act.wait_ge(lnv_ready.sem, lnv_ready.at(r.it - 1, 1))
                    nc.scalar.activation(rstd[:, :], lnv[:, :], ACT.Exp, scale=-0.5).then_inc(rstd_ready.sem, 1)

                def gelu(r):
                    for c, m in enumerate(FCH):
                        act.wait_ge(gate_full.sem, gate_full.at(r.it - 1, c + 1))
                        nc.scalar.activation(gel[0:m, c, :], bank_of(r, ("gate", 3, TILES, c))[0:m, :], ACT.Gelu, bias=col[0:m, 3 + c:4 + c]).then_inc(gelu_ready.sem, 1)
                    nc.scalar.preload_act_table_set(LN_EXP_SET)

                def exponentials(r, s):
                    it, t = r.tile(s, 2)
                    for f in range(2):
                        act.wait_ge(sc_sub.sem, sc_sub.at(it, 2 * t + f + 1))
                        if f == 0:
                            act.wait_ge(den_ready.sem, den_ready.at(it, t))
                        to = slice(512 * f, 512 * (f + 1))
                        nc.scalar.activation(pe_[:, to], pr[:, to], ACT.Exp, scale=8.0).then_inc(exp_ready.sem, 1)

                def copy_qkT(r, s, f):
                    t = r.tile(s, 1)[1]
                    if f < 2:
                        to = qT[:, 4 * f:4 * f + 4, :]
                    else:
                        to = kT[:, 4 * f - 8:4 * f - 4, WIN + P * t:WIN + P * (t + 1)]
                    copy_fill(r, to, "t", s, 1, f, qkT_full, qkT_copied, 4)

                def act_round(r):
                    for s in range(TILES):
                        if r.has(s, 1):
                            copy_qkT(r, s, 0)
                        if r.has(s, 2):
                            exponentials(r, s)
                        if r.has(s, 1):
                            copy_qkT(r, s, 1)
                        if r.before and s == 2:
                            centred(r)
                        for f in range(2):
                            if r.has(s, 2):
                                copy_fill(r, prT[:, 4 * f:4 * f + 4, :], "p", s, 2, f, pT_full, pT_copied, 2)
                        if r.now:
                            squares(r, s, 1, k_sq)
                            squares(r, s, 0, q_sq)
                        if r.has(s, 1):
                            copy_qkT(r, s, 2)
                            copy_qkT(r, s, 3)
                        if r.before and s == 2:
                            inverse_deviation(r)
                        if r.before and s == 3:
                            gelu(r)
                        if r.now:
                            moved = v_moved[(s - 2) % TILES]
                            act.wait_ge(moved.sem, moved.at(r.it, moved.per if s >= 2 else 0))
                            for par in range(2):
                                copy_fill(r, v_tok[:, s % 2, par, :], "v", s, 0, par, v_full, v_copied, 2)
                            inverse_norms(r, s)
                        if r.has(s, 2):
                            t = r.tile(s, 2)[1]
                            for f in range(2):
                                copy_fill(r, oT[:, 4 * f:4 * f + 4, P * t:P * (t + 1)], "o", s, 2, f, oT_full, oT_copied, 2)

                act_round(Round(0, True, False))
                with act.Fori(1, ROUNDS) as it:
                    act_round(Round(it, True, True))
                act_round(Round(ROUNDS, False, True))

            @block.vector
            def _(dve):
                def copy_at(to, of):
                    return nc.vector.tensor_scalar(to, of, 1.0, None, ALU.mult)

                nc.vector.memset(mean_w[:, :], 1.0 / P).then_inc(c_dve.sem, 1)
                nc.vector.memset(kT[:, :, 0:WIN], 0.0).then_inc(c_dve.sem, 1)
                nc.vector.memset(v_win[:, 0, :], 0.0).then_inc(c_dve.sem, 1)
                dve.wait_ge(s_const.sem, 32)
                nc.vector.tensor_copy(mask_bf[:, :, :, :], mask_f[:, :, :].unsqueeze(2).to_broadcast([P, 2, PAIRS, 2 * WIN])).then_inc(c_dve.sem, 1)
                dve.wait_ge(c_ident.sem, 2)
                nc.vector.tensor_copy(ident_bf[:, :], ident[:, :]).then_inc(c_dve.sem, 1)
                nc.vector.memset(eps_col[:, :], EPS).then_inc(c_dve.sem, 1)
                nc.vector.tensor_scalar(centre_w[:, :], ident[:, :], 1.0 / P, None, ALU.subtract).then_inc(c_dve.sem, 1)
                for b in range(B):
                    nc.vector.memset(state[:, b * SHIFTED:b * SHIFTED + 1], 0.0).then_inc(c_dve.sem, 1)
                dve.wait_ge(c_dve.sem, 7 + B)
                with dve.Fori(0, B) as b:
                    dve.wait_ge(n_x.sem, n_x.at(b, 16))
                    dve.wait_ge(n_state.sem, n_state.at(b, 0))
                    per_token = lambda a: a[:, :].unsqueeze(2).to_broadcast([P, TILES, P])
                    nc.vector.tensor_reduce(msum[:, :], xtok, AX.X, ALU.add).then_inc(n_steps.sem, 1)
                    dve.wait_ge(n_steps.sem, n_steps.at(b, 1))
                    nc.vector.tensor_scalar(mmean[:, :], msum[:, :], 1.0 / P, None, ALU.mult).then_inc(n_steps.sem, 1)
                    dve.wait_ge(n_steps.sem, n_steps.at(b, 2))
                    nc.vector.tensor_tensor(xctok, xtok, per_token(mmean), ALU.subtract).then_inc(n_steps.sem, 1)
                    dve.wait_ge(n_steps.sem, n_steps.at(b, 3))
                    nc.vector.tensor_tensor(sqtok, xctok, xctok, ALU.mult).then_inc(n_steps.sem, 1)
                    dve.wait_ge(n_steps.sem, n_steps.at(b, 4))
                    nc.vector.tensor_reduce(vsum[:, :], sqtok, AX.X, ALU.add).then_inc(n_steps.sem, 1)
                    dve.wait_ge(n_steps.sem, n_steps.at(b, 5))
                    nc.vector.tensor_scalar(veps[:, :], vsum[:, :], 1.0 / P, EPS, ALU.mult, ALU.add).then_inc(n_var.sem, 1)
                    dve.wait_ge(n_rstd.sem, n_rstd.at(b, 1))
                    nc.vector.tensor_tensor(xntok, xctok, per_token(rstd0), ALU.mult).then_inc(n_xn.sem, 1)
                    dve.wait_ge(n_tr.sem, n_tr.at(b, 1))
                    copy_at(state[:, state_cols(b, 1, T)], ring[:, 0, :]).then_inc(n_state.sem, 1)
                dve.wait_ge(n_state.sem, B)

                def shift_tokens(to, b, done):
                    copy_at(to[0:64, :], state[0:64, state_cols(b, 1, T)]).then_inc(done.sem, 1)
                    copy_at(to[64:P, :], state[64:P, state_cols(b, 0, T)]).then_inc(done.sem, 1)

                def rotate(r, s, half):
                    if half == 0:
                        if s == 0:
                            dve.wait_ge(rot_ready.sem, rot_ready.at(r.it >> 2, 1))
                        dve.wait_ge(qk_scaled.sem, qk_scaled.at(r.it, 2 * s))
                        dve.wait_ge(qk_full.sem, qk_full.at(r.it, 4 * s + 2))
                    else:
                        dve.wait_ge(k_sq.sem, k_sq.at(r.it, s + 1))
                    of = qk_ps[:, 2 * half:2 * half + 2, :].rearrange("p a n -> p (a n)")
                    own = of.rearrange("p (h d) -> p h d", d=DH)
                    to = slice(INNER * half, INNER * (half + 1))
                    nc.vector.tensor_tensor(
                        t1[:, to].rearrange("p (h d) -> p h d", d=DH), own,
                        rot[:, 2 * half, s:s + 1, :].to_broadcast([P, HEADS, DH]), ALU.mult).then_inc(qk_rot.sem, 1)
                    swapped = of.rearrange("p (h s d) -> p h s d", s=2, d=DH // 2)[:, :, ::-1, :]
                    nc.vector.tensor_tensor(
                        t2[:, to].rearrange("p (h s d) -> p h s d", s=2, d=DH // 2), swapped,
                        rot[:, 2 * half + 1, s:s + 1, :].to_broadcast([P, HEADS, DH]).rearrange("p h (s d) -> p h s d", s=2),
                        ALU.mult).then_inc(qk_rot.sem, 1)

                def sum_squares(r, s, half):
                    done = (q_sq, k_sq)[half]
                    dve.wait_ge(done.sem, done.at(r.it, s + 1))
                    nc.vector.tensor_reduce(lnsum[:, HEADS * half:HEADS * (half + 1)], sq[:, INNER * half:INNER * (half + 1)].rearrange("p (h d) -> p h d", d=DH),
                                            AX.X, ALU.add).then_inc(ss_sum.sem, 1)
                    if half == 1:
                        dve.wait_ge(ss_sum.sem, ss_sum.at(r.it, 2 * (s + 1)))
                        nc.vector.tensor_scalar(ss[:, :], lnsum[:, :], NORM_FLOOR, None, ALU.max).then_inc(ss_ready.sem, 1)

                def newton_step(r, s):
                    dve.wait_ge(rs_ready.sem, rs_ready.at(r.it, s + 1))
                    dve.wait_ge(qk_scaled.sem, qk_scaled.at(r.it, 2 * s))
                    nc.vector.tensor_tensor(nw1[:, :], rs[:, :], rs[:, :], ALU.mult).then_inc(newton.sem, 1)
                    dve.wait_ge(newton.sem, newton.at(r.it, 2 * s + 1))
                    nc.vector.scalar_tensor_tensor(nw2[:, :], nw1[:, :], -0.5 * LN_SCALE * LN_SCALE ** 0.5, ss[:, :], ALU.mult, ALU.mult).then_inc(newton.sem, 1)
                    dve.wait_ge(newton.sem, newton.at(r.it, 2 * s + 2))
                    nc.vector.scalar_tensor_tensor(rn[:, :], nw2[:, :], 1.5 * LN_SCALE ** 0.5, rs[:, :], ALU.add, ALU.mult).then_inc(rn_ready.sem, 1)

                def row_max(r, s):
                    it, t = r.tile(s, 1)
                    dve.wait_ge(sc_full.sem, sc_full.at(it, t + 1))
                    nc.vector.tensor_reduce(smax[:, :], sc_ps[:, :, :].rearrange("p a n -> p (a n)").rearrange("p (h k) -> p h k", k=64), AX.X, ALU.max).then_inc(max_ready.sem, 1)
                    dve.wait_ge(max_ready.sem, max_ready.at(it, t + 1))
                    for f in range(2):
                        pairs = slice(4 * f, 4 * (f + 1))
                        nc.vector.tensor_tensor(
                            pr[:, :].rearrange("p (h a k) -> p a h k", a=2, k=64)[:, :, pairs, :],
                            sc_ps[:, :, :].rearrange("p a (h k) -> p a h k", k=64)[:, :, pairs, :],
                            smax[:, :].rearrange("p (a h) -> p a h", a=2)[:, :, pairs].unsqueeze(3).to_broadcast([P, 2, 4, 64]), ALU.subtract).then_inc(sc_sub.sem, 1)

                def row_sum(r, s):
                    it, t = r.tile(s, 2)
                    dve.wait_ge(exp_ready.sem, exp_ready.at(it, 2 * (t + 1)))
                    nc.vector.tensor_reduce(den[:, :], pe_[:, :].rearrange("p (h k) -> p h k", k=64), AX.X, ALU.add).then_inc(den_ready.sem, 1)
                    dve.wait_ge(den_ready.sem, den_ready.at(it, t + 1))
                    nc.vector.reciprocal(rden[:, :], den[:, :]).then_inc(rden_ready.sem, 1)

                def normalise(r, s):
                    it, t = r.tile(s, 2)
                    dve.wait_ge(rden_ready.sem, rden_ready.at(it, t + 1))
                    dve.wait_ge(oT_full.sem, oT_full.at(it, 2 * t))
                    dve.wait_ge(av_full.sem, av_full.at(it, t + 1))
                    for f in range(2):
                        pairs = slice(4 * f, 4 * (f + 1))
                        nc.vector.tensor_tensor(
                            o_tok[:, :].rearrange("p (h a d) -> p a h d", a=2, d=DH)[:, :, pairs, :],
                            sc_ps[:, :, :].rearrange("p a (h d) -> p a h d", d=DH)[:, :, pairs, :],
                            rden[:, :].rearrange("p (h a) -> p a h", a=2)[:, :, pairs].unsqueeze(3).to_broadcast([P, 2, 4, DH]), ALU.mult).then_inc(o_ready.sem, 1)

                def add_attention(r):
                    dve.wait_ge(x_ffn.sem, x_ffn.at(r.it - 1, 0))
                    dve.wait_ge(wo_full.sem, wo_full.at(r.it - 1, 1))
                    now = state[:, state_cols((r.it + 3) & 3, 1, T)]
                    nc.vector.tensor_tensor(now, bank_of(r, ("wo", 2, TILES, 0)), now, ALU.add).then_inc(x_attn.sem, 1)
                    dve.wait_ge(x_attn.sem, x_attn.at(r.it - 1, 1))
                    shift_tokens(xs2, (r.it + 3) & 3, xs2_ready)

                def ffn_norm(r):
                    dve.wait_ge(rstd_ready.sem, rstd_ready.at(r.it - 1, 1))
                    nc.vector.tensor_tensor(xh[:, :], xc[:, :], rstd[:, :], ALU.mult).then_inc(xh_ready.sem, 1)
                    dve.wait_ge(xh_ready.sem, xh_ready.at(r.it - 1, 1))
                    nc.vector.tensor_scalar(xn[:, :], xh[:, :], col[:, 6:7], col[:, 7:8], ALU.mult, ALU.add).then_inc(xn_ready.sem, 1)

                def ffn_gated(r, c):
                    m = FCH[c]
                    dve.wait_ge(gelu_ready.sem, gelu_ready.at(r.it - 1, c + 1))
                    dve.wait_ge(lin_full.sem, lin_full.at(r.it - 1, c + 1))
                    nc.vector.scalar_tensor_tensor(u[0:m, c, :], bank_of(r, ("lin", 3, TILES, c))[0:m, :], col[0:m, c:c + 1], gel[0:m, c, :],
                                                   ALU.add, ALU.mult).then_inc(u_ready.sem, 1)

                def add_ffn(r):
                    dve.wait_ge(w2_full.sem, w2_full.at(r.it - 1, 1))
                    now = state[:, state_cols((r.it + 3) & 3, 1, T)]
                    nc.vector.scalar_tensor_tensor(now, bank_of(r, ("w2", 3, TILES, 0)), col[:, 8:9], now, ALU.add, ALU.add).then_inc(x_ffn.sem, 1)

                def dve_round(r):
                    for s in range(TILES):
                        if r.before and s == 2:
                            add_attention(r)
                        if r.now:
                            rotate(r, s, 0)
                        if r.has(s, 2):
                            row_sum(r, s)
                        if r.now:
                            rotate(r, s, 1)
                            sum_squares(r, s, 0)
                        if r.has(s, 2):
                            normalise(r, s)
                        if r.before and s == 3:
                            ffn_gated(r, 0)
                        if r.now:
                            sum_squares(r, s, 1)
                        if r.before and s == 2:
                            ffn_norm(r)
                        if r.before and s == 3:
                            ffn_gated(r, 1)
                            ffn_gated(r, 2)
                        if r.now:
                            newton_step(r, s)
                        if r.before and s == 3:
                            add_ffn(r)
                        if r.has(s, 1):
                            row_max(r, s)
                    if r.now:
                        dve.wait_ge(v_full.sem, v_full.at(r.it, v_full.per))
                        dve.wait_ge(x_ffn.sem, x_ffn.at(r.it, 0))
                        shift_tokens(xs, (r.it + 1) & 3, xs_ready)

                shift_tokens(xs, 0, xs_ready)
                dve_round(Round(0, True, False))
                with dve.Fori(1, ROUNDS) as it:
                    dve_round(Round(it, True, True))
                dve_round(Round(ROUNDS, False, True))



RH, RK, RV = 4, 32, 64
NE, BN = 8, 64
AK = P ** -0.5
STEPS = 52


def build_mixers(nc, state, x, out, w_ret, w_ro, ret_cols, g_norm, ret_rot, ret_decay, ret_diag, ret_block,
                 w_att, att_rot, att_mask, w_gate, w_down, w_up, b_down, b_up, expert_rows, before):
    ctx = ExitStack()
    with ctx:
        def sb(name, shape, dt=F32):
            return ctx.enter_context(nc.sbuf_tensor(name, shape, dt))

        def sig(name, per=1):
            return Signal(ctx, nc, name, per)

        proj = ctx.enter_context(nc.psum_tensor("proj", [P, 2, 512], F32))
        head = ctx.enter_context(nc.psum_tensor("head", [P, 4, 512], F32))
        turn = ctx.enter_context(nc.psum_tensor("turn", [P, 512], F32))
        outs = ctx.enter_context(nc.psum_tensor("outs", [P, 512], F32))

        c_ident = sb("m_ident", [P, P])
        mean_w = sb("m_mean_w", [P, P])
        eps_col = sb("m_eps_col", [P, 1])
        wr = sb("wr", [P, 6 * P])
        wro = sb("wro", [P, 2, P])
        rcol = sb("rcol", [P, 3])
        gnw = sb("gnw", [P, 2 * P])
        rrot = sb("rrot", [P, 2, TILES, 2 * P])
        rdec = sb("rdec", [P, 2, P])
        rdiag = sb("rdiag", [P, RH, P])
        rblock = sb("rblock", [P, 2 * P])
        wa = sb("wa", [P, 3 * P])
        arot = sb("arot", [P, 2, TILES, 2 * P])
        amask = sb("amask", [P, TILES, T])
        wg = sb("wg", [P, NE])
        wd = sb("wd", [P, NE * BN])
        wu = sb("wu", [P, 4, P])
        bd = sb("bd", [P, 4])
        bu = sb("bu", [NE, P])
        erows = sb("erows", [NE, 4, P])
        ebefore = sb("ebefore", [P, NE, NE])

        xtok = sb("m_xtok", [P, TILES, P])
        msum = sb("m_msum", [P, TILES])
        mmean = sb("m_mmean", [P, TILES])
        vsum = sb("m_vsum", [P, TILES])
        xctok = sb("m_xctok", [P, TILES, P])
        sqtok = sb("m_sqtok", [P, TILES, P])
        var = sb("m_var", [P, TILES])
        lv = sb("m_lv", [P, TILES])
        rstd0 = sb("m_rstd0", [P, TILES])
        xntok = sb("m_xntok", [P, TILES, P])
        nrtok = sb("m_nrtok", [P, TILES, P])
        x0T = sb("x0T", [P, T])
        xnT = sb("xnT", [P, T])
        nrT = sb("nrT", [P, T])
        rt1 = sb("rt1", [P, 2 * P])
        rt2 = sb("rt2", [P, 2 * P])
        rqk = sb("rqk", [P, 2 * P])
        qcr = sb("qcr", [P, P])
        kst = sb("kst", [P, P])
        vsb = sb("vsb", [P, 2 * P])
        sg = sb("sg", [P, 2 * P])
        rT = sb("rT", [P, 3, P])
        at = sb("at", [P, RH, P])
        st = sb("st", [P, 2 * P])
        stn = sb("stn", [P, 2 * P])
        osq = sb("osq", [P, 2 * P])
        oss = sb("oss", [P, RH])
        oln = sb("oln", [P, RH])
        orst = sb("orst", [P, RH])
        o1 = sb("o1", [P, 2 * P])
        o2 = sb("o2", [P, 2 * P])
        o3 = sb("o3", [P, 2 * P])
        orT = sb("orT", [P, 2, T])
        sT = sb("sT", [P, T])
        gT = sb("gT", [P, T])
        sgT = sb("sgT", [P, T])
        x1T = sb("x1T", [P, T])
        xc = sb("m_xc", [P, T])
        xsq = sb("m_xsq", [P, T])
        lnv = sb("m_lnv", [P, T])
        rstd = sb("m_rstd", [P, T])
        xm = sb("xm", [P, T])
        aq1 = sb("aq1", [P, 2 * P])
        aq2 = sb("aq2", [P, 2 * P])
        aqk = sb("aqk", [P, 2 * P])
        aqT = sb("aqT", [P, TILES, P])
        akT = sb("akT", [P, TILES, P])
        av = sb("av", [P, TILES, P])
        asc = sb("asc", [P, T])
        amx = sb("amx", [P, 1])
        aneg = sb("aneg", [P, 1])
        aex = sb("aex", [P, T])
        aden = sb("aden", [P, 1])
        arden = sb("arden", [P, 1])
        apr = sb("apr", [P, T])
        apT = sb("apT", [P, TILES, P])
        s1T = sb("s1T", [P, T])
        lg = sb("lg", [P, TILES, NE])
        beats = sb("beats", [P, TILES, NE, NE])
        ties = sb("ties", [P, TILES, NE, NE])
        tied = sb("tied", [P, TILES, NE, NE])
        wins = sb("wins", [P, TILES, NE, NE])
        rank = sb("rank", [P, TILES, NE])
        sel = sb("sel", [P, TILES, NE])
        gmx = sb("gmx", [P, TILES])
        gsub = sb("gsub", [P, TILES, NE])
        gex = sb("gex", [P, TILES, NE])
        gsel = sb("gsel", [P, TILES, NE])
        gden = sb("gden", [P, TILES])
        grd = sb("grd", [P, TILES])
        gate = sb("gate", [P, TILES, NE])
        gaT = sb("gaT", [NE, T])
        hid = sb("hid", [P, 4, T])
        hg = sb("hg", [P, 4, T])
        moe = sb("moe", [P, T])
        x2T = sb("x2T", [P, T])
        xo = sb("xo", [P, TILES, P])

        loads = [(wr[:, :], w_ret), (wro[:, :, :], w_ro), (rcol[:, :], ret_cols), (rrot[:, :, :, :], ret_rot),
                 (rdec[:, :, :], ret_decay), (rdiag[:, :, :], ret_diag), (rblock[:, :], ret_block), (wa[:, :], w_att),
                 (arot[:, :, :, :], att_rot), (amask[:, :, :], att_mask), (wg[:, :], w_gate), (wd[:, :], w_down),
                 (wu[:, :, :], w_up), (bd[:, :], b_down), (bu[:, :], b_up), (erows[:, :, :], expert_rows)]
        c_loads = sig("c_loads")
        m_ident = sig("m_identity")
        c_set = sig("c_set")
        x_in = sig("x_in", 16)
        steps = sig("steps", 0)
        x_stats = sig("x_stats", 2)
        x_ln = sig("x_ln", 2)
        x_rstd = sig("x_rstd", 2)
        xn_there = sig("xn_there", 2)
        xT_full = sig("xT_full", 3)
        xT_there = sig("xT_there", 3)
        r_proj = sig("r_proj", TILES)
        r_v = sig("r_v", TILES)
        r_sg = sig("r_sg", TILES)
        r_rot = sig("r_rot", TILES)
        r_dec = sig("r_dec", TILES)
        r_turned = sig("r_turned", TILES)
        r_T = sig("r_T", TILES)
        r_sc = sig("r_sc", TILES)
        r_at = sig("r_at", TILES)
        r_out = sig("r_out", TILES)
        r_upd = sig("r_upd", TILES - 1)
        r_state = sig("r_state", TILES - 1)
        r_sq = sig("r_sq", TILES)
        r_ms = sig("r_ms", TILES)
        r_ln = sig("r_ln", TILES)
        r_rstd = sig("r_rstd", TILES)
        r_o = sig("r_o", TILES)
        r_oturn = sig("r_oturn", TILES)
        r_oT = sig("r_oT", TILES)
        r_wo = sig("r_wo")
        s_gate = sig("s_gate")
        x1_there = sig("x1_there")
        m_mean = sig("m_mean")
        m_xc = sig("m_xc_there")
        m_sq = sig("m_sq")
        m_varf = sig("m_varf")
        m_lnv = sig("m_lnv_there")
        m_rstd = sig("m_rstd_there")
        xm_there = sig("xm_there")
        a_proj = sig("a_proj", TILES)
        a_v = sig("a_v", TILES)
        a_rot = sig("a_rot", TILES)
        a_turned = sig("a_turned", TILES)
        a_T = sig("a_T", TILES)
        a_sc = sig("a_sc", TILES)
        a_max = sig("a_max", TILES)
        a_exp = sig("a_exp", TILES)
        a_p = sig("a_p", TILES)
        a_pturn = sig("a_pturn", TILES)
        a_pT = sig("a_pT", TILES)
        a_out = sig("a_out", TILES)
        s1_there = sig("s1_there")
        e_lg = sig("e_lg")
        e_sub = sig("e_sub")
        e_exp = sig("e_exp")
        e_gate = sig("e_gate")
        e_gturn = sig("e_gturn")
        e_gT = sig("e_gT")
        e_down = sig("e_down", 4)
        e_hid = sig("e_hid", 4)
        e_spread = sig("e_spread", 4)
        e_hg = sig("e_hg", 4)
        e_up = sig("e_up")
        e_silu = sig("e_silu")
        x2_there = sig("x2_there")
        x2_turn = sig("x2_turn")
        xo_there = sig("xo_there")
        stored = sig("stored", 16)

        with nc.Block() as block:

            @block.sync
            def _(sp):
                sp.dma_start(gnw[:, :], g_norm.to_broadcast([P, 2 * P])).then_inc(c_loads.sem, 16)
                sp.dma_start(ebefore[:, :, :].rearrange("p e f -> p (e f)"), before.to_broadcast([P, NE * NE])).then_inc(c_loads.sem, 16)
                for to, of in loads:
                    sp.dma_start(to, of).then_inc(c_loads.sem, 16)
                with sp.Fori(0, B) as b:
                    sp.wait_ge(xT_full.sem, xT_full.at(b, 0))
                    sp.dma_start(xtok[:, :, :], x[bass.ds(b, 1), :, :].rearrange("o (t p) d -> p (o t) d", p=P)).then_inc(x_in.sem, 16)
                    sp.wait_ge(xo_there.sem, xo_there.at(b, 1))
                    sp.dma_start(out[bass.ds(b, 1), :, :].rearrange("o (t p) d -> p (o t) d", p=P), xo[:, :, :]).then_inc(stored.sem, 16)
                sp.wait_ge(stored.sem, 16 * B)

            all_loads = 16 * (len(loads) + 2)

            @block.gpsimd
            def _(pool):
                nc.gpsimd.memset(c_ident[:, :], 0.0).then_inc(m_ident.sem, 1)
                pool.wait_ge(m_ident.sem, 1)
                nc.gpsimd.affine_select(out=c_ident[:, :], in_=c_ident[:, :], compare_op=ALU.not_equal, fill=1.0,
                                        base=0, pattern=[[-1, P]], channel_multiplier=1).then_inc(m_ident.sem, 1)

            @block.tensor
            def _(pe):
                pe.wait_ge(m_ident.sem, 2)
                pe.wait_ge(c_set.sem, 2)
                pe.wait_ge(c_loads.sem, all_loads)
                with pe.Fori(0, B) as b:
                    def turn4(of, done, to=turn):
                        for t in range(TILES):
                            ins = nc.tensor.transpose(to[:, t * P:(t + 1) * P], of(t), c_ident[:, :])
                        ins.then_inc(done.sem, 1)

                    for n, of in enumerate((xtok, xntok, nrtok)):
                        if n == 0:
                            pe.wait_ge(x_in.sem, x_in.at(b, 16))
                            pe.wait_ge(xo_there.sem, xo_there.at(b, 0))
                        else:
                            pe.wait_ge(xn_there.sem, xn_there.at(b, n))
                            pe.wait_ge(xT_there.sem, xT_there.at(b, n))
                        turn4(lambda t: of[:, t, :], xT_full)
                    pe.wait_ge(xT_there.sem, xT_there.at(b, 3))

                    for t in range(TILES):
                        xt = nrT[:, t * P:(t + 1) * P]
                        pe.wait_ge(r_rot.sem, r_rot.at(b, t))
                        pe.wait_ge(r_sg.sem, r_sg.at(b, t))
                        if t == 0:
                            pe.wait_ge(a_rot.sem, a_rot.at(b, 0))
                        nc.tensor.matmul(proj[:, 0, :], xt, wr[:, 0:512], start=True, stop=True)
                        nc.tensor.matmul(proj[:, 1, 0:2 * P], xt, wr[:, 512:768], start=True, stop=True).then_inc(r_proj.sem, 1)
                        pe.wait_ge(r_dec.sem, r_dec.at(b, t + 1))
                        pe.wait_ge(r_oT.sem, r_oT.at(b, t))
                        for n, of in enumerate((rqk[:, 0:P], rqk[:, P:2 * P], qcr[:, :])):
                            ins = nc.tensor.transpose(turn[:, n * P:(n + 1) * P], of, c_ident[:, :])
                        ins.then_inc(r_turned.sem, 1)
                        pe.wait_ge(r_T.sem, r_T.at(b, t + 1))
                        pe.wait_ge(r_state.sem, r_state.at(b, t))
                        if t == 0:
                            pe.wait_ge(x2_there.sem, x2_there.at(b, 0))
                        for h in range(RH):
                            rows = slice(RK * h, RK * (h + 1))
                            ins = nc.tensor.matmul(head[:, h, 0:P], rT[rows, 1, :], rT[rows, 0, :], start=True, stop=True)
                        ins.then_inc(r_sc.sem, 1)
                        pe.wait_ge(r_v.sem, r_v.at(b, t + 1))
                        pe.wait_ge(r_at.sem, r_at.at(b, t + 1))
                        pe.wait_ge(r_o.sem, r_o.at(b, t))
                        if t > 0:
                            nc.tensor.matmul(outs[:, 0:2 * P], rT[:, 2, :], st[:, :], start=True, stop=False, skip_group_check=True)
                        for h in range(RH):
                            cols = slice(RV * h, RV * (h + 1))
                            ins = nc.tensor.matmul(outs[:, cols], at[:, h, :], vsb[:, cols], start=(t == 0 and h == 0), stop=(h == RH - 1),
                                                   skip_group_check=True)
                        ins.then_inc(r_out.sem, 1)
                        if t < TILES - 1:
                            nc.tensor.matmul(head[:, 3, 0:2 * P], kst[:, :], vsb[:, :], start=True, stop=True).then_inc(r_upd.sem, 1)
                        pe.wait_ge(r_o.sem, r_o.at(b, t + 1))
                        for n in range(2):
                            ins = nc.tensor.transpose(turn[:, n * P:(n + 1) * P], o3[:, n * P:(n + 1) * P], c_ident[:, :])
                        ins.then_inc(r_oturn.sem, 1)
                    pe.wait_ge(r_oT.sem, r_oT.at(b, TILES))
                    for n in range(2):
                        ins = nc.tensor.matmul(head[:, 0, :], wro[:, n, :], orT[:, n, :], start=(n == 0), stop=(n == 1))
                    ins.then_inc(r_wo.sem, 1)

                    pe.wait_ge(x1_there.sem, x1_there.at(b, 1))
                    nc.tensor.matmul(head[:, 1, :], mean_w[:, :], x1T[:, :], start=True, stop=True).then_inc(m_mean.sem, 1)
                    pe.wait_ge(m_sq.sem, m_sq.at(b, 1))
                    nc.tensor.matmul(head[:, 2, :], mean_w[:, :], xsq[:, :], start=True, stop=True).then_inc(m_varf.sem, 1)
                    pe.wait_ge(xm_there.sem, xm_there.at(b, 1))

                    for t in range(TILES):
                        ins = nc.tensor.matmul(head[:, 3, NE * t:NE * (t + 1)], xm[:, t * P:(t + 1) * P], wg[:, :], start=True, stop=True)
                    ins.then_inc(e_lg.sem, 1)

                    for t in range(TILES):
                        pe.wait_ge(a_rot.sem, a_rot.at(b, t))
                        pe.wait_ge(a_v.sem, a_v.at(b, t))
                        nc.tensor.matmul(proj[:, 0, 0:3 * P], xm[:, t * P:(t + 1) * P], wa[:, :], start=True, stop=True).then_inc(a_proj.sem, 1)
                        pe.wait_ge(a_rot.sem, a_rot.at(b, t + 1))
                        pe.wait_ge(a_T.sem, a_T.at(b, t))
                        for n in range(2):
                            ins = nc.tensor.transpose(turn[:, n * P:(n + 1) * P], aqk[:, n * P:(n + 1) * P], c_ident[:, :])
                        ins.then_inc(a_turned.sem, 1)
                    pe.wait_ge(a_T.sem, a_T.at(b, TILES))
                    for t in range(TILES):
                        pe.wait_ge(a_max.sem, a_max.at(b, t))
                        nc.tensor.matmul(head[:, 0, :], aqT[:, t, :], akT[:, :, :], start=True, stop=True).then_inc(a_sc.sem, 1)
                        pe.wait_ge(a_p.sem, a_p.at(b, t + 1))
                        turn4(lambda n: apr[:, n * P:(n + 1) * P], a_pturn)
                        pe.wait_ge(a_pT.sem, a_pT.at(b, t + 1))
                        for n in range(TILES):
                            ins = nc.tensor.matmul(outs[:, t * P:(t + 1) * P], av[:, n, :], apT[:, n, :], start=(n == 0), stop=(n == TILES - 1))
                        ins.then_inc(a_out.sem, 1)

                    pe.wait_ge(e_gate.sem, e_gate.at(b, 1))
                    for t in range(TILES):
                        ins = nc.tensor.transpose(turn[0:NE, t * P:(t + 1) * P], gate[:, t, :], c_ident[:, :])
                    ins.then_inc(e_gturn.sem, 1)
                    pe.wait_ge(e_gT.sem, e_gT.at(b, 1))
                    for c in range(4):
                        pe.wait_ge(e_hg.sem, e_hg.at(b, c))
                        nc.tensor.matmul(head[:, 1, :], wd[:, P * c:P * (c + 1)], xm[:, :], start=True, stop=True).then_inc(e_down.sem, 1)
                        nc.tensor.matmul(head[:, 2, :], erows[:, c, :], gaT[:, :], start=True, stop=True).then_inc(e_spread.sem, 1)
                    pe.wait_ge(e_hg.sem, e_hg.at(b, 4))
                    for c in range(4):
                        nc.tensor.matmul(head[:, 3, :], wu[:, c, :], hg[:, c, :], start=(c == 0), stop=False)
                    nc.tensor.matmul(head[:, 3, :], bu[:, :], gaT[:, :], start=False, stop=True).then_inc(e_up.sem, 1)
                    pe.wait_ge(x2_there.sem, x2_there.at(b, 1))
                    turn4(lambda t: x2T[:, t * P:(t + 1) * P], x2_turn)

            @block.scalar
            def _(act):
                act.wait_ge(c_set.sem, 2)
                act.wait_ge(c_loads.sem, all_loads)
                with act.Fori(0, B) as b:
                    for n in range(2):
                        act.wait_ge(x_stats.sem, x_stats.at(b, n + 1))
                        nc.scalar.activation(lv[:, :], var[:, :], ACT.Ln).then_inc(x_ln.sem, 1)
                        act.wait_ge(x_ln.sem, x_ln.at(b, n + 1))
                        nc.scalar.activation(rstd0[:, :], lv[:, :], ACT.Exp, scale=-0.5).then_inc(x_rstd.sem, 1)
                    nc.scalar.activation(sgT[:, :], state[:, bass.ds(b * SHIFTED + 1, T)], ACT.Silu).then_inc(s_gate.sem, 1)
                    for n, to in enumerate((x0T, xnT)):
                        act.wait_ge(xT_full.sem, xT_full.at(b, n + 1))
                        nc.scalar.copy(to[:, :], turn[:, :]).then_inc(xT_there.sem, 1)
                    act.wait_ge(xT_full.sem, xT_full.at(b, 3))
                    nc.scalar.activation(nrT[:, :], turn[:, :], ACT.Identity, bias=rcol[:, 1:2], scale=rcol[:, 0:1]).then_inc(xT_there.sem, 1)

                    for t in range(TILES):
                        act.wait_ge(r_rot.sem, r_rot.at(b, t + 1))
                        nc.scalar.copy(vsb[:, :], proj[:, 0, 2 * P:4 * P]).then_inc(r_v.sem, 1)
                        nc.scalar.activation(sg[:, :], proj[:, 1, 0:2 * P], ACT.Silu).then_inc(r_sg.sem, 1)
                        act.wait_ge(r_turned.sem, r_turned.at(b, t + 1))
                        nc.scalar.copy(rT[:, :, :], turn[:, 0:3 * P]).then_inc(r_T.sem, 1)
                        act.wait_ge(r_out.sem, r_out.at(b, t + 1))
                        nc.scalar.activation(osq[:, :], outs[:, 0:2 * P], ACT.Square).then_inc(r_sq.sem, 1)
                        act.wait_ge(r_ms.sem, r_ms.at(b, t + 1))
                        nc.scalar.activation(oln[:, :], oss[:, :], ACT.Ln, bias=eps_col[:, 0:1], scale=1.0 / RV).then_inc(r_ln.sem, 1)
                        act.wait_ge(r_ln.sem, r_ln.at(b, t + 1))
                        nc.scalar.activation(orst[:, :], oln[:, :], ACT.Exp, scale=-0.5).then_inc(r_rstd.sem, 1)
                        act.wait_ge(r_oturn.sem, r_oturn.at(b, t + 1))
                        nc.scalar.copy(orT[:, :, t * P:(t + 1) * P], turn[:, 0:2 * P]).then_inc(r_oT.sem, 1)

                    act.wait_ge(m_xc.sem, m_xc.at(b, 1))
                    nc.scalar.activation(xsq[:, :], xc[:, :], ACT.Square).then_inc(m_sq.sem, 1)
                    act.wait_ge(m_varf.sem, m_varf.at(b, 1))
                    nc.scalar.activation(lnv[:, :], head[:, 2, :], ACT.Ln, bias=eps_col[:, 0:1]).then_inc(m_lnv.sem, 1)
                    act.wait_ge(m_lnv.sem, m_lnv.at(b, 1))
                    nc.scalar.activation(rstd[:, :], lnv[:, :], ACT.Exp, scale=-0.5).then_inc(m_rstd.sem, 1)

                    act.wait_ge(e_sub.sem, e_sub.at(b, 1))
                    nc.scalar.activation(gex[:, :, :], gsub[:, :, :], ACT.Exp).then_inc(e_exp.sem, 1)
                    for t in range(TILES):
                        act.wait_ge(a_rot.sem, a_rot.at(b, t + 1))
                        nc.scalar.copy(av[:, t, :], proj[:, 0, 2 * P:3 * P]).then_inc(a_v.sem, 1)
                        act.wait_ge(a_turned.sem, a_turned.at(b, t + 1))
                        nc.scalar.copy(aqT[:, t, :], turn[:, 0:P])
                        nc.scalar.copy(akT[:, t, :], turn[:, P:2 * P]).then_inc(a_T.sem, 1)
                    for t in range(TILES):
                        act.wait_ge(a_max.sem, a_max.at(b, t + 1))
                        act.wait_ge(a_p.sem, a_p.at(b, t))
                        nc.scalar.activation(aex[:, :], asc[:, :], ACT.Exp, bias=aneg[:, 0:1], scale=AK, accum_out=aden[:, 0:1]).then_inc(a_exp.sem, 1)
                        act.wait_ge(a_pturn.sem, a_pturn.at(b, t + 1))
                        nc.scalar.copy(apT[:, :, :], turn[:, :]).then_inc(a_pT.sem, 1)

                    act.wait_ge(a_out.sem, a_out.at(b, TILES))
                    nc.scalar.copy(s1T[:, :], outs[:, :]).then_inc(s1_there.sem, 1)
                    act.wait_ge(e_gturn.sem, e_gturn.at(b, 1))
                    nc.scalar.copy(gaT[:, :], turn[0:NE, :]).then_inc(e_gT.sem, 1)
                    for c in range(4):
                        act.wait_ge(e_down.sem, e_down.at(b, c + 1))
                        nc.scalar.activation(hid[:, c, :], head[:, 1, :], ACT.Relu, bias=bd[:, c:c + 1]).then_inc(e_hid.sem, 1)
                    act.wait_ge(e_up.sem, e_up.at(b, 1))
                    nc.scalar.activation(moe[:, :], head[:, 3, :], ACT.Silu, scale=0.5).then_inc(e_silu.sem, 1)

            @block.vector
            def _(dve):
                nc.vector.memset(mean_w[:, :], 1.0 / P).then_inc(c_set.sem, 1)
                nc.vector.memset(eps_col[:, :], EPS).then_inc(c_set.sem, 1)
                dve.wait_ge(c_loads.sem, all_loads)
                count = [0]
                with dve.Fori(0, B) as b:
                    def then(ins):
                        count[0] += 1
                        ins.then_inc(steps.sem, 1)
                        dve.wait_ge(steps.sem, steps.at(b, count[0]))

                    steps.per = STEPS
                    dve.wait_ge(x_in.sem, x_in.at(b, 16))
                    for n, (of, to) in enumerate(((xtok, xntok), (xntok, nrtok))):
                        per_token = lambda a: a[:, :].unsqueeze(2).to_broadcast([P, TILES, P])
                        then(nc.vector.tensor_reduce(msum[:, :], of[:, :, :], AX.X, ALU.add))
                        then(nc.vector.tensor_scalar(mmean[:, :], msum[:, :], 1.0 / P, None, ALU.mult))
                        then(nc.vector.tensor_tensor(xctok[:, :, :], of[:, :, :], per_token(mmean), ALU.subtract))
                        then(nc.vector.tensor_tensor(sqtok[:, :, :], xctok[:, :, :], xctok[:, :, :], ALU.mult))
                        then(nc.vector.tensor_reduce(vsum[:, :], sqtok[:, :, :], AX.X, ALU.add))
                        nc.vector.tensor_scalar(var[:, :], vsum[:, :], 1.0 / P, EPS, ALU.mult, ALU.add).then_inc(x_stats.sem, 1)
                        dve.wait_ge(x_rstd.sem, x_rstd.at(b, n + 1))
                        nc.vector.tensor_tensor(to[:, :, :], xctok[:, :, :], per_token(rstd0), ALU.mult).then_inc(xn_there.sem, 1)
                        dve.wait_ge(xn_there.sem, xn_there.at(b, n + 1))

                    for t in range(TILES):
                        dve.wait_ge(r_proj.sem, r_proj.at(b, t + 1))
                        if t > 0:
                            dve.wait_ge(r_upd.sem, r_upd.at(b, t))
                        of = proj[:, 0, 0:2 * P]
                        nc.vector.tensor_tensor(rt1[:, :], of, rrot[:, 0, t, :], ALU.mult)
                        then(nc.vector.tensor_tensor(
                            rt2[:, :].rearrange("p (h s d) -> p h s d", s=2, d=RK // 2),
                            of.rearrange("p (h s d) -> p h s d", s=2, d=RK // 2)[:, :, ::-1, :],
                            rrot[:, 1, t, :].rearrange("p (h s d) -> p h s d", s=2, d=RK // 2), ALU.mult))
                        nc.vector.tensor_tensor(rqk[:, :], rt1[:, :], rt2[:, :], ALU.add).then_inc(r_rot.sem, 1)
                        dve.wait_ge(r_rot.sem, r_rot.at(b, t + 1))
                        nc.vector.tensor_tensor(qcr[:, :], rqk[:, 0:P], rdec[:, 0, :], ALU.mult)
                        nc.vector.tensor_tensor(kst[:, :], rqk[:, P:2 * P], rdec[:, 1, :], ALU.mult).then_inc(r_dec.sem, 1)
                        dve.wait_ge(r_sc.sem, r_sc.at(b, t + 1))
                        nc.vector.tensor_tensor(at[:, :, :], head[:, :, 0:P], rdiag[:, :, :], ALU.mult).then_inc(r_at.sem, 1)
                        if t < TILES - 1:
                            dve.wait_ge(r_upd.sem, r_upd.at(b, t + 1))
                            if t == 0:
                                nc.vector.tensor_tensor(st[:, :], head[:, 3, 0:2 * P], rblock[:, :], ALU.mult).then_inc(r_state.sem, 1)
                            else:
                                then(nc.vector.tensor_tensor(stn[:, :], head[:, 3, 0:2 * P], rblock[:, :], ALU.mult))
                                nc.vector.scalar_tensor_tensor(st[:, :], st[:, :], rcol[:, 2:3], stn[:, :], ALU.mult, ALU.add).then_inc(r_state.sem, 1)
                        dve.wait_ge(r_sq.sem, r_sq.at(b, t + 1))
                        nc.vector.tensor_reduce(oss[:, :], osq[:, :].rearrange("p (h d) -> p h d", d=RV), AX.X, ALU.add).then_inc(r_ms.sem, 1)
                        dve.wait_ge(r_rstd.sem, r_rstd.at(b, t + 1))
                        then(nc.vector.tensor_tensor(o1[:, :].rearrange("p (h d) -> p h d", d=RV), outs[:, 0:2 * P].rearrange("p (h d) -> p h d", d=RV),
                                                     orst[:, :].unsqueeze(2).to_broadcast([P, RH, RV]), ALU.mult))
                        then(nc.vector.tensor_tensor(o2[:, :], o1[:, :], gnw[:, :], ALU.mult))
                        dve.wait_ge(r_sg.sem, r_sg.at(b, t + 1))
                        nc.vector.tensor_tensor(o3[:, :], o2[:, :], sg[:, :], ALU.mult).then_inc(r_o.sem, 1)

                    dve.wait_ge(r_wo.sem, r_wo.at(b, 1))
                    then(nc.vector.tensor_tensor(sT[:, :], head[:, 0, :], xnT[:, :], ALU.add))
                    dve.wait_ge(s_gate.sem, s_gate.at(b, 1))
                    then(nc.vector.tensor_tensor(gT[:, :], sT[:, :], sgT[:, :], ALU.mult))
                    nc.vector.tensor_tensor(x1T[:, :], gT[:, :], x0T[:, :], ALU.add).then_inc(x1_there.sem, 1)
                    dve.wait_ge(x1_there.sem, x1_there.at(b, 1))
                    dve.wait_ge(m_mean.sem, m_mean.at(b, 1))
                    nc.vector.tensor_tensor(xc[:, :], x1T[:, :], head[:, 1, :], ALU.subtract).then_inc(m_xc.sem, 1)
                    dve.wait_ge(m_rstd.sem, m_rstd.at(b, 1))
                    nc.vector.tensor_tensor(xm[:, :], xc[:, :], rstd[:, :], ALU.mult).then_inc(xm_there.sem, 1)

                    dve.wait_ge(e_lg.sem, e_lg.at(b, 1))
                    then(nc.vector.tensor_copy(lg[:, :, :], head[:, 3, 0:NE * TILES].rearrange("p (t e) -> p t e", e=NE)))
                    mine = lg[:, :, :].unsqueeze(3).to_broadcast([P, TILES, NE, NE])
                    theirs = lg[:, :, :].unsqueeze(2).to_broadcast([P, TILES, NE, NE])
                    nc.vector.tensor_tensor(beats[:, :, :, :], theirs, mine, ALU.is_gt)
                    then(nc.vector.tensor_tensor(ties[:, :, :, :], theirs, mine, ALU.is_equal))
                    then(nc.vector.tensor_tensor(tied[:, :, :, :], ties[:, :, :, :], ebefore[:, :, :].unsqueeze(1).to_broadcast([P, TILES, NE, NE]), ALU.mult))
                    then(nc.vector.tensor_tensor(wins[:, :, :, :], beats[:, :, :, :], tied[:, :, :, :], ALU.add))
                    then(nc.vector.tensor_reduce(rank[:, :, :], wins[:, :, :, :], AX.X, ALU.add))
                    nc.vector.tensor_scalar(sel[:, :, :], rank[:, :, :], 2.0, None, ALU.is_lt)
                    then(nc.vector.tensor_reduce(gmx[:, :], lg[:, :, :], AX.X, ALU.max))
                    nc.vector.tensor_tensor(gsub[:, :, :], lg[:, :, :], gmx[:, :].unsqueeze(2).to_broadcast([P, TILES, NE]), ALU.subtract).then_inc(e_sub.sem, 1)
                    dve.wait_ge(e_exp.sem, e_exp.at(b, 1))
                    then(nc.vector.tensor_tensor(gsel[:, :, :], gex[:, :, :], sel[:, :, :], ALU.mult))
                    then(nc.vector.tensor_reduce(gden[:, :], gsel[:, :, :], AX.X, ALU.add))
                    then(nc.vector.reciprocal(grd[:, :], gden[:, :]))
                    nc.vector.tensor_tensor(gate[:, :, :], gsel[:, :, :], grd[:, :].unsqueeze(2).to_broadcast([P, TILES, NE]), ALU.mult).then_inc(e_gate.sem, 1)

                    for t in range(TILES):
                        dve.wait_ge(a_proj.sem, a_proj.at(b, t + 1))
                        if t > 0:
                            dve.wait_ge(a_turned.sem, a_turned.at(b, t))
                        of = proj[:, 0, 0:2 * P]
                        nc.vector.tensor_tensor(aq1[:, :], of, arot[:, 0, t, :], ALU.mult)
                        then(nc.vector.tensor_tensor(
                            aq2[:, :].rearrange("p (h s d) -> p h s d", s=2, d=64),
                            of.rearrange("p (h s d) -> p h s d", s=2, d=64)[:, :, ::-1, :],
                            arot[:, 1, t, :].rearrange("p (h s d) -> p h s d", s=2, d=64), ALU.mult))
                        nc.vector.tensor_tensor(aqk[:, :], aq1[:, :], aq2[:, :], ALU.add).then_inc(a_rot.sem, 1)
                    for t in range(TILES):
                        dve.wait_ge(a_sc.sem, a_sc.at(b, t + 1))
                        if t > 0:
                            dve.wait_ge(a_exp.sem, a_exp.at(b, t))
                        then(nc.vector.tensor_tensor(asc[:, :], head[:, 0, :], amask[:, t, :], ALU.add))
                        then(nc.vector.tensor_reduce(amx[:, :], asc[:, :], AX.X, ALU.max))
                        nc.vector.tensor_scalar(aneg[:, :], amx[:, :], -AK, None, ALU.mult).then_inc(a_max.sem, 1)
                        dve.wait_ge(a_exp.sem, a_exp.at(b, t + 1))
                        then(nc.vector.reciprocal(arden[:, :], aden[:, :]))
                        if t > 0:
                            dve.wait_ge(a_pturn.sem, a_pturn.at(b, t))
                        nc.vector.tensor_scalar(apr[:, :], aex[:, :], arden[:, 0:1], None, ALU.mult).then_inc(a_p.sem, 1)

                    for c in range(4):
                        dve.wait_ge(e_hid.sem, e_hid.at(b, c + 1))
                        dve.wait_ge(e_spread.sem, e_spread.at(b, c + 1))
                        nc.vector.tensor_tensor(hg[:, c, :], head[:, 2, :], hid[:, c, :], ALU.mult).then_inc(e_hg.sem, 1)
                    dve.wait_ge(e_silu.sem, e_silu.at(b, 1))
                    dve.wait_ge(s1_there.sem, s1_there.at(b, 1))
                    then(nc.vector.tensor_tensor(gT[:, :], s1T[:, :], moe[:, :], ALU.mult))
                    nc.vector.tensor_tensor(x2T[:, :], gT[:, :], x1T[:, :], ALU.add).then_inc(x2_there.sem, 1)
                    dve.wait_ge(x2_turn.sem, x2_turn.at(b, 1))
                    dve.wait_ge(stored.sem, stored.at(b, 0))
                    nc.vector.tensor_copy(xo[:, :, :], turn[:, :].rearrange("p (t d) -> p t d", d=P)).then_inc(xo_there.sem, 1)
                assert count[0] == STEPS, count[0]


def rotary_tables():
    f = np.float32
    half = np.arange(0, DH, 2, dtype=f)
    freqs = np.arange(T, dtype=f)[:, None] * (f(1.0) / f(10000.0) ** (half / f(DH)))[None, :]
    freqs = np.concatenate([freqs, freqs], -1)
    base = (half + f(0.4 * DH)) / f(1.4 * DH)
    power = (np.arange(T, dtype=f) - T // 2) / f(WIN // 2)
    scale = base[None, :] ** power[:, None]
    scale = np.concatenate([scale, scale], -1)
    sign = np.where(np.arange(DH) < DH // 2, -1.0, 1.0).astype(f)
    cos, sin = np.cos(freqs), np.sin(freqs) * sign
    out = np.stack([cos * scale, sin * scale, cos / scale, sin / scale])
    return np.ascontiguousarray(out.reshape(4, TILES, P, DH).transpose(2, 0, 1, 3), dtype=f)


def window_mask():
    query = (np.arange(P) % WIN)[:, None]
    key = np.arange(2 * WIN)[None, :]
    ok = (key >= query) & (key <= query + WIN)
    first = ok & ((np.arange(P)[:, None] >= WIN) | (key >= WIN))
    return np.where(np.stack([first, ok], 1), 0.0, MASKED).astype(np.float32)


def pack_layers(a):
    f = np.float32
    g = lambda n: np.asarray(a["L0_ffn_" + n])
    qkv = g("Wqkv")
    v = qkv[:, :, 2 * INNER:].reshape(DEPTH, P, PAIRS, 2, DH).transpose(0, 1, 3, 2, 4).reshape(DEPTH, P, INNER)
    w_qkv = np.concatenate([qkv[:, :, :2 * INNER], v], 2)
    w_o = g("Wo").reshape(DEPTH, PAIRS, P, P).transpose(0, 2, 1, 3).reshape(DEPTH, P, PAIRS * P)
    w_2 = np.zeros((DEPTH, 3 * P, P), f)
    w_2[:, :FF] = g("W2")
    w_2 = w_2.reshape(DEPTH, 3, P, P).transpose(0, 2, 1, 3).reshape(DEPTH, P, 3 * P)
    cols = np.zeros((DEPTH, 9, P), f)
    b1 = g("b1")
    for k in range(2):
        for c, m in enumerate(FCH):
            cols[:, 3 * k + c, :m] = b1[:, FF * k + P * c:FF * k + P * c + m]
    cols[:, 6], cols[:, 7], cols[:, 8] = g("ln_g"), g("ln_b"), g("b2")
    cols = cols.transpose(0, 2, 1)
    qs, ks = g("q_scale"), g("k_scale")
    swap = lambda s: np.concatenate([s[:, DH // 2:], s[:, :DH // 2]], 1)
    scales = np.stack([qs, swap(qs), ks, swap(ks)], 1)
    return {k: np.ascontiguousarray(v) for k, v in dict(
        w_qkv=w_qkv, w_o=w_o, w_1=g("W1"), w_2=w_2, cols=cols, qk_scale=scales).items()}


def mixer_tables():
    f = np.float32
    t = np.arange(T, dtype=f)
    tiles = lambda a: a.reshape(TILES, P, -1).transpose(1, 0, 2)

    def rope(theta, groups, scale):
        ang = t[:, None] * theta[None, :]
        c, s = np.cos(ang), np.sin(ang)
        both = [np.concatenate([c, c], 1), np.concatenate([-s, s], 1)]
        rows = [np.concatenate([np.tile(a, (1, groups)) * f(scale), np.tile(a, (1, groups))], 1) for a in both]
        return np.stack([tiles(a) for a in rows], 1).astype(f)

    gamma = f(1.0) - np.exp2(f(-5.0) - np.arange(RH, dtype=f))
    i = np.arange(P, dtype=f)
    wide = lambda a: np.repeat(a.T, RK, axis=1)
    gap = i[None, :] - i[:, None]
    diag = np.where(gap >= 0, gamma[:, None, None] ** np.maximum(gap, 0), 0.0).transpose(1, 0, 2)
    rows, cols = np.arange(P), np.arange(2 * P)
    return {k: np.ascontiguousarray(v, dtype=f) for k, v in dict(
        ret_rot=rope(f(1.0) / f(10000.0) ** (np.arange(0, RK, 2, dtype=f) / f(RK)), RH, RK ** -0.5),
        ret_decay=np.stack([wide(gamma[:, None] ** (i + 1)), wide(gamma[:, None] ** (P - 1 - i))], 1),
        ret_diag=diag,
        ret_block=(rows[:, None] // RK == cols[None, :] // RV),
        state_decay=np.repeat(gamma ** P, RK),
        att_rot=rope(f(10000.0) ** (f(-2.0) * np.arange(P // 2, dtype=f) / f(P)), 1, 1.0),
        att_mask=tiles(np.where(np.arange(T)[None, :] <= np.arange(T)[:, None] + 1, 0.0, MASKED)),
        expert_rows=np.arange(NE)[:, None, None] == (BN * 2 * np.arange(4)[:, None] + rows)[None] // BN,
        before=(np.arange(NE)[None, :] < np.arange(NE)[:, None]).reshape(1, NE * NE)).items()}


def pack_mixers(a):
    g = lambda n: np.asarray(a[n])
    r = lambda n: g("L0_attn_" + n)
    pairs = np.concatenate([np.arange(0, P, 2), np.arange(1, P, 2)])
    att = np.concatenate([g("L1_attn_Wq")[pairs].T, g("L1_attn_Wk")[pairs].T, g("L1_attn_Wv").T], 1)
    return {k: np.ascontiguousarray(v) for k, v in dict(
        w_ret=np.concatenate([r("Wq"), r("Wk"), r("Wv"), r("Wg")], 1),
        w_ro=r("Wo").reshape(2, P, P).transpose(1, 0, 2),
        g_norm=np.tile(r("g_norm_w"), RH)[None, :],
        w_att=att,
        w_gate=g("L1_ffn_w_gate"),
        w_down=g("L1_ffn_Wd").transpose(1, 0, 2).reshape(P, NE * BN),
        w_up=g("L1_ffn_Wu").reshape(4, P, P).transpose(1, 0, 2),
        b_down=g("L1_ffn_bd").reshape(4, P).T,
        b_up=g("L1_ffn_bu")).items()}


def build(nc, x, out, net, mix):
    with nc.sbuf_tensor("state", [P, B * SHIFTED], F32) as state:
        build_network(nc, x=x, state=state, **net)
        build_mixers(nc, state=state, x=x, out=out, **mix)


def kernel(**inputs):
    import concourse.bacc as bacc
    from concourse.bass_utils import run_bass_kernel_spmd

    net = dict(pack_layers(inputs), rotary=rotary_tables(), win_mask=window_mask())
    mix = dict(pack_mixers(inputs), **mixer_tables())
    mix["ret_cols"] = np.ascontiguousarray(np.stack(
        [np.asarray(inputs["L0_attn_ln_w"]), np.asarray(inputs["L0_attn_ln_b"]), mix.pop("state_decay")], 1))
    nc = bacc.Bacc("TRN2", target_bir_lowering=False, num_devices=1)
    arrays = {}

    def dram(name, a):
        arrays[f"in_{name}"] = a
        return nc.dram_tensor(f"in_{name}", a.shape, mybir.dt.from_np(a.dtype), kind="ExternalInput").ap()

    x = dram("x", np.ascontiguousarray(inputs["L0_attn_x"]))
    out = nc.dram_tensor("out_x", (B, T, P), F32, kind="ExternalOutput").ap()
    build(nc, x, out, {k: dram(k, v) for k, v in net.items()}, {k: dram(k, v) for k, v in mix.items()})
    r = run_bass_kernel_spmd(nc, [arrays], core_ids=[0])
    return r.results[0]["out_x"]
```

```python
from contextlib import ExitStack

import numpy as np

import concourse.bass as bass
from concourse import mybir

F32 = mybir.dt.float32
BF16 = mybir.dt.bfloat16
ALU = mybir.AluOpType
ACT = mybir.ActivationFunctionType
AX = mybir.AxisListType

P = 128
B, T = 4, 512
TILES = T // P
EPS = 1e-5
LN_EXP_SET = "natural_log_exp_and_others"
MASKED = -1e30

DEPTH = 6
HEADS, DH = 16, 64
PAIRS = HEADS // 2
INNER = HEADS * DH
WIN = 32
WINDOWS = T // WIN
TW = P // WIN
FF = int(P * 4 * 2 / 3)
FCH = [128, 128, FF - 256]
SHIFTED = T + 4
NORM_FLOOR = 1e-24
LN_SCALE = 2.0 ** 20


class Signal:

    def __init__(self, ctx, nc, name, per=1, start=0):
        self.sem, self.per, self.start = ctx.enter_context(nc.semaphore(name)), per, start

    def at(self, rnd, n):
        return rnd * self.per + n + self.start


def build_network(nc, w_qkv, w_o, w_1, w_2, cols, qk_scale, rotary, win_mask, state):
    ctx = ExitStack()
    with ctx:
        def sb(name, shape, dt=F32):
            return ctx.enter_context(nc.sbuf_tensor(name, shape, dt))

        def sig(name, per=1, start=0):
            return Signal(ctx, nc, name, per, start)

        qk_ps = ctx.enter_context(nc.psum_tensor("qk_ps", [P, 4, 512], F32))
        sc_ps = ctx.enter_context(nc.psum_tensor("sc_ps", [P, 2, 512], F32))
        ring = ctx.enter_context(nc.psum_tensor("ring", [P, 2, 512], F32))

        ident = sb("ident", [P, P])
        ident_bf = sb("ident_bf", [P, P], BF16)
        mean_w = sb("mean_w", [P, P])
        centre_w = sb("centre_w", [P, P])
        mask_f = sb("mask_f", [P, 2, 2 * WIN])
        mask_bf = sb("mask_bf", [P, 2, PAIRS, 2 * WIN], BF16)
        rot_base = sb("rot_base", [P, 4, TILES, DH])
        rot = sb("rot", [P, 4, TILES, DH])
        qks = sb("qks", [P, DEPTH * 4, DH])
        wqkv = sb("wqkv", [P, 3 * INNER])
        wo = sb("wo", [P, PAIRS, P])
        w1 = sb("w1", [P, 2 * FF])
        w2 = sb("w2", [P, 3, P])
        col = sb("col", [P, 9])
        xs = sb("xs", [P, T])
        xs2 = sb("xs2", [P, T])
        t1 = sb("t1", [P, 2 * INNER])
        t2 = sb("t2", [P, 2 * INNER])
        sq = sb("sq", [P, 2 * INNER])
        qkn = sb("qkn", [P, 2 * INNER])
        ss = sb("ss", [P, 2 * HEADS])
        rs = sb("rs", [P, 2 * HEADS])
        lnss = sb("lnss", [P, 2 * HEADS])
        nw1 = sb("nw1", [P, 2 * HEADS])
        nw2 = sb("nw2", [P, 2 * HEADS])
        rn = sb("rn", [P, 2 * HEADS])
        qT = sb("qT", [P, PAIRS, P])
        kT = sb("kT", [P, PAIRS, WIN + T])
        v_tok = sb("v_tok", [P, 2, 2, PAIRS * DH])
        v_win = sb("v_win", [P, WINDOWS, PAIRS * DH])
        smax = sb("smax", [P, HEADS])
        den = sb("den", [P, HEADS])
        rden = sb("rden", [P, HEADS])
        pr = sb("pr", [P, INNER])
        pe_ = sb("pexp", [P, INNER])
        prT = sb("prT", [P, PAIRS, P])
        o_tok = sb("o_tok", [P, INNER])
        oT = sb("oT", [P, PAIRS, T])
        xc = sb("xc", [P, T])
        xsq = sb("xsq", [P, T])
        lnv = sb("lnv", [P, T])
        xn = sb("xn", [P, T])
        gel = sb("gel", [P, 3, T])
        lnsum = sb("lnsum", [P, 2 * HEADS])
        eps_col = sb("eps_col", [P, 1])
        primer = sb("primer", [P, 5])

        s_const = sig("s_const")
        s_wqk = sig("s_wqk", 16)
        s_wv = sig("s_wv", 16)
        s_qks = sig("s_qks")
        s_wrest = sig("s_wrest", 64)
        v_moved = [sig(f"v_moved{t}", 16 * (16 - 2 * (t == TILES - 1))) for t in range(TILES)]
        c_ident = sig("c_ident")
        c_dve = sig("c_dve")
        rot_ready = sig("rot_ready", start=1)
        xs_ready = sig("xs_ready", 2)
        v_full = sig("v_full", 2 * TILES)
        v_copied = sig("v_copied", 2 * TILES)
        qk_full = sig("qk_full", 4 * TILES)
        q_sq = sig("q_sq", TILES)
        k_sq = sig("k_sq", TILES)
        qk_rot = sig("qk_rot", 4 * TILES, start=1)
        ss_sum = sig("ss_sum", 2 * TILES)
        ss_ready = sig("ss_ready", TILES)
        ss_ln = sig("ss_ln", TILES)
        rs_ready = sig("rs_ready", TILES)
        newton = sig("newton", 2 * TILES)
        rn_ready = sig("rn_ready", TILES)
        qk_added = sig("qk_added", 2 * TILES)
        qk_scaled = sig("qk_scaled", 2 * TILES)
        qkT_full = sig("qkT_full", 4 * TILES, start=1)
        qkT_copied = sig("qkT_copied", 4 * TILES)
        sc_full = sig("sc_full", TILES)
        max_ready = sig("max_ready", TILES)
        sc_sub = sig("sc_sub", 2 * TILES)
        exp_ready = sig("exp_ready", 2 * TILES)
        den_ready = sig("den_ready", TILES)
        rden_ready = sig("rden_ready", TILES)
        pT_full = sig("pT_full", 2 * TILES)
        pT_copied = sig("pT_copied", 2 * TILES)
        av_full = sig("av_full", TILES)
        o_ready = sig("o_ready", 2 * TILES)
        oT_full = sig("oT_full", 2 * TILES)
        oT_copied = sig("oT_copied", 2 * TILES)
        wo_full = sig("wo_full")
        x_attn = sig("x_attn")
        xs2_ready = sig("xs2_ready", 2)
        xc_full = sig("xc_full")
        xc_copied = sig("xc_copied")
        xsq_ready = sig("xsq_ready")
        var_full = sig("var_full")
        lnv_ready = sig("lnv_ready")
        rstd_ready = sig("rstd_ready")
        xh_ready = sig("xh_ready")
        xn_ready = sig("xn_ready", start=1)
        gate_full = sig("gate_full", 3)
        lin_full = sig("lin_full", 3)
        gelu_ready = sig("gelu_ready", 3)
        u_ready = sig("u_ready", 3)
        w2_full = sig("w2_full")
        x_ffn = sig("x_ffn", start=1)

        ROUNDS = DEPTH * B

        class Round:

            def __init__(self, it, now, before):
                self.it, self.now, self.before = it, now, before

            def has(self, s, lag):
                return self.now if s >= lag else self.before

            def tile(self, s, lag):
                return (self.it, s - lag) if s >= lag else (self.it - 1, s - lag + TILES)

        order = []
        for s in range(TILES):
            order += [("t", s, 1, f) for f in range(2)]
            order += [("wo", s, TILES, 0)] * (s == 2)
            order += [("p", s, 2, f) for f in range(2)]
            order += [("xc", s, TILES, 0)] * (s == 2)
            order += [("t", s, 1, f) for f in range(2, 4)]
            order += [(k, s, TILES, c) for c in (0, 1) for k in ("gate", "lin")] * (s == 3)
            order += [("var", s, TILES, 0)] * (s == 2)
            order += [("v", s, 0, 0)]
            order += [(k, s, TILES, 2) for k in ("gate", "lin")] * (s == 3)
            order += [("v", s, 0, 1)]
            order += [("w2", s, TILES, 0)] * (s == 3)
            order += [("o", s, 2, f) for f in range(2)]

        def fills(r):
            of = [f for f in order if r.has(f[1], f[2])]
            assert len(of) % 2 == 0
            return of

        def bank_of(r, fill):
            return ring[:, fills(r).index(fill) % 2, :]

        readers = dict(v=(v_copied, 2), t=(qkT_copied, 4), p=(pT_copied, 2), o=(oT_copied, 2), wo=(x_attn, 1), xc=(xc_copied, 1),
                       var=(lnv_ready, 1), gate=(gelu_ready, 3), lin=(u_ready, 3), w2=(x_ffn, 1))

        def bank_free(r, fill):
            of = fills(r)
            n = of.index(fill)
            it = r.it
            if n < 2:
                if not r.before:
                    return None
                it, of = r.it - 1, order
            what, s, lag, f = of[n - 2]
            signal, many = readers[what]
            if lag == TILES:
                return signal.sem, signal.at(it - 1, f + 1)
            rnd, t = (it, s - lag) if s >= lag else (it - 1, s - lag + TILES)
            return signal.sem, signal.at(rnd, many * t + f + 1)

        def state_cols(b, first, n):
            return bass.ds(b * SHIFTED + first, n)

        with nc.Block() as block:

            @block.sync
            def _(sp):
                for n, (to, of) in enumerate(((mask_f[:, :, :], win_mask), (rot_base[:, :, :, :], rotary))):
                    sp.dma_start(to, of).then_inc(s_const.sem, 16)

                def load_qk_weights(l):
                    sp.dma_start(wqkv[:, 0:2 * INNER], w_qkv[bass.ds(l, 1), :, 0:2 * INNER].rearrange("o p n -> p (o n)")).then_inc(s_wqk.sem, 16)

                def load_v_weights(l):
                    sp.dma_start(wqkv[:, 2 * INNER:], w_qkv[bass.ds(l, 1), :, 2 * INNER:].rearrange("o p n -> p (o n)")).then_inc(s_wv.sem, 16)

                def move_windows(it, t):
                    sp.wait_ge(v_copied.sem, v_copied.at(it, 2 * (t + 1)))
                    for q in range(TW):
                        w = TW * t + q
                        for par in range(2):
                            of = v_tok[WIN * q:WIN * (q + 1), t % 2, par, :]
                            sp.dma_start(v_win[64 * par + WIN:64 * par + 2 * WIN, w, :], of).then_inc(v_moved[t].sem, 16)
                            if w + 1 < WINDOWS:
                                sp.dma_start(v_win[64 * par:64 * par + WIN, w + 1, :], of).then_inc(v_moved[t].sem, 16)

                def layer(l, more):
                    for t in range(TILES):
                        move_windows(l * B, t)
                    sp.wait_ge(x_ffn.sem, x_ffn.at(l * B, 0))
                    sp.dma_start(wo[:, :, :], w_o[bass.ds(l, 1), :, :].rearrange("o p (c n) -> p (o c) n", n=P)).then_inc(s_wrest.sem, 16)
                    sp.dma_start(w1[:, :], w_1[bass.ds(l, 1), :, :].rearrange("o p n -> p (o n)")).then_inc(s_wrest.sem, 16)
                    sp.dma_start(w2[:, :, :], w_2[bass.ds(l, 1), :, :].rearrange("o p (c n) -> p (o c) n", n=P)).then_inc(s_wrest.sem, 16)
                    sp.dma_start(col[:, :], cols[bass.ds(l, 1), :, :].rearrange("o p n -> p (o n)")).then_inc(s_wrest.sem, 16)
                    with sp.Fori(1, B - 1) as b:
                        for t in range(TILES):
                            move_windows(l * B + b, t)
                    last = l * B + B - 1
                    for t in range(TILES):
                        if more and t == TILES - 1:
                            sp.wait_ge(qk_full.sem, qk_full.at(last, qk_full.per))
                            load_qk_weights(l + 1)
                        move_windows(last, t)
                    if more:
                        load_v_weights(l + 1)

                load_qk_weights(0)
                load_v_weights(0)
                sp.dma_start(qks[:, :, :].rearrange("p k d -> p (k d)"), qk_scale.to_broadcast([P, DEPTH * 4 * DH])).then_inc(s_qks.sem, 16)
                if DEPTH > 1:
                    with sp.Fori(0, DEPTH - 1) as l:
                        layer(l, True)
                layer(DEPTH - 1, False)

            @block.gpsimd
            def _(pool):
                nc.gpsimd.memset(ident[:, :], 0.0).then_inc(c_ident.sem, 1)
                pool.wait_ge(c_ident.sem, 1)
                nc.gpsimd.affine_select(out=ident[:, :], in_=ident[:, :], compare_op=ALU.not_equal, fill=1.0,
                                        base=0, pattern=[[-1, P]], channel_multiplier=1).then_inc(c_ident.sem, 1)
                pool.wait_ge(s_const.sem, 32)
                pool.wait_ge(s_qks.sem, 16)
                with pool.Fori(0, DEPTH) as l:
                    pool.wait_ge(qk_rot.sem, qk_rot.at(l * B, 0))
                    for k in range(4):
                        ins = nc.gpsimd.tensor_tensor(
                            rot[:, k, :, :], rot_base[:, k, :, :],
                            qks[:, bass.ds(l * 4 + k, 1), :].to_broadcast([P, TILES, DH]), ALU.mult)
                    ins.then_inc(rot_ready.sem, 1)
                    with pool.Fori(0, B) as b:
                        it = l * B + b
                        for t in range(TILES):
                            for half in range(2):
                                pool.wait_ge(qk_rot.sem, qk_rot.at(it, 4 * t + 2 * (half + 1)))
                                to = slice(INNER * half, INNER * (half + 1))
                                nc.gpsimd.tensor_tensor(t1[:, to], t1[:, to], t2[:, to], ALU.add).then_inc(qk_added.sem, 1)
                            pool.wait_ge(qk_added.sem, qk_added.at(it, 2 * (t + 1)))
                            pool.wait_ge(rn_ready.sem, rn_ready.at(it, t + 1))
                            pool.wait_ge(qkT_full.sem, qkT_full.at(it, 4 * t))
                            for half in range(2):
                                to = slice(INNER * half, INNER * (half + 1))
                                nc.gpsimd.tensor_tensor(
                                    qkn[:, to].rearrange("p (h d) -> p h d", d=DH), t1[:, to].rearrange("p (h d) -> p h d", d=DH),
                                    rn[:, HEADS * half:HEADS * (half + 1)].unsqueeze(2).to_broadcast([P, HEADS, DH]), ALU.mult).then_inc(qk_scaled.sem, 1)

            @block.tensor
            def _(pe):
                pe.wait_ge(c_ident.sem, 2)
                pe.wait_ge(c_dve.sem, 7)

                def ring_bank(r, what, s, lag, f):
                    fill = (what, s, lag, f)
                    before = bank_free(r, fill)
                    if before:
                        pe.wait_ge(before[0], before[1])
                    return bank_of(r, fill)

                def project_v(r, s, par):
                    if s == 0 and par == 0:
                        pe.wait_ge(s_wv.sem, s_wv.at(r.it >> 2, 16))
                    to = ring_bank(r, "v", s, 0, par)
                    nc.tensor.matmul(to, xs[:, s * P:(s + 1) * P], wqkv[:, 2 * INNER + 512 * par:2 * INNER + 512 * (par + 1)],
                                     start=True, stop=True).then_inc(v_full.sem, 1)

                def project_qk(r, s, c):
                    if c == 0:
                        if s == 0:
                            pe.wait_ge(s_wqk.sem, s_wqk.at(r.it >> 2, 16))
                            pe.wait_ge(xs_ready.sem, xs_ready.at(r.it, 2))
                        pe.wait_ge(q_sq.sem, q_sq.at(r.it, s))
                    if c == 2:
                        pe.wait_ge(qk_rot.sem, qk_rot.at(r.it, 4 * s))
                    nc.tensor.matmul(qk_ps[:, c, :], xs[:, s * P:(s + 1) * P], wqkv[:, 512 * c:512 * (c + 1)],
                                     start=True, stop=True).then_inc(qk_full.sem, 1)

                def transpose_qk(r, s, f):
                    it, t = r.tile(s, 1)
                    if f % 2 == 0:
                        pe.wait_ge(qk_scaled.sem, qk_scaled.at(it, 2 * t + f // 2 + 1))
                    to = ring_bank(r, "t", s, 1, f)
                    for n in range(4):
                        c = 4 * f + n
                        ins = nc.tensor.transpose(to[:, n * P:(n + 1) * P], qkn[:, c * P:(c + 1) * P], ident[:, :])
                    ins.then_inc(qkT_full.sem, 1)

                def scores(r, s, f):
                    it, t = r.tile(s, 1)
                    if f == 0:
                        pe.wait_ge(qkT_copied.sem, qkT_copied.at(it, 4 * (t + 1)))
                        pe.wait_ge(o_ready.sem, o_ready.at(it, 2 * t))
                        for par in range(2):
                            nc.tensor.matmul(sc_ps[:, par, :], ident_bf[:, :], mask_bf[:, int(t > 0), :, :],
                                             start=True, stop=False, skip_group_check=True)
                    for pair in range(4 * f, 4 * (f + 1)):
                        for q in range(TW):
                            for par in range(2):
                                ins = nc.tensor.matmul(
                                    sc_ps[WIN * q:WIN * (q + 1), par, 64 * pair:64 * (pair + 1)],
                                    qT[64 * par:64 * (par + 1), pair, WIN * q:WIN * (q + 1)],
                                    kT[64 * par:64 * (par + 1), pair, P * t + WIN * q:P * t + WIN * (q + 2)],
                                    start=False, stop=True, skip_group_check=True)
                    if f == 1:
                        ins.then_inc(sc_full.sem, 1)

                def transpose_p(r, s, f):
                    it, t = r.tile(s, 2)
                    pe.wait_ge(exp_ready.sem, exp_ready.at(it, 2 * t + f + 1))
                    to = ring_bank(r, "p", s, 2, f)
                    for n in range(4):
                        c = 4 * f + n
                        ins = nc.tensor.transpose(to[:, n * P:(n + 1) * P], pe_[:, c * P:(c + 1) * P], ident[:, :])
                    ins.then_inc(pT_full.sem, 1)

                def attend(r, s, f):
                    it, t = r.tile(s, 2)
                    if f == 0:
                        pe.wait_ge(pT_copied.sem, pT_copied.at(it, 2 * (t + 1)))
                        pe.wait_ge(v_moved[t].sem, v_moved[t].at(it, v_moved[t].per))
                        pe.wait_ge(sc_sub.sem, sc_sub.at(it, 2 * (t + 1)))
                        nc.tensor.matmul(sc_ps[:, 0, 0:DH], prT[0:64, 0, :], v_win[0:64, TW * t, 0:DH], start=True, stop=True)
                    for pair in range(4 * f, 4 * (f + 1)):
                        for q in range(TW):
                            for par in range(2):
                                ins = nc.tensor.matmul(
                                    sc_ps[WIN * q:WIN * (q + 1), par, DH * pair:DH * (pair + 1)],
                                    prT[64 * par:64 * (par + 1), pair, WIN * q:WIN * (q + 1)],
                                    v_win[64 * par:64 * (par + 1), TW * t + q, DH * pair:DH * (pair + 1)],
                                    start=True, stop=True)
                    if f == 1:
                        ins.then_inc(av_full.sem, 1)

                def transpose_o(r, s, f):
                    it, t = r.tile(s, 2)
                    pe.wait_ge(o_ready.sem, o_ready.at(it, 2 * t + f + 1))
                    to = ring_bank(r, "o", s, 2, f)
                    for n in range(4):
                        c = 4 * f + n
                        ins = nc.tensor.transpose(to[:, n * P:(n + 1) * P], o_tok[:, c * P:(c + 1) * P], ident[:, :])
                    ins.then_inc(oT_full.sem, 1)

                def output_projection(r):
                    pe.wait_ge(s_wrest.sem, s_wrest.at((r.it - 1) >> 2, 64))
                    pe.wait_ge(oT_copied.sem, oT_copied.at(r.it - 1, 2 * TILES))
                    to = ring_bank(r, "wo", 2, TILES, 0)
                    for c in range(PAIRS):
                        ins = nc.tensor.matmul(to, wo[:, c, :], oT[:, c, :], start=(c == 0), stop=(c == PAIRS - 1))
                    ins.then_inc(wo_full.sem, 1)

                def ffn_centre(r):
                    pe.wait_ge(xs2_ready.sem, xs2_ready.at(r.it - 1, 2))
                    nc.tensor.matmul(ring_bank(r, "xc", 2, TILES, 0), centre_w[:, :], xs2[:, :], start=True, stop=True).then_inc(xc_full.sem, 1)

                def ffn_variance(r):
                    pe.wait_ge(xsq_ready.sem, xsq_ready.at(r.it - 1, 1))
                    nc.tensor.matmul(ring_bank(r, "var", 2, TILES, 0), mean_w[:, :], xsq[:, :], start=True, stop=True).then_inc(var_full.sem, 1)

                def ffn_up(r, c):
                    m = FCH[c]
                    if c == 0:
                        pe.wait_ge(xn_ready.sem, xn_ready.at(r.it - 1, 1))
                    nc.tensor.matmul(ring_bank(r, "gate", 3, TILES, c)[0:m, :], w1[:, FF + P * c:FF + P * c + m], xn[:, :],
                                     start=True, stop=True).then_inc(gate_full.sem, 1)
                    nc.tensor.matmul(ring_bank(r, "lin", 3, TILES, c)[0:m, :], w1[:, P * c:P * c + m], xn[:, :],
                                     start=True, stop=True).then_inc(lin_full.sem, 1)

                def ffn_down(r):
                    pe.wait_ge(u_ready.sem, u_ready.at(r.it - 1, 3))
                    to = ring_bank(r, "w2", 3, TILES, 0)
                    for c, m in enumerate(FCH):
                        ins = nc.tensor.matmul(to, w2[0:m, c, :], gel[0:m, c, :], start=(c == 0), stop=(c == 2))
                    ins.then_inc(w2_full.sem, 1)

                def pe_round(r):
                    for s in range(TILES):
                        for f in range(2):
                            if r.now:
                                project_qk(r, s, f)
                            if r.has(s, 1):
                                transpose_qk(r, s, f)
                        if r.before and s == 2:
                            output_projection(r)
                        for f in range(2):
                            if r.has(s, 2):
                                transpose_p(r, s, f)
                            if r.now:
                                project_qk(r, s, 2 + f)
                        if r.before and s == 2:
                            ffn_centre(r)
                        if r.has(s, 1):
                            transpose_qk(r, s, 2)
                        if s == 3 and r.has(s, 1):
                            transpose_qk(r, s, 3)
                        if r.has(s, 2):
                            attend(r, s, 0)
                        if r.before and s == 3:
                            ffn_up(r, 0)
                        if s < 3 and r.has(s, 1):
                            transpose_qk(r, s, 3)
                        if r.before and s == 2:
                            ffn_variance(r)
                        if r.now and s == 2:
                            project_v(r, s, 0)
                        if r.has(s, 2):
                            attend(r, s, 1)
                        if r.before and s == 3:
                            ffn_up(r, 1)
                        if r.now and s != 2:
                            project_v(r, s, 0)
                        if r.before and s == 3:
                            ffn_up(r, 2)
                        if r.now:
                            project_v(r, s, 1)
                        if r.before and s == 3:
                            ffn_down(r)
                        for f in range(2):
                            if r.has(s, 1):
                                scores(r, s, f)
                            if r.has(s, 2):
                                transpose_o(r, s, f)

                pe_round(Round(0, True, False))
                with pe.Fori(1, ROUNDS) as it:
                    pe_round(Round(it, True, True))
                pe_round(Round(ROUNDS, False, True))

            @block.scalar
            def _(act):
                nc.scalar.preload_act_table_set(LN_EXP_SET)
                def copy_fill(r, to, what, s, lag, f, full, done, n):
                    it, t = r.tile(s, lag)
                    act.wait_ge(full.sem, full.at(it, n * t + f + 1))
                    nc.scalar.copy(to, bank_of(r, (what, s, lag, f))).then_inc(done.sem, 1)

                def squares(r, s, half, done):
                    act.wait_ge(ss_sum.sem, ss_sum.at(r.it, 2 * s))
                    if half == 0:
                        act.wait_ge(qk_rot.sem, qk_rot.at(r.it, 4 * s + 2))
                    else:
                        act.wait_ge(qk_full.sem, qk_full.at(r.it, 4 * (s + 1)))
                    nc.scalar.activation(sq[:, INNER * half:INNER * (half + 1)].rearrange("p (a n) -> p a n", a=2), qk_ps[:, 2 * half:2 * half + 2, :],
                                         ACT.Square).then_inc(done.sem, 1)

                def inverse_norms(r, s):
                    act.wait_ge(ss_ready.sem, ss_ready.at(r.it, s + 1))
                    nc.scalar.activation(lnss[:, :], ss[:, :], ACT.Ln, scale=LN_SCALE).then_inc(ss_ln.sem, 1)
                    act.wait_ge(ss_ln.sem, ss_ln.at(r.it, s + 1))
                    act.wait_ge(rn_ready.sem, rn_ready.at(r.it, s))
                    nc.scalar.activation(rs[:, :], lnss[:, :], ACT.Exp, scale=-0.5).then_inc(rs_ready.sem, 1)

                def centred(r):
                    act.wait_ge(xn_ready.sem, xn_ready.at(r.it - 1, 0))
                    act.wait_ge(xc_full.sem, xc_full.at(r.it - 1, 1))
                    nc.scalar.copy(xc[:, :], bank_of(r, ("xc", 2, TILES, 0))).then_inc(xc_copied.sem, 1)
                    act.wait_ge(xc_copied.sem, xc_copied.at(r.it - 1, 1))
                    nc.scalar.activation(xsq[:, :], xc[:, :], ACT.Square).then_inc(xsq_ready.sem, 1)

                def inverse_deviation(r):
                    act.wait_ge(var_full.sem, var_full.at(r.it - 1, 1))
                    nc.scalar.activation(lnv[:, :], bank_of(r, ("var", 2, TILES, 0)), ACT.Ln, bias=eps_col[:, 0:1]).then_inc(lnv_ready.sem, 1)
                    act.wait_ge(lnv_ready.sem, lnv_ready.at(r.it - 1, 1))
                    nc.scalar.activation(lnv[:, :], lnv[:, :], ACT.Exp, scale=-0.5).then_inc(rstd_ready.sem, 1)

                def gelu(r, c):
                    m = FCH[c]
                    act.wait_ge(gate_full.sem, gate_full.at(r.it - 1, c + 1))
                    nc.scalar.activation(gel[0:m, c, :], bank_of(r, ("gate", 3, TILES, c))[0:m, :], ACT.Gelu, bias=col[0:m, 3 + c:4 + c]).then_inc(gelu_ready.sem, 1)

                def exponentials(r, s):
                    it, t = r.tile(s, 2)
                    for f in range(2):
                        act.wait_ge(sc_sub.sem, sc_sub.at(it, 2 * t + f + 1))
                        if f == 0:
                            act.wait_ge(den_ready.sem, den_ready.at(it, t))
                        to = slice(512 * f, 512 * (f + 1))
                        nc.scalar.activation(pe_[:, to], pr[:, to], ACT.Exp, scale=8.0).then_inc(exp_ready.sem, 1)

                def copy_qkT(r, s, f):
                    t = r.tile(s, 1)[1]
                    if f < 2:
                        to = qT[:, 4 * f:4 * f + 4, :]
                    else:
                        to = kT[:, 4 * f - 8:4 * f - 4, WIN + P * t:WIN + P * (t + 1)]
                    copy_fill(r, to, "t", s, 1, f, qkT_full, qkT_copied, 4)

                def copy_v(r, s, par):
                    copy_fill(r, v_tok[:, s % 2, par, :], "v", s, 0, par, v_full, v_copied, 2)

                def act_round(r):
                    for s in range(TILES):
                        if r.has(s, 1):
                            copy_qkT(r, s, 0)
                        if r.has(s, 2):
                            exponentials(r, s)
                        if r.has(s, 1):
                            copy_qkT(r, s, 1)
                        for f in range(2):
                            if r.has(s, 2):
                                copy_fill(r, prT[:, 4 * f:4 * f + 4, :], "p", s, 2, f, pT_full, pT_copied, 2)
                        if r.before and s == 2:
                            centred(r)
                        if r.now:
                            squares(r, s, 1, k_sq)
                        if r.has(s, 1):
                            copy_qkT(r, s, 2)
                            copy_qkT(r, s, 3)
                        if r.now:
                            squares(r, s, 0, q_sq)
                        moved = v_moved[(s - 2) % TILES]
                        if r.before and s == 3:
                            gelu(r, 0)
                            gelu(r, 1)
                            if r.now:
                                act.wait_ge(moved.sem, moved.at(r.it, moved.per))
                                copy_v(r, s, 0)
                            gelu(r, 2)
                            if r.now:
                                copy_v(r, s, 1)
                            nc.scalar.preload_act_table_set(LN_EXP_SET)
                            if r.now:
                                inverse_norms(r, s)
                        else:
                            if r.before and s == 2:
                                inverse_deviation(r)
                            if r.now:
                                act.wait_ge(moved.sem, moved.at(r.it, moved.per if s >= 2 else 0))
                                copy_v(r, s, 0)
                                copy_v(r, s, 1)
                                inverse_norms(r, s)
                        if r.has(s, 2):
                            t = r.tile(s, 2)[1]
                            for f in range(2):
                                copy_fill(r, oT[:, 4 * f:4 * f + 4, P * t:P * (t + 1)], "o", s, 2, f, oT_full, oT_copied, 2)

                act_round(Round(0, True, False))
                with act.Fori(1, ROUNDS) as it:
                    act_round(Round(it, True, True))
                act_round(Round(ROUNDS, False, True))

            @block.vector
            def _(dve):
                def copy_at(to, of):
                    return nc.vector.tensor_scalar(to, of, 1.0, None, ALU.mult)

                nc.vector.memset(mean_w[:, :], 1.0 / P).then_inc(c_dve.sem, 1)
                nc.vector.memset(kT[:, :, 0:WIN], 0.0).then_inc(c_dve.sem, 1)
                nc.vector.memset(v_win[:, 0, :], 0.0).then_inc(c_dve.sem, 1)
                dve.wait_ge(s_const.sem, 32)
                nc.vector.tensor_copy(mask_bf[:, :, :, :], mask_f[:, :, :].unsqueeze(2).to_broadcast([P, 2, PAIRS, 2 * WIN])).then_inc(c_dve.sem, 1)
                dve.wait_ge(c_ident.sem, 2)
                nc.vector.tensor_copy(ident_bf[:, :], ident[:, :]).then_inc(c_dve.sem, 1)
                nc.vector.memset(eps_col[:, :], EPS).then_inc(c_dve.sem, 1)
                nc.vector.tensor_scalar(centre_w[:, :], ident[:, :], 1.0 / P, None, ALU.subtract).then_inc(c_dve.sem, 1)
                dve.wait_ge(c_dve.sem, 7)
                for n, raised in enumerate((rot_ready, x_ffn, xn_ready, qkT_full, qk_rot)):
                    nc.vector.memset(primer[:, n:n + 1], 0.0).then_inc(raised.sem, 1)

                def shift_tokens(to, b, done):
                    copy_at(to[0:64, :], state[0:64, state_cols(b, 1, T)]).then_inc(done.sem, 1)
                    copy_at(to[64:P, :], state[64:P, state_cols(b, 0, T)]).then_inc(done.sem, 1)

                def rotate(r, s, half):
                    if half == 0:
                        if s == 0:
                            dve.wait_ge(rot_ready.sem, rot_ready.at(r.it >> 2, 1))
                        dve.wait_ge(qk_scaled.sem, qk_scaled.at(r.it, 2 * s))
                        dve.wait_ge(qk_full.sem, qk_full.at(r.it, 4 * s + 2))
                    else:
                        dve.wait_ge(k_sq.sem, k_sq.at(r.it, s + 1))
                    of = qk_ps[:, 2 * half:2 * half + 2, :].rearrange("p a n -> p (a n)")
                    own = of.rearrange("p (h d) -> p h d", d=DH)
                    to = slice(INNER * half, INNER * (half + 1))
                    nc.vector.tensor_tensor(
                        t1[:, to].rearrange("p (h d) -> p h d", d=DH), own,
                        rot[:, 2 * half, s:s + 1, :].to_broadcast([P, HEADS, DH]), ALU.mult).then_inc(qk_rot.sem, 1)
                    swapped = of.rearrange("p (h s d) -> p h s d", s=2, d=DH // 2)[:, :, ::-1, :]
                    nc.vector.tensor_tensor(
                        t2[:, to].rearrange("p (h s d) -> p h s d", s=2, d=DH // 2), swapped,
                        rot[:, 2 * half + 1, s:s + 1, :].to_broadcast([P, HEADS, DH]).rearrange("p h (s d) -> p h s d", s=2),
                        ALU.mult).then_inc(qk_rot.sem, 1)

                def sum_squares(r, s, half):
                    done = (q_sq, k_sq)[half]
                    dve.wait_ge(done.sem, done.at(r.it, s + 1))
                    nc.vector.tensor_reduce(lnsum[:, HEADS * half:HEADS * (half + 1)], sq[:, INNER * half:INNER * (half + 1)].rearrange("p (h d) -> p h d", d=DH),
                                            AX.X, ALU.add).then_inc(ss_sum.sem, 1)
                    if half == 0:
                        dve.wait_ge(ss_sum.sem, ss_sum.at(r.it, 2 * (s + 1)))
                        nc.vector.tensor_scalar(ss[:, :], lnsum[:, :], NORM_FLOOR, None, ALU.max).then_inc(ss_ready.sem, 1)

                def newton_step(r, s):
                    dve.wait_ge(rs_ready.sem, rs_ready.at(r.it, s + 1))
                    dve.wait_ge(qk_scaled.sem, qk_scaled.at(r.it, 2 * s))
                    nc.vector.tensor_tensor(nw1[:, :], rs[:, :], rs[:, :], ALU.mult).then_inc(newton.sem, 1)
                    dve.wait_ge(newton.sem, newton.at(r.it, 2 * s + 1))
                    nc.vector.scalar_tensor_tensor(nw2[:, :], nw1[:, :], -0.5 * LN_SCALE * LN_SCALE ** 0.5, ss[:, :], ALU.mult, ALU.mult).then_inc(newton.sem, 1)
                    dve.wait_ge(newton.sem, newton.at(r.it, 2 * s + 2))
                    nc.vector.scalar_tensor_tensor(rn[:, :], nw2[:, :], 1.5 * LN_SCALE ** 0.5, rs[:, :], ALU.add, ALU.mult).then_inc(rn_ready.sem, 1)

                def row_max(r, s):
                    it, t = r.tile(s, 1)
                    dve.wait_ge(sc_full.sem, sc_full.at(it, t + 1))
                    nc.vector.tensor_reduce(smax[:, :], sc_ps[:, :, :].rearrange("p a n -> p (a n)").rearrange("p (h k) -> p h k", k=64), AX.X, ALU.max).then_inc(max_ready.sem, 1)
                    dve.wait_ge(max_ready.sem, max_ready.at(it, t + 1))
                    for f in range(2):
                        pairs = slice(4 * f, 4 * (f + 1))
                        nc.vector.tensor_tensor(
                            pr[:, :].rearrange("p (h a k) -> p a h k", a=2, k=64)[:, :, pairs, :],
                            sc_ps[:, :, :].rearrange("p a (h k) -> p a h k", k=64)[:, :, pairs, :],
                            smax[:, :].rearrange("p (a h) -> p a h", a=2)[:, :, pairs].unsqueeze(3).to_broadcast([P, 2, 4, 64]), ALU.subtract).then_inc(sc_sub.sem, 1)

                def row_sum(r, s):
                    it, t = r.tile(s, 2)
                    dve.wait_ge(exp_ready.sem, exp_ready.at(it, 2 * (t + 1)))
                    nc.vector.tensor_reduce(den[:, :], pe_[:, :].rearrange("p (h k) -> p h k", k=64), AX.X, ALU.add).then_inc(den_ready.sem, 1)
                    dve.wait_ge(den_ready.sem, den_ready.at(it, t + 1))
                    nc.vector.reciprocal(rden[:, :], den[:, :]).then_inc(rden_ready.sem, 1)

                def normalise(r, s):
                    it, t = r.tile(s, 2)
                    dve.wait_ge(rden_ready.sem, rden_ready.at(it, t + 1))
                    dve.wait_ge(oT_full.sem, oT_full.at(it, 2 * t))
                    dve.wait_ge(av_full.sem, av_full.at(it, t + 1))
                    for f in range(2):
                        pairs = slice(4 * f, 4 * (f + 1))
                        nc.vector.tensor_tensor(
                            o_tok[:, :].rearrange("p (h a d) -> p a h d", a=2, d=DH)[:, :, pairs, :],
                            sc_ps[:, :, :].rearrange("p a (h d) -> p a h d", d=DH)[:, :, pairs, :],
                            rden[:, :].rearrange("p (h a) -> p a h", a=2)[:, :, pairs].unsqueeze(3).to_broadcast([P, 2, 4, DH]), ALU.mult).then_inc(o_ready.sem, 1)

                def add_attention(r):
                    dve.wait_ge(x_ffn.sem, x_ffn.at(r.it - 1, 0))
                    dve.wait_ge(wo_full.sem, wo_full.at(r.it - 1, 1))
                    now = state[:, state_cols((r.it + 3) & 3, 1, T)]
                    nc.vector.tensor_tensor(now, bank_of(r, ("wo", 2, TILES, 0)), now, ALU.add).then_inc(x_attn.sem, 1)
                    dve.wait_ge(x_attn.sem, x_attn.at(r.it - 1, 1))
                    shift_tokens(xs2, (r.it + 3) & 3, xs2_ready)

                def ffn_norm(r):
                    dve.wait_ge(rstd_ready.sem, rstd_ready.at(r.it - 1, 1))
                    nc.vector.tensor_tensor(xc[:, :], xc[:, :], lnv[:, :], ALU.mult).then_inc(xh_ready.sem, 1)
                    dve.wait_ge(xh_ready.sem, xh_ready.at(r.it - 1, 1))
                    nc.vector.tensor_scalar(xn[:, :], xc[:, :], col[:, 6:7], col[:, 7:8], ALU.mult, ALU.add).then_inc(xn_ready.sem, 1)

                def ffn_gated(r, c):
                    m = FCH[c]
                    dve.wait_ge(gelu_ready.sem, gelu_ready.at(r.it - 1, c + 1))
                    dve.wait_ge(lin_full.sem, lin_full.at(r.it - 1, c + 1))
                    nc.vector.scalar_tensor_tensor(gel[0:m, c, :], bank_of(r, ("lin", 3, TILES, c))[0:m, :], col[0:m, c:c + 1], gel[0:m, c, :],
                                                   ALU.add, ALU.mult).then_inc(u_ready.sem, 1)

                def add_ffn(r):
                    dve.wait_ge(w2_full.sem, w2_full.at(r.it - 1, 1))
                    now = state[:, state_cols((r.it + 3) & 3, 1, T)]
                    nc.vector.scalar_tensor_tensor(now, bank_of(r, ("w2", 3, TILES, 0)), col[:, 8:9], now, ALU.add, ALU.add).then_inc(x_ffn.sem, 1)

                def dve_round(r):
                    for s in range(TILES):
                        if r.now:
                            rotate(r, s, 0)
                        if r.has(s, 2):
                            row_sum(r, s)
                        if r.before and s == 2:
                            add_attention(r)
                        if r.now:
                            rotate(r, s, 1)
                            sum_squares(r, s, 1)
                        if r.before and s == 3:
                            ffn_gated(r, 0)
                        if r.has(s, 2):
                            normalise(r, s)
                        if r.before and s == 3:
                            ffn_gated(r, 1)
                            ffn_gated(r, 2)
                        if r.now:
                            sum_squares(r, s, 0)
                            newton_step(r, s)
                        if r.before and s == 2:
                            ffn_norm(r)
                        if r.before and s == 3:
                            add_ffn(r)
                        if r.now and s == 3:
                            dve.wait_ge(v_full.sem, v_full.at(r.it, v_full.per))
                            dve.wait_ge(x_ffn.sem, x_ffn.at(r.it, 0))
                            shift_tokens(xs, (r.it + 1) & 3, xs_ready)
                        if r.has(s, 1):
                            row_max(r, s)

                shift_tokens(xs, 0, xs_ready)
                dve_round(Round(0, True, False))
                with dve.Fori(1, ROUNDS) as it:
                    dve_round(Round(it, True, True))
                dve_round(Round(ROUNDS, False, True))



RH, RK, RV = 4, 32, 64
BT = B * TILES


def build_retention(nc, state, x0T, sT, x, w_ret, w_ro, ret_cols, g_norm, ret_rot, ret_decay, ret_diag, ret_block):
    ctx = ExitStack()
    with ctx:
        def sb(name, shape, dt=F32):
            return ctx.enter_context(nc.sbuf_tensor(name, shape, dt))

        def sig(name, per=1, start=0):
            return Signal(ctx, nc, name, per, start)

        pa = ctx.enter_context(nc.psum_tensor("pa", [P, 2, 512], F32))
        pb = ctx.enter_context(nc.psum_tensor("pb", [P, 2, 512], F32))
        pc = ctx.enter_context(nc.psum_tensor("pc", [P, 2, 512], F32))
        pd = ctx.enter_context(nc.psum_tensor("pd", [P, 2, 512], F32))

        ident = sb("r_ident", [P, P])
        eps_col = sb("r_eps_col", [P, 1])
        primer = sb("r_primer", [P, 2])
        wr = sb("wr", [P, 6 * P])
        wro = sb("wro", [P, 2, P])
        rcol = sb("rcol", [P, 3])
        gnw = sb("gnw", [P, 2 * P])
        rrot = sb("rrot", [P, 2, TILES, RK])
        rdec = sb("rdec", [P, 2, P])
        rdiag = sb("rdiag", [P, RH, P])
        rblock = sb("rblock", [P, 2 * P])
        xtok = sb("r_xtok", [P, BT, P])
        xc = sb("r_xc", [P, BT, P])
        sqs = sb("r_sqs", [P, BT, P])
        xn = sb("r_xn", [P, BT, P])
        nr = sb("r_nr", [P, BT, P])
        msum = sb("r_msum", [P, BT])
        mean = sb("r_mean", [P, BT])
        vsum = sb("r_vsum", [P, BT])
        var = sb("r_var", [P, BT])
        lnv = sb("r_lnv", [P, BT])
        rstd = sb("r_rstd", [P, BT])
        nrT = sb("nrT", [P, B, T])
        nrc = sb("nrc", [P, B, P])
        rt1 = sb("rt1", [P, B, 2 * P])
        rt2 = sb("rt2", [P, B, 2 * P])
        rqk = sb("rqk", [P, B, 2 * P])
        qcr = sb("qcr", [P, B, P])
        kst = sb("kst", [P, B, P])
        vsb = sb("vsb", [P, B, 2 * P])
        sg = sb("sg", [P, B, 2 * P])
        sgn = sb("sgn", [P, B, 2 * P])
        rT = sb("rT", [P, 3, B, P])
        at = sb("at", [P, RH, B, P])
        st = sb("st", [P, B, 2 * P])
        stn = sb("stn", [P, B, 2 * P])
        osq = sb("osq", [P, B, 2 * P])
        oss = sb("oss", [P, B * RH])
        oln = sb("oln", [P, B * RH])
        orst = sb("orst", [P, B * RH])
        o1 = sb("o1", [P, B, 2 * P])
        o2 = sb("o2", [P, B, 2 * P])
        orT = sb("orT", [P, 2, B, P])

        loads = [(wr[:, :], w_ret), (wro[:, :, :], w_ro), (rcol[:, :], ret_cols), (rrot[:, :, :, :], ret_rot),
                 (rdec[:, :, :], ret_decay), (rdiag[:, :, :], ret_diag), (rblock[:, :], ret_block)]
        all_loads = 16 * (len(loads) + 1)
        c_loads = sig("r_loads")
        r_ident = sig("r_identity")
        c_set = sig("r_set")
        x_in = [sig("r_x_in_0"), sig("r_x_in_1")]
        steps = sig("r_steps")
        centred = sig("r_centred", 2)
        squared = sig("r_squared", 2)
        stats = sig("r_stats", 2)
        ln_there = sig("r_ln_there", 2)
        rstd_there = sig("r_rstd_there", 2)
        normed = sig("r_normed", 2)
        turned = sig("r_turned_all", 2)
        copied = sig("r_copied_all", 2)
        r_in = sig("r_in")
        r_qk = sig("r_qk")
        r_v = sig("r_v")
        r_g = sig("r_g")
        r_term = sig("r_term")
        r_rot = sig("r_rot")
        r_qcr = sig("r_qcr")
        r_kst = sig("r_kst")
        r_vsb = sig("r_vsb")
        r_sg = sig("r_sg")
        r_sgn = sig("r_sgn")
        r_turned = sig("r_turned", 3)
        r_T = sig("r_T", 3)
        r_sc = sig("r_sc", 2)
        r_at = sig("r_at", 2)
        r_out = sig("r_out")
        r_upd = sig("r_upd")
        r_stn = sig("r_stn")
        r_state = sig("r_state", start=1)
        r_sq = sig("r_sq")
        r_ms = sig("r_ms")
        r_oln = sig("r_oln")
        r_orst = sig("r_orst")
        r_o1 = sig("r_o1")
        r_o = sig("r_o", start=1)
        r_oturn = sig("r_oturn", 2)
        r_oT = sig("r_oT", 2)
        r_wo = sig("r_wo")
        s_there = sig("r_s_there", start=1)

        of_half = lambda half: slice(BT // 2 * half, BT // 2 * (half + 1))
        whole = lambda a: a[:, :, :].rearrange("p a n -> p (a n)")

        with nc.Block() as block:

            @block.sync
            def _(sp):
                for b in range(B):
                    sp.dma_start(xtok[:, TILES * b:TILES * (b + 1), :], x[b, :, :].rearrange("(t p) d -> p t d", p=P)).then_inc(x_in[b // 2].sem, 16)
                for to, of in loads:
                    sp.dma_start(to, of).then_inc(c_loads.sem, 16)
                sp.dma_start(gnw[:, :], g_norm.to_broadcast([P, 2 * P])).then_inc(c_loads.sem, 16)

            @block.gpsimd
            def _(pool):
                nc.gpsimd.memset(ident[:, :], 0.0).then_inc(r_ident.sem, 1)
                pool.wait_ge(r_ident.sem, 1)
                nc.gpsimd.affine_select(out=ident[:, :], in_=ident[:, :], compare_op=ALU.not_equal, fill=1.0,
                                        base=0, pattern=[[-1, P]], channel_multiplier=1).then_inc(r_ident.sem, 1)
                pool.wait_ge(c_loads.sem, all_loads)

                def weigh(t):
                    pool.wait_ge(r_rot.sem, r_rot.at(t, 1))
                    pool.wait_ge(r_upd.sem, r_upd.at(t, 0))
                    nc.gpsimd.tensor_tensor(kst[:, :, :], rqk[:, :, P:2 * P], rdec[:, 1:2, :].to_broadcast([P, B, P]), ALU.mult).then_inc(r_kst.sem, 1)
                    pool.wait_ge(r_sg.sem, r_sg.at(t, 1))
                    pool.wait_ge(r_o.sem, r_o.at(t, 0))
                    nc.gpsimd.tensor_tensor(sgn[:, :, :], sg[:, :, :], gnw[:, :].unsqueeze(1).to_broadcast([P, B, 2 * P]), ALU.mult).then_inc(r_sgn.sem, 1)

                weigh(0)
                with pool.Fori(1, TILES) as t:
                    weigh(t)

            @block.tensor
            def _(pe):
                def turn(to, of, b):
                    return nc.tensor.transpose(to[:, b // 4 % 2, P * (b % 4):P * (b % 4 + 1)], of, ident[:, :])

                pe.wait_ge(r_ident.sem, 2)
                for n, (of, to) in enumerate(((xtok, (pa, pb)), (xn, (pc, pd)), (nr, (pa, pb)))):
                    for half in range(2):
                        if n == 0:
                            pe.wait_ge(x_in[half].sem, 16 * B // 2)
                        else:
                            pe.wait_ge(normed.sem, normed.at(n - 1, half + 1))
                        if n == 2:
                            pe.wait_ge(copied.sem, copied.at(0, half + 1))
                        for i in range(BT // 2 * half, BT // 2 * (half + 1)):
                            ins = turn(to[half], of[:, i, :], i)
                        ins.then_inc(turned.sem, 1)
                pe.wait_ge(copied.sem, copied.at(2, 2))
                pe.wait_ge(c_loads.sem, all_loads)

                def project(t):
                    pe.wait_ge(r_in.sem, r_in.at(t, 1))
                    pe.wait_ge(r_at.sem, r_at.at(t, 0))
                    for k, (bank, done) in enumerate(((pa, r_qk), (pc, r_g), (pb, r_v))):
                        if k == 2:
                            pe.wait_ge(r_stn.sem, r_stn.at(t, 0))
                        weights = wr[:, (0, 512, 256)[k]:(0, 512, 256)[k] + 256]
                        for b in range(B):
                            ins = nc.tensor.matmul(bank[:, b // 2, 256 * (b % 2):256 * (b % 2 + 1)], nrc[:, b, :], weights, start=True, stop=True)
                        ins.then_inc(done.sem, 1)

                def retain(t, more):
                    pe.wait_ge(r_rot.sem, r_rot.at(t, 1))
                    pe.wait_ge(s_there.sem, s_there.at(t, 0))
                    for b in range(B):
                        ins = nc.tensor.transpose(pd[:, 0, P * b:P * (b + 1)], rqk[:, b, 0:P], ident[:, :])
                    ins.then_inc(r_turned.sem, 1)
                    for b in range(B):
                        ins = nc.tensor.transpose(pd[:, 1, P * b:P * (b + 1)], rqk[:, b, P:2 * P], ident[:, :])
                    ins.then_inc(r_turned.sem, 1)
                    pe.wait_ge(r_qcr.sem, r_qcr.at(t, 1))
                    pe.wait_ge(r_vsb.sem, r_vsb.at(t, 1))
                    for b in range(B):
                        ins = nc.tensor.transpose(pb[:, 0, P * b:P * (b + 1)], qcr[:, b, :], ident[:, :])
                    ins.then_inc(r_turned.sem, 1)
                    pe.wait_ge(r_kst.sem, r_kst.at(t, 1))
                    upd = lambda b: nc.tensor.matmul(pb[:, 1 - b // 2, 256 * (b % 2):256 * (b % 2 + 1)], kst[:, b, :], vsb[:, b, :], start=True, stop=True)
                    upd(0)
                    upd(1)
                    pe.wait_ge(r_T.sem, r_T.at(t, 2))
                    pe.wait_ge(r_sg.sem, r_sg.at(t, 1))
                    for h in range(RH):
                        rows = slice(RK * h, RK * (h + 1))
                        for b in range(B):
                            ins = nc.tensor.matmul((pa, pc)[h // 2][:, h % 2, P * b:P * (b + 1)], rT[rows, 1, b, :], rT[rows, 0, b, :], start=True, stop=True)
                        if h % 2 == 1:
                            ins.then_inc(r_sc.sem, 1)
                    pe.wait_ge(r_T.sem, r_T.at(t, 3))
                    upd(2)
                    upd(3).then_inc(r_upd.sem, 1)
                    pe.wait_ge(r_state.sem, r_state.at(t, 0))
                    for b in range(B):
                        nc.tensor.matmul(pd[:, b // 2, 256 * (b % 2):256 * (b % 2 + 1)], rT[:, 2, b, :], st[:, b, :],
                                         start=(b % 2 == 0), stop=False, skip_group_check=True)
                    for h in range(RH):
                        pe.wait_ge(r_at.sem, r_at.at(t, h // 2 + 1))
                        for b in range(B):
                            first = 256 * (b % 2) + RV * h
                            ins = nc.tensor.matmul(pd[:, b // 2, first:first + RV], at[:, h, b, :], vsb[:, b, RV * h:RV * (h + 1)],
                                                   start=False, stop=(b % 2 == 1 and h == RH - 1), skip_group_check=True)
                    ins.then_inc(r_out.sem, 1)
                    if more:
                        project(t + 1)
                    pe.wait_ge(r_o.sem, r_o.at(t, 1))
                    for n in range(2):
                        for b in range(B):
                            ins = nc.tensor.transpose(pd[:, n, P * b:P * (b + 1)], o2[:, b, P * n:P * (n + 1)], ident[:, :])
                        ins.then_inc(r_oturn.sem, 1)
                    pe.wait_ge(r_oT.sem, r_oT.at(t, 2))
                    for n in range(2):
                        ins = nc.tensor.matmul(pd[:, 0, :], wro[:, n, :], orT[:, n, :, :].rearrange("p b n -> p (b n)"), start=(n == 0), stop=(n == 1))
                    ins.then_inc(r_wo.sem, 1)

                project(0)
                with pe.Fori(0, TILES - 1) as t:
                    retain(t, True)
                retain(TILES - 1, False)

            @block.scalar
            def _(act):
                nc.scalar.preload_act_table_set(LN_EXP_SET)
                for half, bank in enumerate((pa, pb)):
                    act.wait_ge(turned.sem, turned.at(0, half + 1))
                    nc.scalar.copy(x0T[:, 1024 * half:1024 * (half + 1)], bank[:, :, :].rearrange("p a n -> p (a n)")).then_inc(copied.sem, 1)
                for n in range(2):
                    for half in range(2):
                        act.wait_ge(centred.sem, centred.at(n, half + 1))
                        nc.scalar.activation(sqs[:, of_half(half), :], xc[:, of_half(half), :], ACT.Square).then_inc(squared.sem, 1)
                    for half in range(2):
                        act.wait_ge(stats.sem, stats.at(n, half + 1))
                        nc.scalar.activation(lnv[:, of_half(half)], var[:, of_half(half)], ACT.Ln).then_inc(ln_there.sem, 1)
                        act.wait_ge(ln_there.sem, ln_there.at(n, half + 1))
                        nc.scalar.activation(rstd[:, of_half(half)], lnv[:, of_half(half)], ACT.Exp, scale=-0.5).then_inc(rstd_there.sem, 1)
                for n, banks in ((1, (pc, pd)), (2, (pa, pb))):
                    for half in range(2):
                        act.wait_ge(turned.sem, turned.at(n, half + 1))
                        for b in range(2 * half, 2 * half + 2):
                            to = state[:, b * SHIFTED + 1:b * SHIFTED + 1 + T] if n == 1 else nrT[:, b, :]
                            ins = nc.scalar.copy(to, banks[half][:, b % 2, :])
                        ins.then_inc(copied.sem, 1)
                act.wait_ge(c_loads.sem, all_loads)

                def take(t):
                    act.wait_ge(r_g.sem, r_g.at(t, 1))
                    act.wait_ge(r_sgn.sem, r_sgn.at(t, 0))
                    nc.scalar.activation(whole(sg), pc[:, :, :].rearrange("p a n -> p (a n)"), ACT.Silu).then_inc(r_sg.sem, 1)
                    act.wait_ge(r_v.sem, r_v.at(t, 1))
                    nc.scalar.copy(whole(vsb), pb[:, :, :].rearrange("p a n -> p (a n)")).then_inc(r_vsb.sem, 1)

                def finish(t, more):
                    for n, bank in enumerate((pd[:, 0, :], pd[:, 1, :], pb[:, 0, :])):
                        act.wait_ge(r_turned.sem, r_turned.at(t, n + 1))
                        nc.scalar.copy(rT[:, n, :, :].rearrange("p b n -> p (b n)"), bank).then_inc(r_T.sem, 1)
                    nc.scalar.preload_act_table_set(LN_EXP_SET)
                    act.wait_ge(r_out.sem, r_out.at(t, 1))
                    nc.scalar.activation(whole(osq), pd[:, :, :].rearrange("p a n -> p (a n)"), ACT.Square).then_inc(r_sq.sem, 1)
                    act.wait_ge(r_ms.sem, r_ms.at(t, 1))
                    nc.scalar.activation(oln[:, :], oss[:, :], ACT.Ln, bias=eps_col[:, 0:1], scale=1.0 / RV).then_inc(r_oln.sem, 1)
                    act.wait_ge(r_oln.sem, r_oln.at(t, 1))
                    nc.scalar.activation(orst[:, :], oln[:, :], ACT.Exp, scale=-0.5).then_inc(r_orst.sem, 1)
                    if more:
                        take(t + 1)
                    for n in range(2):
                        act.wait_ge(r_oturn.sem, r_oturn.at(t, n + 1))
                        nc.scalar.copy(orT[:, n, :, :].rearrange("p b n -> p (b n)"), pd[:, n, :]).then_inc(r_oT.sem, 1)

                take(0)
                with act.Fori(0, TILES - 1) as t:
                    finish(t, True)
                finish(TILES - 1, False)

            @block.vector
            def _(dve):
                count = [0]

                def then(ins):
                    count[0] += 1
                    ins.then_inc(steps.sem, 1)
                    dve.wait_ge(steps.sem, count[0])

                nc.vector.memset(eps_col[:, :], EPS).then_inc(c_set.sem, 1)
                nc.vector.memset(whole(st), 0.0).then_inc(r_state.sem, 1)
                nc.vector.memset(primer[:, 0:1], 0.0).then_inc(r_o.sem, 1)
                nc.vector.memset(primer[:, 1:2], 0.0).then_inc(s_there.sem, 1)
                for b in range(B):
                    nc.vector.memset(state[:, b * SHIFTED:b * SHIFTED + 1], 0.0).then_inc(c_set.sem, 1)
                dve.wait_ge(c_set.sem, 1 + B)
                per_token = lambda a, half: a[:, of_half(half)].unsqueeze(2).to_broadcast([P, BT // 2, P])
                for n, (of, to) in enumerate(((xtok, xn), (xn, nr))):
                    for half in range(2):
                        if n == 0:
                            dve.wait_ge(x_in[half].sem, 16 * B // 2)
                        else:
                            dve.wait_ge(normed.sem, normed.at(0, half + 1))
                        then(nc.vector.tensor_reduce(msum[:, of_half(half)], of[:, of_half(half), :], AX.X, ALU.add))
                        then(nc.vector.tensor_scalar(mean[:, of_half(half)], msum[:, of_half(half)], 1.0 / P, None, ALU.mult))
                        nc.vector.tensor_tensor(xc[:, of_half(half), :], of[:, of_half(half), :], per_token(mean, half), ALU.subtract).then_inc(centred.sem, 1)
                    for half in range(2):
                        dve.wait_ge(squared.sem, squared.at(n, half + 1))
                        then(nc.vector.tensor_reduce(vsum[:, of_half(half)], sqs[:, of_half(half), :], AX.X, ALU.add))
                        nc.vector.tensor_scalar(var[:, of_half(half)], vsum[:, of_half(half)], 1.0 / P, EPS, ALU.mult, ALU.add).then_inc(stats.sem, 1)
                    for half in range(2):
                        dve.wait_ge(rstd_there.sem, rstd_there.at(n, half + 1))
                        nc.vector.tensor_tensor(to[:, of_half(half), :], xc[:, of_half(half), :], per_token(rstd, half), ALU.mult).then_inc(normed.sem, 1)
                dve.wait_ge(copied.sem, copied.at(2, 2))
                dve.wait_ge(c_loads.sem, all_loads)

                def gather(t):
                    dve.wait_ge(r_v.sem, r_v.at(t, 0))
                    nc.vector.tensor_scalar(nrc[:, :, :], nrT[:, :, bass.ds(t * P, P)], rcol[:, 0:1], rcol[:, 1:2], ALU.mult, ALU.add).then_inc(r_in.sem, 1)

                def rotate(t):
                    dve.wait_ge(r_qk.sem, r_qk.at(t, 1))
                    dve.wait_ge(r_turned.sem, r_turned.at(t, 0))
                    dve.wait_ge(r_kst.sem, r_kst.at(t, 0))
                    of = pa[:, :, :].rearrange("p a (c n) -> p (a c) n", c=2)
                    heads = lambda a: a.rearrange("p b (h s d) -> p (b h) s d", s=2, d=RK // 2)
                    table = lambda k: rrot[:, k, bass.ds(t, 1), :].to_broadcast([P, B * 2 * RH, RK]).rearrange("p h (s d) -> p h s d", s=2)
                    nc.vector.tensor_tensor(heads(rt1[:, :, :]), heads(of), table(0), ALU.mult)
                    nc.vector.tensor_tensor(heads(rt2[:, :, :]), heads(of)[:, :, ::-1, :], table(1), ALU.mult).then_inc(r_term.sem, 1)
                    dve.wait_ge(r_term.sem, r_term.at(t, 1))
                    nc.vector.tensor_tensor(rqk[:, :, :], rt1[:, :, :], rt2[:, :, :], ALU.add).then_inc(r_rot.sem, 1)
                    dve.wait_ge(r_rot.sem, r_rot.at(t, 1))
                    nc.vector.tensor_tensor(qcr[:, :, :], rqk[:, :, 0:P], rdec[:, 0:1, :].to_broadcast([P, B, P]), ALU.mult).then_inc(r_qcr.sem, 1)

                def retain(t, more):
                    for k, bank in enumerate((pa, pc)):
                        dve.wait_ge(r_sc.sem, r_sc.at(t, k + 1))
                        nc.vector.tensor_tensor(at[:, 2 * k:2 * k + 2, :, :], bank[:, :, :].rearrange("p a (b n) -> p a b n", n=P),
                                                rdiag[:, 2 * k:2 * k + 2, :].unsqueeze(2).to_broadcast([P, 2, B, P]), ALU.mult).then_inc(r_at.sem, 1)
                    if more:
                        gather(t + 1)
                    dve.wait_ge(r_upd.sem, r_upd.at(t, 1))
                    nc.vector.tensor_tensor(stn[:, :, :].rearrange("p (a c) n -> p a c n", c=2)[:, ::-1, :, :], pb[:, :, :].rearrange("p a (c n) -> p a c n", c=2),
                                            rblock[:, :].unsqueeze(1).unsqueeze(1).to_broadcast([P, 2, 2, 2 * P]), ALU.mult).then_inc(r_stn.sem, 1)
                    dve.wait_ge(r_sq.sem, r_sq.at(t, 1))
                    nc.vector.tensor_reduce(oss[:, :], osq[:, :, :].rearrange("p b (h d) -> p (b h) d", d=RV), AX.X, ALU.add).then_inc(r_ms.sem, 1)
                    dve.wait_ge(r_stn.sem, r_stn.at(t, 1))
                    nc.vector.scalar_tensor_tensor(st[:, :, :], st[:, :, :], rcol[:, 2:3], stn[:, :, :], ALU.mult, ALU.add).then_inc(r_state.sem, 1)
                    dve.wait_ge(r_orst.sem, r_orst.at(t, 1))
                    nc.vector.tensor_tensor(o1[:, :, :].rearrange("p b (h d) -> p (b h) d", d=RV), pd[:, :, :].rearrange("p a (h d) -> p (a h) d", d=RV),
                                            orst[:, :].unsqueeze(2).to_broadcast([P, B * RH, RV]), ALU.mult).then_inc(r_o1.sem, 1)
                    dve.wait_ge(r_o1.sem, r_o1.at(t, 1))
                    dve.wait_ge(r_sgn.sem, r_sgn.at(t, 1))
                    nc.vector.tensor_tensor(o2[:, :, :], o1[:, :, :], sgn[:, :, :], ALU.mult).then_inc(r_o.sem, 1)
                    if more:
                        rotate(t + 1)
                    dve.wait_ge(r_wo.sem, r_wo.at(t, 1))
                    nc.vector.tensor_tensor(sT[:, :].rearrange("p (b n) -> p b n", b=B)[:, :, bass.ds(t * P, P)],
                                            pd[:, 0, :].rearrange("p (b n) -> p b n", b=B),
                                            state[:, :].rearrange("p (b n) -> p b n", b=B)[:, :, bass.ds(t * P + 1, P)], ALU.add).then_inc(s_there.sem, 1)

                gather(0)
                rotate(0)
                with dve.Fori(0, TILES - 1) as t:
                    retain(t, True)
                retain(TILES - 1, False)


NE, BN = 8, 64
AK = P ** -0.5


def build_second_layer(nc, state, x0T, sT, out, w_att, att_rot, att_mask, w_gate, w_down, w_up, b_down, b_up, expert_rows, before):
    ctx = ExitStack()
    with ctx:
        def sb(name, shape, dt=F32):
            return ctx.enter_context(nc.sbuf_tensor(name, shape, dt))

        def sig(name, per=1, start=0):
            return Signal(ctx, nc, name, per, start)

        pa = ctx.enter_context(nc.psum_tensor("l_pa", [P, 4, 512], F32))
        pb = ctx.enter_context(nc.psum_tensor("l_pb", [P, 4, 512], F32))

        ident = sb("l_ident", [P, P])
        ident_bf = sb("l_ident_bf", [P, P], BF16)
        mean_w = sb("l_mean_w", [P, P])
        centre_w = sb("l_centre_w", [P, P])
        eps_col = sb("l_eps_col", [P, 1])
        primer = sb("l_primer", [P, 7])
        wa = sb("wa", [P, 3 * P])
        arot = sb("arot", [P, 2, TILES, P])
        amask = sb("amask", [P, TILES, T])
        amask_bf = sb("amask_bf", [P, TILES, T], BF16)
        wg = sb("wg", [P, NE])
        wd = sb("wd", [P, NE * BN])
        wu = sb("wu", [P, 4, P])
        bd = sb("bd", [P, 4])
        bu = sb("bu", [NE, P])
        erows = sb("erows", [NE, 4, P])
        ebefore = sb("ebefore", [P, NE, NE])

        sgT = sb("sgT", [P, B, T])
        gT = sb("gT", [P, B, T])
        x1T = sb("x1T", [P, B, T])
        xsq = sb("l_xsq", [P, B, T])
        lnv = sb("l_lnv", [P, B, T])
        rstd = sb("l_rstd", [P, B, T])
        xm = sb("xm", [P, B, T])
        lg = sb("lg", [P, BT, NE])
        beats = sb("beats", [P, BT, NE, NE])
        ties = sb("ties", [P, BT, NE, NE])
        tied = sb("tied", [P, BT, NE, NE])
        wins = sb("wins", [P, BT, NE, NE])
        rank = sb("rank", [P, BT, NE])
        sel = sb("sel", [P, BT, NE])
        gmx = sb("gmx", [P, BT])
        gsub = sb("gsub", [P, BT, NE])
        gex = sb("gex", [P, BT, NE])
        gsel = sb("gsel", [P, BT, NE])
        gden = sb("gden", [P, BT])
        grd = sb("grd", [P, BT])
        gate = sb("gate", [P, BT, NE])
        gaT = sb("gaT", [NE, B, T])
        xmc = sb("xmc", [P, T])
        gac = sb("gac", [NE, T])
        aq1 = sb("aq1", [P, 2, TILES, P])
        aq2 = sb("aq2", [P, 2, TILES, P])
        aqk = sb("aqk", [P, 2, TILES, P])
        aqkT = sb("aqkT", [P, 2, T])
        av = sb("av", [P, TILES, P])
        amx = sb("amx", [P, TILES])
        aneg = sb("aneg", [P, TILES])
        aex = sb("aex", [P, 2, T])
        aden = sb("aden", [P, TILES])
        arden = sb("arden", [P, TILES])
        apr = sb("apr", [P, 2, T])
        apT = sb("apT", [P, 2, TILES, P])
        hid = sb("hid", [P, 4, T])
        hg = sb("hg", [P, 4, T])
        moe = sb("moe", [P, T])
        gs = sb("gs", [P, T])
        x2T = sb("x2T", [P, T])
        xo = sb("xo", [P, B, T])

        loads = [(wa[:, :], w_att), (arot[:, :, :, :], att_rot), (amask[:, :, :], att_mask), (wg[:, :], w_gate), (wd[:, :], w_down),
                 (wu[:, :, :], w_up), (bd[:, :], b_down), (bu[:, :], b_up), (erows[:, :, :], expert_rows)]
        all_loads = 16 * (len(loads) + 1)
        c_loads = sig("l_loads")
        l_ident = sig("l_identity")
        c_set = sig("l_set")
        c_bf = sig("l_bf")
        s_gate = sig("s_gate")
        gated = sig("gated")
        x1_there = sig("x1_there")
        m_centred = sig("m_centred")
        m_sq = sig("m_sq")
        m_var = sig("m_var")
        m_ln = sig("m_ln")
        m_rstd = sig("m_rstd")
        xm_there = sig("xm_there")
        steps = sig("l_steps")
        e_lg = sig("e_lg")
        e_sub = sig("e_sub")
        e_exp = sig("e_exp")
        e_gate = sig("e_gate")
        e_gturn = sig("e_gturn")
        e_gT = sig("e_gT")
        xmc_there = sig("xmc_there")
        gac_there = sig("gac_there")
        a_qk = sig("a_qk")
        a_vproj = sig("a_vproj")
        a_v = sig("a_v")
        a_terms = sig("a_terms")
        a_rot = sig("a_rot")
        a_turned = sig("a_turned", 2)
        a_T = sig("a_T", 2)
        a_sc = sig("a_sc", TILES)
        a_max = sig("a_max", TILES)
        a_neg = sig("a_neg", TILES)
        a_exp = sig("a_exp", TILES)
        a_rden = sig("a_rden", TILES)
        a_p = sig("a_p", TILES, start=1)
        a_pturn = sig("a_pturn", TILES, start=1)
        a_pT = sig("a_pT", TILES)
        a_out = sig("a_out", TILES, start=1)
        e_down = sig("e_down", 4)
        e_hid = sig("e_hid", 4)
        e_spread = sig("e_spread", 4)
        e_hg = sig("e_hg", 4, start=1)
        e_up = sig("e_up", start=1)
        e_silu = sig("e_silu")
        gs_there = sig("gs_there", start=1)
        x2_there = sig("x2_there")
        x2_turn = sig("x2_turn")
        xo_there = sig("xo_there", start=1)
        stored = sig("stored", 16)

        def pair(a, k):
            return a[:, 2 * k:2 * k + 2, :].rearrange("p b n -> p (b n)")

        with nc.Block() as block:

            @block.sync
            def _(sp):
                for to, of in loads:
                    sp.dma_start(to, of).then_inc(c_loads.sem, 16)
                sp.dma_start(ebefore[:, :, :].rearrange("p e f -> p (e f)"), before.to_broadcast([P, NE * NE])).then_inc(c_loads.sem, 16)
                with sp.Fori(0, B) as b:
                    sp.wait_ge(xo_there.sem, xo_there.at(b, 1))
                    sp.dma_start(out[bass.ds(b, 1), :, :].rearrange("o (t p) d -> p (o t) d", p=P), xo[:, bass.ds(b, 1), :].rearrange("p o (t d) -> p (o t) d", d=P)).then_inc(stored.sem, 16)
                sp.wait_ge(stored.sem, 16 * B)

            @block.gpsimd
            def _(pool):
                nc.gpsimd.memset(ident[:, :], 0.0).then_inc(l_ident.sem, 1)
                pool.wait_ge(l_ident.sem, 1)
                nc.gpsimd.affine_select(out=ident[:, :], in_=ident[:, :], compare_op=ALU.not_equal, fill=1.0,
                                        base=0, pattern=[[-1, P]], channel_multiplier=1).then_inc(l_ident.sem, 1)
                pool.wait_ge(c_loads.sem, all_loads)
                nc.gpsimd.tensor_copy(amask_bf[:, :, :], amask[:, :, :]).then_inc(c_bf.sem, 1)
                pool.wait_ge(c_bf.sem, 1)

            @block.tensor
            def _(pe):
                pe.wait_ge(c_set.sem, 4)
                for k in range(2):
                    pe.wait_ge(x1_there.sem, k + 1)
                    for b in (2 * k, 2 * k + 1):
                        ins = nc.tensor.matmul(pa[:, b, :], centre_w[:, :], x1T[:, b, :], start=True, stop=True)
                    ins.then_inc(m_centred.sem, 1)
                for k in range(2):
                    pe.wait_ge(m_sq.sem, k + 1)
                    for b in (2 * k, 2 * k + 1):
                        ins = nc.tensor.matmul(pb[:, b, :], mean_w[:, :], xsq[:, b, :], start=True, stop=True)
                    ins.then_inc(m_var.sem, 1)
                pe.wait_ge(c_loads.sem, all_loads)
                pe.wait_ge(xm_there.sem, 2)
                for i in range(BT):
                    ins = nc.tensor.matmul(pb[:, 0, NE * i:NE * (i + 1)], xm[:, i // TILES, P * (i % TILES):P * (i % TILES + 1)], wg[:, :], start=True, stop=True)
                ins.then_inc(e_lg.sem, 1)

                def project_qk(b):
                    pe.wait_ge(xmc_there.sem, xmc_there.at(b, 1))
                    pe.wait_ge(a_exp.sem, a_exp.at(b, 0))
                    for k in range(2):
                        for t in range(TILES):
                            ins = nc.tensor.matmul(pa[:, k, P * t:P * (t + 1)], xmc[:, P * t:P * (t + 1)], wa[:, P * k:P * (k + 1)], start=True, stop=True)
                    ins.then_inc(a_qk.sem, 1)

                def project_v(b):
                    pe.wait_ge(gs_there.sem, gs_there.at(b, 0))
                    for t in range(TILES):
                        ins = nc.tensor.matmul(pa[:, 2, P * t:P * (t + 1)], xmc[:, P * t:P * (t + 1)], wa[:, 2 * P:3 * P], start=True, stop=True)
                    ins.then_inc(a_vproj.sem, 1)

                project_qk(0)
                project_v(0)
                pe.wait_ge(e_gate.sem, 1)
                for i in range(BT):
                    ins = nc.tensor.transpose(pb[0:NE, i // TILES, P * (i % TILES):P * (i % TILES + 1)], gate[:, i, :], ident[:, :])
                ins.then_inc(e_gturn.sem, 1)
                pe.wait_ge(e_gT.sem, 1)
                pe.wait_ge(c_bf.sem, 1)

                def pe_batch(b, more):
                    def adapters_down(c):
                        pe.wait_ge(e_hg.sem, e_hg.at(b, c))
                        nc.tensor.matmul(pa[:, 3, :], wd[:, P * c:P * (c + 1)], xmc[:, :], start=True, stop=True).then_inc(e_down.sem, 1)
                        if c == 0:
                            pe.wait_ge(gac_there.sem, gac_there.at(b, 1))
                        nc.tensor.matmul(pb[:, 2, :], erows[:, c, :], gac[:, :], start=True, stop=True).then_inc(e_spread.sem, 1)

                    def scores(t):
                        if t >= 2:
                            pe.wait_ge(a_exp.sem, a_exp.at(b, t - 1))
                        nc.tensor.matmul(pa[:, t % 2, :], ident_bf[:, :], amask_bf[:, t, :], start=True, stop=False, skip_group_check=True)
                        nc.tensor.matmul(pa[:, t % 2, :], aqkT[:, 0, P * t:P * (t + 1)], aqkT[:, 1, :], start=False, stop=True,
                                         skip_group_check=True).then_inc(a_sc.sem, 1)

                    def transpose_p(t):
                        if t >= 2:
                            pe.wait_ge(a_pT.sem, a_pT.at(b, t - 1))
                        pe.wait_ge(a_p.sem, a_p.at(b, t + 1))
                        for n in range(TILES):
                            ins = nc.tensor.transpose(pb[:, t % 2, P * n:P * (n + 1)], apr[:, t % 2, P * n:P * (n + 1)], ident[:, :])
                        ins.then_inc(a_pturn.sem, 1)

                    def attend(t):
                        pe.wait_ge(a_pT.sem, a_pT.at(b, t + 1))
                        for n in range(TILES):
                            ins = nc.tensor.matmul(pa[:, 2, P * t:P * (t + 1)], av[:, n, :], apT[:, t % 2, n, :], start=(n == 0), stop=(n == TILES - 1))
                        ins.then_inc(a_out.sem, 1)

                    pe.wait_ge(xo_there.sem, xo_there.at(b, 0))
                    adapters_down(0)
                    adapters_down(1)
                    pe.wait_ge(a_rot.sem, a_rot.at(b, 1))
                    for k in range(2):
                        for t in range(TILES):
                            ins = nc.tensor.transpose(pb[:, k, P * t:P * (t + 1)], aqk[:, k, t, :], ident[:, :])
                        ins.then_inc(a_turned.sem, 1)
                    adapters_down(2)
                    pe.wait_ge(a_T.sem, a_T.at(b, 2))
                    pe.wait_ge(a_v.sem, a_v.at(b, 1))
                    scores(0)
                    scores(1)
                    adapters_down(3)
                    transpose_p(0)
                    scores(2)
                    transpose_p(1)
                    attend(0)
                    scores(3)
                    attend(1)
                    pe.wait_ge(e_hg.sem, e_hg.at(b, 4))
                    for c in range(4):
                        nc.tensor.matmul(pb[:, 3, :], wu[:, c, :], hg[:, c, :], start=(c == 0), stop=False)
                        if c == 1:
                            transpose_p(2)
                    nc.tensor.matmul(pb[:, 3, :], bu[:, :], gac[:, :], start=False, stop=True).then_inc(e_up.sem, 1)
                    transpose_p(3)
                    attend(2)
                    attend(3)
                    if more:
                        project_qk(b + 1)
                        project_v(b + 1)
                    pe.wait_ge(x2_there.sem, x2_there.at(b, 1))
                    for t in range(TILES):
                        ins = nc.tensor.transpose(pa[:, 3, P * t:P * (t + 1)], x2T[:, P * t:P * (t + 1)], ident[:, :])
                    ins.then_inc(x2_turn.sem, 1)

                with pe.Fori(0, B - 1) as b:
                    pe_batch(b, True)
                pe_batch(B - 1, False)

            @block.scalar
            def _(act):
                act.wait_ge(c_set.sem, 4)
                for k in range(2):
                    for b in (2 * k, 2 * k + 1):
                        ins = nc.scalar.activation(sgT[:, b, :], state[:, b * SHIFTED + 1:b * SHIFTED + 1 + T], ACT.Silu)
                    ins.then_inc(s_gate.sem, 1)
                nc.scalar.preload_act_table_set(LN_EXP_SET)
                for k in range(2):
                    act.wait_ge(m_centred.sem, k + 1)
                    nc.scalar.activation(pair(xsq, k), pair(pa, k), ACT.Square).then_inc(m_sq.sem, 1)
                for k in range(2):
                    act.wait_ge(m_var.sem, k + 1)
                    nc.scalar.activation(pair(lnv, k), pair(pb, k), ACT.Ln, bias=eps_col[:, 0:1]).then_inc(m_ln.sem, 1)
                    act.wait_ge(m_ln.sem, k + 1)
                    nc.scalar.activation(pair(rstd, k), pair(lnv, k), ACT.Exp, scale=-0.5).then_inc(m_rstd.sem, 1)
                act.wait_ge(e_sub.sem, 1)
                nc.scalar.activation(gex[:, :, :], gsub[:, :, :], ACT.Exp).then_inc(e_exp.sem, 1)
                act.wait_ge(e_gturn.sem, 1)
                nc.scalar.copy(gaT[:, :, :], pb[0:NE, :, :]).then_inc(e_gT.sem, 1)
                act.wait_ge(e_gT.sem, 1)
                act.wait_ge(c_loads.sem, all_loads)
                with act.Fori(0, B) as b:
                    def hidden(c):
                        act.wait_ge(e_down.sem, e_down.at(b, c + 1))
                        nc.scalar.activation(hid[:, c, :], pa[:, 3, :], ACT.Relu, bias=bd[:, c:c + 1]).then_inc(e_hid.sem, 1)

                    def exponentials(t):
                        act.wait_ge(a_neg.sem, a_neg.at(b, t + 1))
                        act.wait_ge(a_p.sem, a_p.at(b, max(t - 1, 0)))
                        nc.scalar.activation(aex[:, t % 2, :], pa[:, t % 2, :], ACT.Exp, bias=aneg[:, t:t + 1], scale=AK,
                                             accum_out=aden[:, t:t + 1]).then_inc(a_exp.sem, 1)

                    def copy_pT(t):
                        act.wait_ge(a_pturn.sem, a_pturn.at(b, t + 1))
                        act.wait_ge(a_out.sem, a_out.at(b, max(t - 1, 0)))
                        nc.scalar.copy(apT[:, t % 2, :, :], pb[:, t % 2, :]).then_inc(a_pT.sem, 1)

                    act.wait_ge(a_vproj.sem, a_vproj.at(b, 1))
                    nc.scalar.copy(av[:, :, :], pa[:, 2, :]).then_inc(a_v.sem, 1)
                    hidden(0)
                    hidden(1)
                    for k in range(2):
                        act.wait_ge(a_turned.sem, a_turned.at(b, k + 1))
                        nc.scalar.copy(aqkT[:, k, :], pb[:, k, :]).then_inc(a_T.sem, 1)
                    hidden(2)
                    exponentials(0)
                    exponentials(1)
                    hidden(3)
                    copy_pT(0)
                    exponentials(2)
                    copy_pT(1)
                    exponentials(3)
                    copy_pT(2)
                    copy_pT(3)
                    act.wait_ge(e_up.sem, e_up.at(b, 1))
                    nc.scalar.activation(moe[:, :], pb[:, 3, :], ACT.Silu, scale=0.5).then_inc(e_silu.sem, 1)
                    nc.scalar.preload_act_table_set(LN_EXP_SET)
                    act.wait_ge(x2_turn.sem, x2_turn.at(b, 1))
                    nc.scalar.activation(xo[:, :, :].rearrange("p b n -> p (b n)")[:, bass.ds(b * T, T)], pa[:, 3, :], ACT.Copy).then_inc(xo_there.sem, 1)

            @block.vector
            def _(dve):
                count = [0]

                def then(ins):
                    count[0] += 1
                    ins.then_inc(steps.sem, 1)
                    dve.wait_ge(steps.sem, count[0])

                def copy_at(to, of):
                    return nc.vector.tensor_scalar(to, of, 1.0, None, ALU.mult)

                nc.vector.memset(mean_w[:, :], 1.0 / P).then_inc(c_set.sem, 1)
                nc.vector.memset(eps_col[:, :], EPS).then_inc(c_set.sem, 1)
                dve.wait_ge(l_ident.sem, 2)
                nc.vector.tensor_scalar(centre_w[:, :], ident[:, :], 1.0 / P, None, ALU.subtract).then_inc(c_set.sem, 1)
                nc.vector.tensor_copy(ident_bf[:, :], ident[:, :]).then_inc(c_set.sem, 1)
                for n, raised in enumerate((a_p, a_pturn, a_out, e_hg, e_up, xo_there, gs_there)):
                    nc.vector.memset(primer[:, n:n + 1], 0.0).then_inc(raised.sem, 1)

                for k in range(2):
                    tokens = slice(2 * k * T, 2 * (k + 1) * T)
                    dve.wait_ge(s_gate.sem, k + 1)
                    nc.vector.tensor_tensor(pair(gT, k), sT[:, tokens], pair(sgT, k), ALU.mult).then_inc(gated.sem, 1)
                    dve.wait_ge(gated.sem, k + 1)
                    nc.vector.tensor_tensor(pair(x1T, k), pair(gT, k), x0T[:, tokens], ALU.add).then_inc(x1_there.sem, 1)
                for k in range(2):
                    dve.wait_ge(m_rstd.sem, k + 1)
                    nc.vector.tensor_tensor(pair(xm, k), pair(pa, k), pair(rstd, k), ALU.mult).then_inc(xm_there.sem, 1)

                dve.wait_ge(xm_there.sem, 2)
                nc.vector.tensor_copy(xmc[:, :], xm[:, 0, :]).then_inc(xmc_there.sem, 1)

                dve.wait_ge(c_loads.sem, all_loads)
                dve.wait_ge(e_lg.sem, 1)
                then(nc.vector.tensor_copy(lg[:, :, :], pb[:, 0, 0:NE * BT].rearrange("p (t e) -> p t e", e=NE)))
                mine = lg[:, :, :].unsqueeze(3).to_broadcast([P, BT, NE, NE])
                theirs = lg[:, :, :].unsqueeze(2).to_broadcast([P, BT, NE, NE])
                nc.vector.tensor_tensor(beats[:, :, :, :], theirs, mine, ALU.is_gt)
                nc.vector.tensor_reduce(gmx[:, :], lg[:, :, :], AX.X, ALU.max)
                then(nc.vector.tensor_tensor(ties[:, :, :, :], theirs, mine, ALU.is_equal))
                nc.vector.tensor_tensor(gsub[:, :, :], lg[:, :, :], gmx[:, :].unsqueeze(2).to_broadcast([P, BT, NE]), ALU.subtract).then_inc(e_sub.sem, 1)
                then(nc.vector.tensor_tensor(tied[:, :, :, :], ties[:, :, :, :], ebefore[:, :, :].unsqueeze(1).to_broadcast([P, BT, NE, NE]), ALU.mult))
                then(nc.vector.tensor_tensor(wins[:, :, :, :], beats[:, :, :, :], tied[:, :, :, :], ALU.add))
                then(nc.vector.tensor_reduce(rank[:, :, :], wins[:, :, :, :], AX.X, ALU.add))
                then(nc.vector.tensor_scalar(sel[:, :, :], rank[:, :, :], 2.0, None, ALU.is_lt))
                dve.wait_ge(e_exp.sem, 1)
                then(nc.vector.tensor_tensor(gsel[:, :, :], gex[:, :, :], sel[:, :, :], ALU.mult))
                then(nc.vector.tensor_reduce(gden[:, :], gsel[:, :, :], AX.X, ALU.add))
                then(nc.vector.reciprocal(grd[:, :], gden[:, :]))
                nc.vector.tensor_tensor(gate[:, :, :], gsel[:, :, :], grd[:, :].unsqueeze(2).to_broadcast([P, BT, NE]), ALU.mult).then_inc(e_gate.sem, 1)


                def rotate(b):
                    dve.wait_ge(a_qk.sem, a_qk.at(b, 1))
                    of = pa[:, 0:2, :].rearrange("p k (t n) -> p k t n", n=P)
                    for k in range(2):
                        nc.vector.tensor_tensor(aq1[:, k, :, :], of[:, k, :, :], arot[:, 0, :, :], ALU.mult)
                        ins = nc.vector.tensor_tensor(
                            aq2[:, k, :, :].rearrange("p t (s d) -> p t s d", s=2),
                            of[:, k, :, :].rearrange("p t (s d) -> p t s d", s=2)[:, :, ::-1, :],
                            arot[:, 1, :, :].rearrange("p t (s d) -> p t s d", s=2), ALU.mult)
                    ins.then_inc(a_terms.sem, 1)
                    dve.wait_ge(a_terms.sem, a_terms.at(b, 1))
                    nc.vector.tensor_tensor(aqk[:, :, :, :], aq1[:, :, :, :], aq2[:, :, :, :], ALU.add).then_inc(a_rot.sem, 1)

                rotate(0)
                dve.wait_ge(e_gT.sem, 1)
                nc.vector.tensor_copy(gac[:, :], gaT[:, 0, :]).then_inc(gac_there.sem, 1)

                def dve_batch(b, more):
                    def gated_hidden(c):
                        dve.wait_ge(e_hid.sem, e_hid.at(b, c + 1))
                        dve.wait_ge(e_spread.sem, e_spread.at(b, c + 1))
                        if c == 0:
                            dve.wait_ge(e_up.sem, e_up.at(b, 0))
                        nc.vector.tensor_tensor(hg[:, c, :], pb[:, 2, :], hid[:, c, :], ALU.mult).then_inc(e_hg.sem, 1)

                    def row_max(t):
                        dve.wait_ge(a_sc.sem, a_sc.at(b, t + 1))
                        nc.vector.tensor_reduce(amx[:, t:t + 1], pa[:, t % 2, :], AX.X, ALU.max).then_inc(a_max.sem, 1)
                        dve.wait_ge(a_max.sem, a_max.at(b, t + 1))
                        nc.vector.tensor_scalar(aneg[:, t:t + 1], amx[:, t:t + 1], -AK, None, ALU.mult).then_inc(a_neg.sem, 1)

                    def normalise(t):
                        dve.wait_ge(a_exp.sem, a_exp.at(b, t + 1))
                        nc.vector.reciprocal(arden[:, t:t + 1], aden[:, t:t + 1]).then_inc(a_rden.sem, 1)
                        dve.wait_ge(a_rden.sem, a_rden.at(b, t + 1))
                        dve.wait_ge(a_pturn.sem, a_pturn.at(b, max(t - 1, 0)))
                        nc.vector.tensor_scalar(apr[:, t % 2, :], aex[:, t % 2, :], arden[:, t:t + 1], None, ALU.mult).then_inc(a_p.sem, 1)

                    gated_hidden(0)
                    gated_hidden(1)
                    gated_hidden(2)
                    row_max(0)
                    row_max(1)
                    normalise(0)
                    gated_hidden(3)
                    if more:
                        dve.wait_ge(e_down.sem, e_down.at(b, 4))
                        copy_at(xmc[:, :], xm[:, :, :].rearrange("p b n -> p (b n)")[:, bass.ds((b + 1) * T, T)]).then_inc(xmc_there.sem, 1)
                    normalise(1)
                    row_max(2)
                    normalise(2)
                    row_max(3)
                    normalise(3)
                    if more:
                        dve.wait_ge(e_up.sem, e_up.at(b, 1))
                        copy_at(gac[:, :], gaT[:, :, :].rearrange("p b n -> p (b n)")[:, bass.ds((b + 1) * T, T)]).then_inc(gac_there.sem, 1)
                    dve.wait_ge(e_silu.sem, e_silu.at(b, 1))
                    dve.wait_ge(a_out.sem, a_out.at(b, TILES))
                    nc.vector.tensor_tensor(gs[:, :], pa[:, 2, :], moe[:, :], ALU.mult).then_inc(gs_there.sem, 1)
                    dve.wait_ge(gs_there.sem, gs_there.at(b, 1))
                    nc.vector.tensor_tensor(x2T[:, :], gs[:, :], x1T[:, :, :].rearrange("p b n -> p (b n)")[:, bass.ds(b * T, T)], ALU.add).then_inc(x2_there.sem, 1)
                    if more:
                        rotate(b + 1)

                with dve.Fori(0, B - 1) as b:
                    dve_batch(b, True)
                dve_batch(B - 1, False)


def rotary_tables():
    f = np.float32
    half = np.arange(0, DH, 2, dtype=f)
    freqs = np.arange(T, dtype=f)[:, None] * (f(1.0) / f(10000.0) ** (half / f(DH)))[None, :]
    freqs = np.concatenate([freqs, freqs], -1)
    base = (half + f(0.4 * DH)) / f(1.4 * DH)
    power = (np.arange(T, dtype=f) - T // 2) / f(WIN // 2)
    scale = base[None, :] ** power[:, None]
    scale = np.concatenate([scale, scale], -1)
    sign = np.where(np.arange(DH) < DH // 2, -1.0, 1.0).astype(f)
    cos, sin = np.cos(freqs), np.sin(freqs) * sign
    out = np.stack([cos * scale, sin * scale, cos / scale, sin / scale])
    return np.ascontiguousarray(out.reshape(4, TILES, P, DH).transpose(2, 0, 1, 3), dtype=f)


def window_mask():
    query = (np.arange(P) % WIN)[:, None]
    key = np.arange(2 * WIN)[None, :]
    ok = (key >= query) & (key <= query + WIN)
    first = ok & ((np.arange(P)[:, None] >= WIN) | (key >= WIN))
    return np.where(np.stack([first, ok], 1), 0.0, MASKED).astype(np.float32)


def pack_layers(a):
    f = np.float32
    g = lambda n: np.asarray(a["L0_ffn_" + n])
    qkv = g("Wqkv")
    v = qkv[:, :, 2 * INNER:].reshape(DEPTH, P, PAIRS, 2, DH).transpose(0, 1, 3, 2, 4).reshape(DEPTH, P, INNER)
    w_qkv = np.concatenate([qkv[:, :, :2 * INNER], v], 2)
    w_o = g("Wo").reshape(DEPTH, PAIRS, P, P).transpose(0, 2, 1, 3).reshape(DEPTH, P, PAIRS * P)
    w_2 = np.zeros((DEPTH, 3 * P, P), f)
    w_2[:, :FF] = g("W2")
    w_2 = w_2.reshape(DEPTH, 3, P, P).transpose(0, 2, 1, 3).reshape(DEPTH, P, 3 * P)
    cols = np.zeros((DEPTH, 9, P), f)
    b1 = g("b1")
    for k in range(2):
        for c, m in enumerate(FCH):
            cols[:, 3 * k + c, :m] = b1[:, FF * k + P * c:FF * k + P * c + m]
    cols[:, 6], cols[:, 7], cols[:, 8] = g("ln_g"), g("ln_b"), g("b2")
    cols = cols.transpose(0, 2, 1)
    qs, ks = g("q_scale"), g("k_scale")
    swap = lambda s: np.concatenate([s[:, DH // 2:], s[:, :DH // 2]], 1)
    scales = np.stack([qs, swap(qs), ks, swap(ks)], 1)
    return {k: np.ascontiguousarray(v) for k, v in dict(
        w_qkv=w_qkv, w_o=w_o, w_1=g("W1"), w_2=w_2, cols=cols, qk_scale=scales.reshape(1, -1)).items()}


def mixer_tables():
    f = np.float32
    t = np.arange(T, dtype=f)
    tiles = lambda a: a.reshape(TILES, P, -1).transpose(1, 0, 2)

    def rope(theta):
        ang = t[:, None] * theta[None, :]
        c, s = np.cos(ang), np.sin(ang)
        return np.stack([tiles(np.concatenate([c, c], 1)), tiles(np.concatenate([-s, s], 1))], 1).astype(f)

    gamma = f(1.0) - np.exp2(f(-5.0) - np.arange(RH, dtype=f))
    i = np.arange(P, dtype=f)
    wide = lambda a: np.repeat(a.T, RK, axis=1)
    gap = i[None, :] - i[:, None]
    diag = np.where(gap >= 0, gamma[:, None, None] ** np.maximum(gap, 0), 0.0).transpose(1, 0, 2)
    rows, cols = np.arange(P), np.arange(2 * P)
    return {k: np.ascontiguousarray(v, dtype=f) for k, v in dict(
        ret_rot=rope(f(1.0) / f(10000.0) ** (np.arange(0, RK, 2, dtype=f) / f(RK))),
        ret_decay=np.stack([wide(gamma[:, None] ** (i + 1)) * f(RK ** -0.5), wide(gamma[:, None] ** (P - 1 - i))], 1),
        ret_diag=diag * f(RK ** -0.5),
        ret_block=(rows[:, None] // RK == cols[None, :] // RV),
        state_decay=np.repeat(gamma ** P, RK),
        att_rot=rope(f(10000.0) ** (f(-2.0) * np.arange(P // 2, dtype=f) / f(P))),
        att_mask=tiles(np.where(np.arange(T)[None, :] <= np.arange(T)[:, None] + 1, 0.0, MASKED)),
        expert_rows=np.arange(NE)[:, None, None] == (BN * 2 * np.arange(4)[:, None] + rows)[None] // BN,
        before=(np.arange(NE)[None, :] < np.arange(NE)[:, None]).reshape(1, NE * NE)).items()}


def pack_mixers(a):
    g = lambda n: np.asarray(a[n])
    r = lambda n: g("L0_attn_" + n)
    pairs = np.concatenate([np.arange(0, P, 2), np.arange(1, P, 2)])
    att = np.concatenate([g("L1_attn_Wq")[pairs].T, g("L1_attn_Wk")[pairs].T, g("L1_attn_Wv").T], 1)
    return {k: np.ascontiguousarray(v) for k, v in dict(
        w_ret=np.concatenate([r("Wq"), r("Wk"), r("Wv"), r("Wg")], 1),
        w_ro=r("Wo").reshape(2, P, P).transpose(1, 0, 2),
        g_norm=np.tile(r("g_norm_w"), RH)[None, :],
        w_att=att,
        w_gate=g("L1_ffn_w_gate"),
        w_down=g("L1_ffn_Wd").transpose(1, 0, 2).reshape(P, NE * BN),
        w_up=g("L1_ffn_Wu").reshape(4, P, P).transpose(1, 0, 2),
        b_down=g("L1_ffn_bd").reshape(4, P).T,
        b_up=g("L1_ffn_bu")).items()}


def build(nc, x, out, retention, network, second):
    with nc.sbuf_tensor("state", [P, B * SHIFTED], F32) as state, \
            nc.sbuf_tensor("x0T", [P, B * T], F32) as x0T, nc.sbuf_tensor("sT", [P, B * T], F32) as sT:
        build_retention(nc, state=state, x0T=x0T, sT=sT, x=x, **retention)
        build_network(nc, state=state, **network)
        build_second_layer(nc, state=state, x0T=x0T, sT=sT, out=out, **second)


def kernel(**inputs):
    import concourse.bacc as bacc
    from concourse.bass_utils import run_bass_kernel_spmd

    mixers = dict(pack_mixers(inputs), **mixer_tables())
    mixers["ret_cols"] = np.ascontiguousarray(np.stack(
        [np.asarray(inputs["L0_attn_ln_w"]), np.asarray(inputs["L0_attn_ln_b"]), mixers.pop("state_decay")], 1))
    of_retention = ("w_ret", "w_ro", "g_norm", "ret_rot", "ret_decay", "ret_diag", "ret_block", "ret_cols")
    retention = {k: mixers.pop(k) for k in of_retention}
    network = dict(pack_layers(inputs), rotary=rotary_tables(), win_mask=window_mask())
    nc = bacc.Bacc("TRN2", target_bir_lowering=False, num_devices=1)
    arrays = {}

    def dram(name, a):
        arrays[f"in_{name}"] = a
        return nc.dram_tensor(f"in_{name}", a.shape, mybir.dt.from_np(a.dtype), kind="ExternalInput").ap()

    x = dram("x", np.ascontiguousarray(inputs["L0_attn_x"]))
    out = nc.dram_tensor("out_x", (B, T, P), F32, kind="ExternalOutput").ap()
    build(nc, x, out, *({k: dram(k, v) for k, v in part.items()} for part in (retention, network, mixers)))
    r = run_bass_kernel_spmd(nc, [arrays], core_ids=[0])
    return r.results[0]["out_x"]
```
